# Optimizing a Trainium2 kernel written in Bass

```python
import numpy as np
import jax
import jax.numpy as jnp

def _softmax(x, axis=-1):
    return jax.nn.softmax(x, axis=axis)

def _gelu(x):
    return jax.nn.gelu(x, approximate=True)

def _silu(x):
    return jax.nn.silu(x)

def _sigmoid(x):
    return jax.nn.sigmoid(x)

def _layernorm(x, axis=-1, eps=1e-05):
    m = jnp.mean(x, axis=axis, keepdims=True)
    v = jnp.var(x, axis=axis, keepdims=True)
    return (x - m) / jnp.sqrt(v + eps)

def _scatter_add(tgt, idx, src, axis=0):
    return tgt.at[idx].add(src)

def _segment_sum(src, seg, n):
    return jax.ops.segment_sum(src, seg, n)
kernel_name = 'mk_sandwich_d2_jaxref_r4_fe0d1c'

def setup_inputs(seed: int=0):
    np.random.seed(seed)
    _w = jnp.asarray

    def _L0_attn_setup():
        import jax, jax.numpy as jnp
        import numpy as np
        D_MODEL = 256
        NUM_HEADS = 16
        D_HEAD = D_MODEL // NUM_HEADS
        LAMBDA_INIT = 0.8
        EPS = 1e-05
        B, N = (4, 256)
        key = jax.random.key(seed)
        ks = jax.random.split(key, 10)
        w_scale = 1.0 / np.sqrt(D_MODEL)
        d2 = 2 * D_HEAD * NUM_HEADS
        return {'X': jax.random.normal(ks[0], (B, N, D_MODEL), jnp.float32), 'Wq': jax.random.normal(ks[1], (d2, D_MODEL), jnp.float32) * w_scale, 'Wk': jax.random.normal(ks[2], (d2, D_MODEL), jnp.float32) * w_scale, 'Wv': jax.random.normal(ks[3], (d2, D_MODEL), jnp.float32) * w_scale, 'Wo': jax.random.normal(ks[4], (D_MODEL, d2), jnp.float32) * w_scale, 'lq1': jax.random.normal(ks[5], (NUM_HEADS, D_HEAD), jnp.float32), 'lk1': jax.random.normal(ks[6], (NUM_HEADS, D_HEAD), jnp.float32), 'lq2': jax.random.normal(ks[7], (NUM_HEADS, D_HEAD), jnp.float32), 'lk2': jax.random.normal(ks[8], (NUM_HEADS, D_HEAD), jnp.float32), 'rms_scale': jnp.ones((2 * D_HEAD,), jnp.float32)}
    _L0_attn_in = _L0_attn_setup()

    def _L0_ffn_setup():
        import jax, jax.numpy as jnp
        import numpy as np
        DIM = 256
        DEPTH = 2
        HEADS = 8
        DIM_HEAD = 64
        WINDOW = 128
        INNER = HEADS * DIM_HEAD
        HID = int(DIM * 4 * 2 / 3)
        B, N = (2, 2048)
        QK_SCALE = 8.0

        def shift_token(t):
            t1, t2 = jnp.split(t, 2, axis=-1)
            t2 = jnp.pad(t2, ((0, 0), (1, 0), (0, 0)))[:, :-1]
            return jnp.concatenate([t1, t2], axis=-1)

        def l2norm(t):
            return t / jnp.clip(jnp.linalg.norm(t, axis=-1, keepdims=True), 1e-12)

        def rotate_half(x):
            x1, x2 = jnp.split(x, 2, axis=-1)
            return jnp.concatenate([-x2, x1], axis=-1)

        def rotary_xpos(q, k):
            n = q.shape[-2]
            half_idx = jnp.arange(0, DIM_HEAD, 2, dtype=jnp.float32)
            inv_freq = 1.0 / 10000.0 ** (half_idx / DIM_HEAD)
            t = jnp.arange(n, dtype=jnp.float32)
            freqs = t[:, None] * inv_freq[None, :]
            freqs = jnp.concatenate([freqs, freqs], axis=-1)
            base = (half_idx + 0.4 * DIM_HEAD) / (1.4 * DIM_HEAD)
            power = (t - n // 2) / float(WINDOW // 2)
            scale = base[None, :] ** power[:, None]
            scale = jnp.concatenate([scale, scale], axis=-1)
            cos, sin = (jnp.cos(freqs), jnp.sin(freqs))
            q = q * cos * scale + rotate_half(q) * sin * scale
            k = k * cos / scale + rotate_half(k) * sin / scale
            return (q, k)

        def local_attention(q, k, v):
            b, h, n, d = q.shape
            w = n // WINDOW
            bq = q.reshape(b, h, w, WINDOW, d) * QK_SCALE
            bk = k.reshape(b, h, w, WINDOW, d)
            bv = v.reshape(b, h, w, WINDOW, d)

            def look_around(t):
                p = jnp.pad(t, ((0, 0), (0, 0), (1, 0), (0, 0), (0, 0)))
                return jnp.concatenate([p[:, :, :w], p[:, :, 1:]], axis=3)
            bk, bv = (look_around(bk), look_around(bv))
            bt = jnp.arange(n).reshape(w, WINDOW)
            btp = jnp.pad(bt, ((1, 0), (0, 0)), constant_values=-1)
            btk = jnp.concatenate([btp[:w], btp[1:]], axis=1)
            sim = jnp.einsum('bhwid,bhwjd->bhwij', bq, bk)
            i = bt[:, :, None]
            j = btk[:, None, :]
            mask = (i < j) | (i > j + WINDOW) | (j == -1)
            sim = jnp.where(mask, -jnp.finfo(sim.dtype).max, sim)
            attn = jax.nn.softmax(sim, axis=-1)
            out = jnp.einsum('bhwij,bhwjd->bhwid', attn, bv)
            return out.reshape(b, h, n, d)

        def _layer(x, wqkv, qs, ksc, wo, lg, lb, w1, b1, w2, b2):
            b, n, _ = x.shape
            h = shift_token(x)
            qkv = h @ wqkv
            q, k, v = jnp.split(qkv, 3, axis=-1)
            to_heads = lambda t: t.reshape(b, n, HEADS, DIM_HEAD).transpose(0, 2, 1, 3)
            q, k, v = (to_heads(q), to_heads(k), to_heads(v))
            q = l2norm(q) * qs
            k = l2norm(k) * ksc
            q, k = rotary_xpos(q, k)
            o = local_attention(q, k, v)
            o = o.transpose(0, 2, 1, 3).reshape(b, n, INNER)
            x = x + o @ wo
            h = shift_token(x)
            mu = h.mean(-1, keepdims=True)
            var = h.var(-1, keepdims=True)
            h = (h - mu) / jnp.sqrt(var + 1e-05) * lg + lb
            h = h @ w1 + b1
            a, g = jnp.split(h, 2, axis=-1)
            h = a * jax.nn.gelu(g, approximate=False)
            x = x + h @ w2 + b2
            return x
        key = jax.random.key(seed)
        ks = jax.random.split(key, 6)
        return {'x': jax.random.normal(ks[0], (B, N, DIM), jnp.float32), 'wqkv': jax.random.normal(ks[1], (DEPTH, DIM, 3 * INNER), jnp.float32) * 0.02, 'q_scale': jnp.ones((DEPTH, DIM_HEAD), jnp.float32), 'k_scale': jnp.ones((DEPTH, DIM_HEAD), jnp.float32), 'wo': jax.random.normal(ks[2], (DEPTH, INNER, DIM), jnp.float32) * 0.02, 'ln_g': jnp.ones((DEPTH, DIM), jnp.float32), 'ln_b': jnp.zeros((DEPTH, DIM), jnp.float32), 'w1': jax.random.normal(ks[3], (DEPTH, DIM, 2 * HID), jnp.float32) * 0.02, 'b1': jnp.zeros((DEPTH, 2 * HID), jnp.float32), 'w2': jax.random.normal(ks[4], (DEPTH, HID, DIM), jnp.float32) * 0.02, 'b2': jnp.zeros((DEPTH, DIM), jnp.float32)}
    _L0_ffn_in = _L0_ffn_setup()

    def _L1_attn_setup():
        import math
        import jax, jax.numpy as jnp
        import numpy as np
        D = 256
        H = 16
        CH = 8
        EPS = 1e-05

        def _layernorm(x, w, b):
            mu = jnp.mean(x, axis=-1, keepdims=True)
            var = jnp.mean((x - mu) ** 2, axis=-1, keepdims=True)
            return (x - mu) * jax.lax.rsqrt(var + EPS) * w + b

        def _token_diffusion(x, Wqk, Wv, Wo, tau):
            b, n, d = x.shape
            dh = d // H
            qk = (x @ Wqk).reshape(b, n, H, dh).transpose(0, 2, 1, 3)
            v = (x @ Wv).reshape(b, n, H, dh).transpose(0, 2, 1, 3)
            dot = jnp.einsum('bhnd,bhmd->bhnm', qk, qk)
            q2 = jnp.sum(qk * qk, axis=-1)
            logits = (2.0 * dot - q2[..., :, None] - q2[..., None, :]) / math.sqrt(dh)
            logits = logits * tau
            attn = jax.nn.softmax(logits, axis=-1)
            out = jnp.einsum('bhnm,bhmd->bhnd', attn, v)
            out = out.transpose(0, 2, 1, 3).reshape(b, n, d)
            return out @ Wo

        def _channel_diffusion(x, Wqk, Wv, Wo, tau):
            b, n, d = x.shape
            dh = d // CH
            qk = (x @ Wqk).transpose(0, 2, 1).reshape(b, CH, dh, n)
            v = (x @ Wv).transpose(0, 2, 1).reshape(b, CH, dh, n)
            dot = jnp.einsum('bhcn,bhdn->bhcd', qk, qk)
            q2 = jnp.sum(qk * qk, axis=-1)
            logits = (2.0 * dot - q2[..., :, None] - q2[..., None, :]) / math.sqrt(n)
            logits = logits * tau
            attn = jax.nn.softmax(logits, axis=-1)
            out = jnp.einsum('bhcd,bhdn->bhcn', attn, v)
            out = out.reshape(b, d, n).transpose(0, 2, 1)
            return out @ Wo
        key = jax.random.key(seed)
        ks = jax.random.split(key, 8)
        s = 1.0 / math.sqrt(D)
        inp = {'x': jax.random.normal(ks[0], (8, 256, D), dtype=jnp.float32), 'Wqk_t': jax.random.normal(ks[1], (D, D), dtype=jnp.float32) * s, 'Wv_t': jax.random.normal(ks[2], (D, D), dtype=jnp.float32) * s, 'Wo_t': jax.random.normal(ks[3], (D, D), dtype=jnp.float32) * s, 'tau_t': jnp.ones((H, 1, 1), dtype=jnp.float32), 'Wqk_c': jax.random.normal(ks[4], (D, D), dtype=jnp.float32) * s, 'Wv_c': jax.random.normal(ks[5], (D, D), dtype=jnp.float32) * s, 'Wo_c': jax.random.normal(ks[6], (D, D), dtype=jnp.float32) * s, 'tau_c': jnp.ones((CH, 1, 1), dtype=jnp.float32), 'ln1_w': jnp.ones((D,), dtype=jnp.float32), 'ln1_b': jnp.zeros((D,), dtype=jnp.float32), 'ln2_w': jnp.ones((D,), dtype=jnp.float32), 'ln2_b': jnp.zeros((D,), dtype=jnp.float32), 'gamma1': 0.0001 * jnp.ones((D,), dtype=jnp.float32), 'gamma2': 0.0001 * jnp.ones((D,), dtype=jnp.float32)}
        return inp
    _L1_attn_in = _L1_attn_setup()

    def _L1_ffn_setup():
        import jax, jax.numpy as jnp
        import numpy as np
        DIM = 256
        E = 8
        K = 2
        EPS = 1e-05

        def _ln(x, g, b):
            mu = jnp.mean(x, axis=-1, keepdims=True)
            var = jnp.mean(jnp.square(x - mu), axis=-1, keepdims=True)
            return (x - mu) * jax.lax.rsqrt(var + EPS) * g + b
        key = jax.random.key(seed)
        ks = jax.random.split(key, 8)
        H = 2 * DIM
        s_in = 1.0 / np.sqrt(DIM)
        s_h = 1.0 / np.sqrt(H)
        return {'x': jax.random.normal(ks[0], (2, 512, DIM), dtype=jnp.float32), 'gate_w': jax.random.uniform(ks[1], (DIM, E), minval=-s_in, maxval=s_in, dtype=jnp.float32), 'w1': jax.random.uniform(ks[2], (E, DIM, H), minval=-s_in, maxval=s_in, dtype=jnp.float32), 'b1': jax.random.uniform(ks[3], (E, H), minval=-s_in, maxval=s_in, dtype=jnp.float32), 'ln1_g': jnp.ones((E, H), dtype=jnp.float32), 'ln1_b': jnp.zeros((E, H), dtype=jnp.float32), 'w2': jax.random.uniform(ks[4], (E, H, DIM), minval=-s_h, maxval=s_h, dtype=jnp.float32), 'b2': jax.random.uniform(ks[5], (E, DIM), minval=-s_h, maxval=s_h, dtype=jnp.float32), 'ln_g': jnp.ones((DIM,), dtype=jnp.float32), 'ln_b': jnp.zeros((DIM,), dtype=jnp.float32)}
    _L1_ffn_in = _L1_ffn_setup()
    _d = {'L0_attn_X': _L0_attn_in['X'], 'L0_attn_Wq': _L0_attn_in['Wq'], 'L0_attn_Wk': _L0_attn_in['Wk'], 'L0_attn_Wv': _L0_attn_in['Wv'], 'L0_attn_Wo': _L0_attn_in['Wo'], 'L0_attn_lq1': _L0_attn_in['lq1'], 'L0_attn_lk1': _L0_attn_in['lk1'], 'L0_attn_lq2': _L0_attn_in['lq2'], 'L0_attn_lk2': _L0_attn_in['lk2'], 'L0_attn_rms_scale': _L0_attn_in['rms_scale'], 'L0_ffn_wqkv': _L0_ffn_in['wqkv'], 'L0_ffn_q_scale': _L0_ffn_in['q_scale'], 'L0_ffn_k_scale': _L0_ffn_in['k_scale'], 'L0_ffn_wo': _L0_ffn_in['wo'], 'L0_ffn_ln_g': _L0_ffn_in['ln_g'], 'L0_ffn_ln_b': _L0_ffn_in['ln_b'], 'L0_ffn_w1': _L0_ffn_in['w1'], 'L0_ffn_b1': _L0_ffn_in['b1'], 'L0_ffn_w2': _L0_ffn_in['w2'], 'L0_ffn_b2': _L0_ffn_in['b2'], 'L1_attn_Wqk_t': _L1_attn_in['Wqk_t'], 'L1_attn_Wv_t': _L1_attn_in['Wv_t'], 'L1_attn_Wo_t': _L1_attn_in['Wo_t'], 'L1_attn_tau_t': _L1_attn_in['tau_t'], 'L1_attn_Wqk_c': _L1_attn_in['Wqk_c'], 'L1_attn_Wv_c': _L1_attn_in['Wv_c'], 'L1_attn_Wo_c': _L1_attn_in['Wo_c'], 'L1_attn_tau_c': _L1_attn_in['tau_c'], 'L1_attn_ln1_w': _L1_attn_in['ln1_w'], 'L1_attn_ln1_b': _L1_attn_in['ln1_b'], 'L1_attn_ln2_w': _L1_attn_in['ln2_w'], 'L1_attn_ln2_b': _L1_attn_in['ln2_b'], 'L1_attn_gamma1': _L1_attn_in['gamma1'], 'L1_attn_gamma2': _L1_attn_in['gamma2'], 'L1_ffn_gate_w': _L1_ffn_in['gate_w'], 'L1_ffn_w1': _L1_ffn_in['w1'], 'L1_ffn_b1': _L1_ffn_in['b1'], 'L1_ffn_ln1_g': _L1_ffn_in['ln1_g'], 'L1_ffn_ln1_b': _L1_ffn_in['ln1_b'], 'L1_ffn_w2': _L1_ffn_in['w2'], 'L1_ffn_b2': _L1_ffn_in['b2'], 'L1_ffn_ln_g': _L1_ffn_in['ln_g'], 'L1_ffn_ln_b': _L1_ffn_in['ln_b']}
    _x0 = _d['L0_attn_X']
    _d['L0_attn_X'] = jax.random.normal(jax.random.fold_in(jax.random.key(seed), 1), (8, 512, 256), dtype=_x0.dtype)
    del _x0
    return _d

def reference(L0_attn_X, L0_attn_Wq, L0_attn_Wk, L0_attn_Wv, L0_attn_Wo, L0_attn_lq1, L0_attn_lk1, L0_attn_lq2, L0_attn_lk2, L0_attn_rms_scale, L0_ffn_wqkv, L0_ffn_q_scale, L0_ffn_k_scale, L0_ffn_wo, L0_ffn_ln_g, L0_ffn_ln_b, L0_ffn_w1, L0_ffn_b1, L0_ffn_w2, L0_ffn_b2, L1_attn_Wqk_t, L1_attn_Wv_t, L1_attn_Wo_t, L1_attn_tau_t, L1_attn_Wqk_c, L1_attn_Wv_c, L1_attn_Wo_c, L1_attn_tau_c, L1_attn_ln1_w, L1_attn_ln1_b, L1_attn_ln2_w, L1_attn_ln2_b, L1_attn_gamma1, L1_attn_gamma2, L1_ffn_gate_w, L1_ffn_w1, L1_ffn_b1, L1_ffn_ln1_g, L1_ffn_ln1_b, L1_ffn_w2, L1_ffn_b2, L1_ffn_ln_g, L1_ffn_ln_b):

    def _L0_attn_ref(X, Wq, Wk, Wv, Wo, lq1, lk1, lq2, lk2, rms_scale):
        import jax, jax.numpy as jnp
        import numpy as np
        D_MODEL = 256
        NUM_HEADS = 16
        D_HEAD = D_MODEL // NUM_HEADS
        LAMBDA_INIT = 0.8
        EPS = 1e-05
        B, N = (4, 256)
        b, n, _ = X.shape
        H, dh = (NUM_HEADS, D_HEAD)

        def proj(W):
            return (X @ W.T).reshape(b, n, H, 2 * dh).transpose(0, 2, 1, 3)
        Q, K, V = (proj(Wq), proj(Wk), proj(Wv))
        Q1, Q2 = jnp.split(Q, 2, axis=-1)
        K1, K2 = jnp.split(K, 2, axis=-1)
        lam = jnp.exp(jnp.sum(lq1 * lk1, axis=-1)) - jnp.exp(jnp.sum(lq2 * lk2, axis=-1)) + LAMBDA_INIT
        lam = lam[None, :, None, None]
        scaling = 1.0 / np.sqrt(dh)
        causal = jnp.tril(jnp.ones((n, n), bool))
        A1 = jnp.where(causal, jnp.einsum('bhnd,bhmd->bhnm', Q1, K1) * scaling, -jnp.inf)
        A2 = jnp.where(causal, jnp.einsum('bhnd,bhmd->bhnm', Q2, K2) * scaling, -jnp.inf)
        attn = jax.nn.softmax(A1, axis=-1) - lam * jax.nn.softmax(A2, axis=-1)
        O = jnp.einsum('bhnm,bhmd->bhnd', attn, V)
        rms = jnp.sqrt(jnp.mean(O * O, axis=-1, keepdims=True) + EPS)
        O = O / rms * rms_scale * (1.0 - LAMBDA_INIT)
        Oc = O.transpose(0, 2, 1, 3).reshape(b, n, H * 2 * dh)
        return Oc @ Wo.T

    def _L0_ffn_ref(x, wqkv, q_scale, k_scale, wo, ln_g, ln_b, w1, b1, w2, b2):
        import jax, jax.numpy as jnp
        import numpy as np
        DIM = 256
        DEPTH = 2
        HEADS = 8
        DIM_HEAD = 64
        WINDOW = 128
        INNER = HEADS * DIM_HEAD
        HID = int(DIM * 4 * 2 / 3)
        B, N = (2, 2048)
        QK_SCALE = 8.0

        def shift_token(t):
            t1, t2 = jnp.split(t, 2, axis=-1)
            t2 = jnp.pad(t2, ((0, 0), (1, 0), (0, 0)))[:, :-1]
            return jnp.concatenate([t1, t2], axis=-1)

        def l2norm(t):
            return t / jnp.clip(jnp.linalg.norm(t, axis=-1, keepdims=True), 1e-12)

        def rotate_half(x):
            x1, x2 = jnp.split(x, 2, axis=-1)
            return jnp.concatenate([-x2, x1], axis=-1)

        def rotary_xpos(q, k):
            n = q.shape[-2]
            half_idx = jnp.arange(0, DIM_HEAD, 2, dtype=jnp.float32)
            inv_freq = 1.0 / 10000.0 ** (half_idx / DIM_HEAD)
            t = jnp.arange(n, dtype=jnp.float32)
            freqs = t[:, None] * inv_freq[None, :]
            freqs = jnp.concatenate([freqs, freqs], axis=-1)
            base = (half_idx + 0.4 * DIM_HEAD) / (1.4 * DIM_HEAD)
            power = (t - n // 2) / float(WINDOW // 2)
            scale = base[None, :] ** power[:, None]
            scale = jnp.concatenate([scale, scale], axis=-1)
            cos, sin = (jnp.cos(freqs), jnp.sin(freqs))
            q = q * cos * scale + rotate_half(q) * sin * scale
            k = k * cos / scale + rotate_half(k) * sin / scale
            return (q, k)

        def local_attention(q, k, v):
            b, h, n, d = q.shape
            w = n // WINDOW
            bq = q.reshape(b, h, w, WINDOW, d) * QK_SCALE
            bk = k.reshape(b, h, w, WINDOW, d)
            bv = v.reshape(b, h, w, WINDOW, d)

            def look_around(t):
                p = jnp.pad(t, ((0, 0), (0, 0), (1, 0), (0, 0), (0, 0)))
                return jnp.concatenate([p[:, :, :w], p[:, :, 1:]], axis=3)
            bk, bv = (look_around(bk), look_around(bv))
            bt = jnp.arange(n).reshape(w, WINDOW)
            btp = jnp.pad(bt, ((1, 0), (0, 0)), constant_values=-1)
            btk = jnp.concatenate([btp[:w], btp[1:]], axis=1)
            sim = jnp.einsum('bhwid,bhwjd->bhwij', bq, bk)
            i = bt[:, :, None]
            j = btk[:, None, :]
            mask = (i < j) | (i > j + WINDOW) | (j == -1)
            sim = jnp.where(mask, -jnp.finfo(sim.dtype).max, sim)
            attn = jax.nn.softmax(sim, axis=-1)
            out = jnp.einsum('bhwij,bhwjd->bhwid', attn, bv)
            return out.reshape(b, h, n, d)

        def _layer(x, wqkv, qs, ksc, wo, lg, lb, w1, b1, w2, b2):
            b, n, _ = x.shape
            h = shift_token(x)
            qkv = h @ wqkv
            q, k, v = jnp.split(qkv, 3, axis=-1)
            to_heads = lambda t: t.reshape(b, n, HEADS, DIM_HEAD).transpose(0, 2, 1, 3)
            q, k, v = (to_heads(q), to_heads(k), to_heads(v))
            q = l2norm(q) * qs
            k = l2norm(k) * ksc
            q, k = rotary_xpos(q, k)
            o = local_attention(q, k, v)
            o = o.transpose(0, 2, 1, 3).reshape(b, n, INNER)
            x = x + o @ wo
            h = shift_token(x)
            mu = h.mean(-1, keepdims=True)
            var = h.var(-1, keepdims=True)
            h = (h - mu) / jnp.sqrt(var + 1e-05) * lg + lb
            h = h @ w1 + b1
            a, g = jnp.split(h, 2, axis=-1)
            h = a * jax.nn.gelu(g, approximate=False)
            x = x + h @ w2 + b2
            return x
        for l in range(DEPTH):
            x = _layer(x, wqkv[l], q_scale[l], k_scale[l], wo[l], ln_g[l], ln_b[l], w1[l], b1[l], w2[l], b2[l])
        return x

    def _L1_attn_ref(x, Wqk_t, Wv_t, Wo_t, tau_t, Wqk_c, Wv_c, Wo_c, tau_c, ln1_w, ln1_b, ln2_w, ln2_b, gamma1, gamma2):
        import math
        import jax, jax.numpy as jnp
        import numpy as np
        D = 256
        H = 16
        CH = 8
        EPS = 1e-05

        def _layernorm(x, w, b):
            mu = jnp.mean(x, axis=-1, keepdims=True)
            var = jnp.mean((x - mu) ** 2, axis=-1, keepdims=True)
            return (x - mu) * jax.lax.rsqrt(var + EPS) * w + b

        def _token_diffusion(x, Wqk, Wv, Wo, tau):
            b, n, d = x.shape
            dh = d // H
            qk = (x @ Wqk).reshape(b, n, H, dh).transpose(0, 2, 1, 3)
            v = (x @ Wv).reshape(b, n, H, dh).transpose(0, 2, 1, 3)
            dot = jnp.einsum('bhnd,bhmd->bhnm', qk, qk)
            q2 = jnp.sum(qk * qk, axis=-1)
            logits = (2.0 * dot - q2[..., :, None] - q2[..., None, :]) / math.sqrt(dh)
            logits = logits * tau
            attn = jax.nn.softmax(logits, axis=-1)
            out = jnp.einsum('bhnm,bhmd->bhnd', attn, v)
            out = out.transpose(0, 2, 1, 3).reshape(b, n, d)
            return out @ Wo

        def _channel_diffusion(x, Wqk, Wv, Wo, tau):
            b, n, d = x.shape
            dh = d // CH
            qk = (x @ Wqk).transpose(0, 2, 1).reshape(b, CH, dh, n)
            v = (x @ Wv).transpose(0, 2, 1).reshape(b, CH, dh, n)
            dot = jnp.einsum('bhcn,bhdn->bhcd', qk, qk)
            q2 = jnp.sum(qk * qk, axis=-1)
            logits = (2.0 * dot - q2[..., :, None] - q2[..., None, :]) / math.sqrt(n)
            logits = logits * tau
            attn = jax.nn.softmax(logits, axis=-1)
            out = jnp.einsum('bhcd,bhdn->bhcn', attn, v)
            out = out.reshape(b, d, n).transpose(0, 2, 1)
            return out @ Wo
        x = x + _token_diffusion(_layernorm(x, ln1_w, ln1_b), Wqk_t, Wv_t, Wo_t, tau_t) * gamma1
        x = x + _channel_diffusion(_layernorm(x, ln2_w, ln2_b), Wqk_c, Wv_c, Wo_c, tau_c) * gamma2
        return x

    def _L1_ffn_ref(x, gate_w, w1, b1, ln1_g, ln1_b, w2, b2, ln_g, ln_b):
        import jax, jax.numpy as jnp
        import numpy as np
        DIM = 256
        E = 8
        K = 2
        EPS = 1e-05

        def _ln(x, g, b):
            mu = jnp.mean(x, axis=-1, keepdims=True)
            var = jnp.mean(jnp.square(x - mu), axis=-1, keepdims=True)
            return (x - mu) * jax.lax.rsqrt(var + EPS) * g + b
        shape = x.shape
        xf = x.reshape(-1, shape[-1])
        gates = jax.nn.softmax(xf @ gate_w, axis=-1)
        topw, topi = jax.lax.top_k(gates, K)
        topw = topw / jnp.sum(topw, axis=-1, keepdims=True)
        combine = jnp.sum(topw[:, :, None] * jax.nn.one_hot(topi, E, dtype=xf.dtype), axis=1)
        h = jnp.einsum('td,edh->teh', xf, w1) + b1
        h = _ln(h, ln1_g, ln1_b)
        h = jax.nn.gelu(h, approximate=False)
        y = jnp.einsum('teh,ehd->ted', h, w2) + b2
        out = jnp.einsum('ted,te->td', y, combine)
        out = _ln(out + xf, ln_g, ln_b)
        return out.reshape(shape)
    x = L0_attn_X
    x = x + _layernorm(_L0_attn_ref(_layernorm(x, axis=-1), L0_attn_Wq, L0_attn_Wk, L0_attn_Wv, L0_attn_Wo, L0_attn_lq1, L0_attn_lk1, L0_attn_lq2, L0_attn_lk2, L0_attn_rms_scale), axis=-1)
    x = x + _layernorm(_L0_ffn_ref(_layernorm(x, axis=-1), L0_ffn_wqkv, L0_ffn_q_scale, L0_ffn_k_scale, L0_ffn_wo, L0_ffn_ln_g, L0_ffn_ln_b, L0_ffn_w1, L0_ffn_b1, L0_ffn_w2, L0_ffn_b2), axis=-1)
    x = x + _layernorm(_L1_attn_ref(_layernorm(x, axis=-1), L1_attn_Wqk_t, L1_attn_Wv_t, L1_attn_Wo_t, L1_attn_tau_t, L1_attn_Wqk_c, L1_attn_Wv_c, L1_attn_Wo_c, L1_attn_tau_c, L1_attn_ln1_w, L1_attn_ln1_b, L1_attn_ln2_w, L1_attn_ln2_b, L1_attn_gamma1, L1_attn_gamma2), axis=-1)
    x = x + _layernorm(_L1_ffn_ref(_layernorm(x, axis=-1), L1_ffn_gate_w, L1_ffn_w1, L1_ffn_b1, L1_ffn_ln1_g, L1_ffn_ln1_b, L1_ffn_w2, L1_ffn_b2, L1_ffn_ln_g, L1_ffn_ln_b), axis=-1)
    return x

_drawn_inputs = setup_inputs


def setup_inputs(seed=0):
    import zlib

    import numpy as np

    out = dict(_drawn_inputs(seed))
    spreads = {'L0_attn_rms_scale': (1.0, 0.2),
     'L0_ffn_q_scale': (1.0, 0.6),
     'L0_ffn_k_scale': (1.0, 0.6),
     'L0_ffn_ln_g': (1.0, 0.6),
     'L0_ffn_ln_b': (0.0, 0.8),
     'L0_ffn_b1': (0.0, 0.8),
     'L0_ffn_b2': (0.0, 0.1),
     'L1_attn_tau_t': (1.0, 0.6),
     'L1_attn_tau_c': (1.0, 0.2),
     'L1_attn_ln1_w': (1.0, 0.6),
     'L1_attn_ln1_b': (0.0, 2.0),
     'L1_attn_ln2_w': (1.0, 0.6),
     'L1_attn_ln2_b': (0.0, 2.0),
     'L1_attn_gamma1': (9.999999747378752e-05, 0.6),
     'L1_attn_gamma2': (9.999999747378752e-05, 0.6),
     'L1_ffn_ln1_g': (1.0, 0.6),
     'L1_ffn_ln1_b': (0.0, 0.8),
     'L1_ffn_ln_g': (1.0, 0.2),
     'L1_ffn_ln_b': (0.0, 0.341)}
    factors = {'L1_attn_Wqk_t': 8.0,
     'L1_attn_Wv_t': 64.0,
     'L1_attn_Wo_t': 64.0,
     'L1_attn_Wv_c': 64.0,
     'L1_attn_Wo_c': 58.85,
     'L1_ffn_b1': 8.0,
     'L1_ffn_b2': 8.0,
     'L1_attn_Wqk_c': 8.0}
    for name, (base, spread) in spreads.items():
        noise = np.random.default_rng([zlib.crc32(name.encode()), seed]).standard_normal(out[name].shape)
        drawn = base * np.exp(spread * noise) if base else spread * noise
        out[name] = jnp.asarray(drawn.astype(out[name].dtype))
    for name, factor in factors.items():
        out[name] = (out[name] * factor).astype(out[name].dtype)
    return out
```

```python
import concourse.bass as bass
from concourse import mybir
from contextlib import ExitStack, contextmanager

fp32 = mybir.dt.float32
bf16 = mybir.dt.bfloat16
ALU = mybir.AluOpType
ACT = mybir.ActivationFunctionType
AX = mybir.AxisListType

B, N, D = 8, 512, 256
P = 128
NT = N // P
KD = D // P
EPS = 1e-5


@contextmanager
def stage(nc):
    with ExitStack() as ctx:
        ctx.semaphores = []
        yield ctx
    nc.clear_and_free_semaphores(ctx.semaphores)
    nc.all_engine_barrier()


class Signal:

    def __init__(self, ctx, nc, name, per_batch):
        self.sem = nc.alloc_semaphore(name=name)
        ctx.semaphores.append(self.sem)
        self.per_batch = per_batch

    def at(self, b, k):
        return b * self.per_batch + k


def standing_wait(eng, sem, value, passed):
    eng.wait_ge(sem, value)
    eng.sem_inc(passed, 1)


class Order:

    def __init__(self, eng, steps, b):
        self.eng, self.steps, self.b, self.n = eng, steps, b, 0

    def __call__(self, ins, standing=None):
        self.n += 1
        ins.then_inc(self.steps.sem, 1)
        self.eng.wait_ge(self.steps.sem, self.steps.at(self.b, self.n))
        if standing is not None:
            self.eng.sem_inc(standing, 1)

    def close(self):
        assert self.n == self.steps.per_batch, f"{self.n} links in a batch"


def row_stats(nc, link, srcs, stats, mv, passed):
    for t, src in enumerate(srcs):
        last = nc.vector.bn_stats(stats[:, t, :], src)
    link(last, standing=passed)
    for t in range(len(srcs)):
        last = nc.vector.bn_aggr(mv[:, t, :], stats[:, t, :])
    return last


class InverseRoots:

    def __init__(self, ctx, nc, name, per_batch):
        self.nc = nc
        self.given = Signal(ctx, nc, name + "_given", per_batch)
        self.added = Signal(ctx, nc, name + "_added", per_batch)
        self.passed = Signal(ctx, nc, name + "_passed", 0)
        self.passed_dve = Signal(ctx, nc, name + "_passed_dve", 0)
        self.ready = Signal(ctx, nc, name + "_ready", per_batch)

    def step(self, pool, b, k, out, src, eps, neg_half):
        standing_wait(pool, self.given.sem, self.given.at(b, k + 1), self.passed.sem)
        self.nc.gpsimd.tensor_scalar(out, src, eps, None, ALU.add).then_inc(self.added.sem, 1)
        pool.wait_ge(self.added.sem, self.added.at(b, k + 1))
        self.nc.gpsimd.tensor_tensor(out, out, neg_half, ALU.pow).then_inc(self.ready.sem, 1)

    def wait(self, eng, b, k):
        eng.wait_ge(self.ready.sem, self.ready.at(b, k + 1))


def normalise(nc, dst, src, mv, rstd, t):
    return nc.vector.tensor_scalar(dst, src, mv[:, t, 0:1], rstd[:, t:t + 1], ALU.subtract, ALU.mult)


def column(vec, p=P):
    return vec.rearrange("(n p) -> p n", p=p)


def differential_attention(nc, x_dram, out_dram, wq, wk, wv, wo, lam_vecs, rms_scale, con):
    H, DH = 16, 16
    D2 = 2 * DH * H
    G = D2 // P
    HG = H // G
    STEPS = H * NT
    GS = HG * NT
    LAMBDA_INIT = 0.8

    with stage(nc) as ctx:
        def sb(name, shape, dt=fp32):
            return ctx.enter_context(nc.sbuf_tensor("a_" + name, shape, dt))

        def signal(name, per_batch=1):
            return Signal(ctx, nc, "a_" + name, per_batch)

        x_in = sb("x_in", [P, NT, D])
        x_res = sb("x_res", [P, NT, D])
        h = sb("h", [P, NT, D])
        y = sb("y", [P, NT, D])
        hT = sb("hT", [P, KD, N])
        qT = sb("qT", [P, G, N])
        kT = sb("kT", [P, 2, G, N])
        v = sb("v", [P, NT, D2])
        probs = sb("probs", [P, 2, 2, N])
        attn = sb("attn", [P, 2, N])
        attnT = sb("attnT", [P, 2, N])
        o = sb("o", [P, NT, D2])
        osq = sb("osq", [P, NT, D2])
        oT = sb("oT", [P, G, N])
        wq_sb = sb("wq", [P, KD, D2])
        wk_sb = sb("wk", [P, KD, D2])
        wv_sb = sb("wv", [P, KD, D2])
        wo_sb = sb("wo", [P, G, D])
        lam_in = sb("lam_in", [P, 4, H * DH])
        lam_pr = sb("lam_pr", [P, 2, H * DH])
        lam_s = sb("lam_s", [P, 2, H])
        neg_lam = sb("neg_lam", [P, H])
        rms_col = sb("rms_col", [P, 1])
        map_mask = sb("map_mask", [P, 2])
        ident = sb("ident", [P, P])
        ident_h = sb("ident_h", [P, P], bf16)
        causal = sb("causal", [P, P], bf16)
        stats = sb("stats", [P, NT, 6])
        mv = sb("mv", [P, NT, 2])
        rstd = sb("rstd", [P, NT])
        neg_max = sb("neg_max", [P, 2, 2])
        sums = sb("sums", [P, 2, 2])
        inv = sb("inv", [P, 2, 2])
        oss = sb("oss", [P, NT * H])
        orstd = sb("orstd", [P, NT * H])
        neg_half = sb("neg_half", [P, NT * H])

        ps_s = [ctx.enter_context(nc.psum_tensor(f"a_ps_s{i}", [P, 2, N], fp32)) for i in range(2)]
        ps_t = [ctx.enter_context(nc.psum_tensor(f"a_ps_t{i}", [P, N], fp32)) for i in range(2)]
        ps_o = [ctx.enter_context(nc.psum_tensor(f"a_ps_o{i}", [P, NT, P], fp32)) for i in range(2)]
        bank = [ps_s[0][:, 0, :], ps_s[0][:, 1, :], ps_s[1][:, 0, :], ps_s[1][:, 1, :]]

        weights_in = signal("weights_in")
        x_loaded, res_loaded = signal("x_loaded", 16), signal("res_loaded", 16)
        stored = signal("stored", 16)
        setup_act, lam_ready = signal("setup_act"), signal("lam_ready")
        h_ready = signal("h_ready")
        hT_psum, hT_ready = signal("hT_psum", KD), signal("hT_ready", KD)
        proj = signal("proj", 2 * G + NT)
        q_ready, k_ready = signal("q_ready", G), signal("k_ready", G)
        v_ready = signal("v_ready", NT)
        scores_ready = signal("scores_ready", STEPS)
        max_ready = signal("max_ready", STEPS)
        probs_ready = signal("probs_ready", STEPS)
        attn_ready = signal("attn_ready", STEPS)
        attnT_psum = signal("attnT_psum", STEPS)
        attnT_act, attnT_dve = signal("attnT_act", STEPS // 2), signal("attnT_dve", STEPS // 2)
        pv_done = signal("pv_done", STEPS)
        o_ready, osq_ready, o_normed = signal("o_ready", G), signal("osq_ready"), signal("o_normed")
        oT_psum, oT_ready = signal("oT_psum", G), signal("oT_ready", G)
        y_psum, y_ready = signal("y_psum", 2), signal("y_ready")
        half_made = signal("half_made")
        setup_order = signal("setup_order")
        dve_order = signal("dve_order", 1 + 3 * STEPS + 2)
        roots = InverseRoots(ctx, nc, "a_roots", 3)

        x_v = x_dram.rearrange("b (t p) d -> b p t d", p=P)
        out_v = out_dram.rearrange("b (t p) d -> b p t d", p=P)
        steps = [(hd, i) for hd in range(H) for i in range(NT)]
        loads = []

        block = ctx.enter_context(nc.Block())

        @block.sync
        def _(sp):
            sp.dma_start(x_in[:, :, :], x_v[0]).then_inc(x_loaded.sem, 16)
            for dst, src in ((wq_sb, wq), (wk_sb, wk), (wv_sb, wv), (wo_sb, wo)):
                loads.append((dst[:, :, :], src.rearrange("(k p) n -> p k n", p=P)))
            for n, vec in enumerate(lam_vecs):
                loads.append((lam_in[:, n, :], vec.rearrange("h d -> (h d)").partition_broadcast(P)))
            for r in range(HG):
                loads.append((rms_col[32 * r:32 * r + 32, :], rms_scale.rearrange("(p a) -> p a", a=1)))
            loads.extend([(ident[:, :], con["ident"]), (ident_h[:, :], con["ident_h"]),
                          (causal[:, :], con["causal"]), (map_mask[:, :], con["map_mask"])])
            for dst, src in loads:
                sp.dma_start(dst, src).then_inc(weights_in.sem, 16)
            sp.dma_start(x_res[:, :, :], x_v[0]).then_inc(res_loaded.sem, 16)
            with sp.Fori(0, B - 1) as b:
                sp.wait_ge(h_ready.sem, h_ready.at(b, 1))
                sp.dma_start(x_in[:, :, :], x_v[b + 1]).then_inc(x_loaded.sem, 16)
                sp.wait_ge(y_ready.sem, y_ready.at(b, 1))
                sp.dma_start(out_v[b], x_res[:, :, :]).then_inc(stored.sem, 16)
                sp.wait_ge(stored.sem, stored.at(b, 16))
                sp.dma_start(x_res[:, :, :], x_v[b + 1]).then_inc(res_loaded.sem, 16)
            sp.wait_ge(y_ready.sem, B)
            sp.dma_start(out_v[B - 1], x_res[:, :, :]).then_inc(stored.sem, 16)
            sp.wait_ge(stored.sem, 16 * B)

        @block.gpsimd
        def _(pool):
            nc.gpsimd.memset(neg_half[:, :], -0.5).then_inc(half_made.sem, 1)
            pool.wait_ge(half_made.sem, 1)
            with pool.Fori(0, B) as b:
                roots.step(pool, b, 0, rstd[:, :], mv[:, :, 1], EPS, neg_half[:, 0:NT])
                roots.step(pool, b, 1, orstd[:, :], oss[:, :], 2 * DH * EPS, neg_half[:, :])
                roots.step(pool, b, 2, rstd[:, :], mv[:, :, 1], EPS, neg_half[:, 0:NT])

        @block.tensor
        def _(pe):
            pe.wait_ge(weights_in.sem, 16 * len(loads))
            with pe.Fori(0, B) as b:
                pe.wait_ge(h_ready.sem, h_ready.at(b, 1))
                for k in range(KD):
                    for t in range(NT):
                        last = nc.tensor.transpose(ps_t[k][:, t * P:(t + 1) * P], h[:, t, k * P:(k + 1) * P],
                                                   ident[:, :])
                    last.then_inc(hT_psum.sem, 1)
                pe.wait_ge(hT_ready.sem, hT_ready.at(b, KD))
                for n in range(2 * G):
                    w = (wq_sb, wk_sb)[n % 2]
                    j = n // 2
                    if n >= 4:
                        free = (q_ready, k_ready)[n % 2]
                        pe.wait_ge(free.sem, free.at(b, j - 1))
                    for k in range(KD):
                        last = nc.tensor.matmul(bank[n % 4], w[:, k, j * P:(j + 1) * P], hT[:, k, :],
                                                start=k == 0, stop=k == KD - 1)
                    last.then_inc(proj.sem, 1)
                for t in range(NT):
                    free = (q_ready, k_ready)[t % 2]
                    pe.wait_ge(free.sem, free.at(b, 3 + t // 2))
                    for k in range(KD):
                        last = nc.tensor.matmul(bank[t], hT[:, k, t * P:(t + 1) * P], wv_sb[:, k, :],
                                                start=k == 0, stop=k == KD - 1)
                    last.then_inc(proj.sem, 1)
                pe.wait_ge(v_ready.sem, v_ready.at(b, NT))
                for s in range(STEPS + 3):
                    if s < STEPS:
                        hd, i = steps[s]
                        j, r, keys = hd // HG, 32 * (hd % HG), (i + 1) * P
                        if s >= 2:
                            pe.wait_ge(probs_ready.sem, probs_ready.at(b, s - 1))
                        for m in range(2):
                            nc.tensor.matmul(ps_s[s % 2][:, m, 0:keys], qT[r:r + 32, j, i * P:(i + 1) * P],
                                             kT[r:r + 32, m, j, 0:keys], start=True, stop=False)
                            last = nc.tensor.matmul(ps_s[s % 2][:, m, i * P:keys], ident_h[:, :], causal[:, :],
                                                    start=False, stop=True)
                        last.then_inc(scores_ready.sem, 1)
                    if 0 <= s - 2 < STEPS:
                        u = s - 2
                        hd, i = steps[u]
                        pe.wait_ge(attn_ready.sem, attn_ready.at(b, u + 1))
                        if u >= 2:
                            free = (attnT_act, attnT_dve)[u % 2]
                            pe.wait_ge(free.sem, free.at(b, u // 2))
                        for c in range(i + 1):
                            last = nc.tensor.transpose(ps_t[u % 2][:, c * P:(c + 1) * P],
                                                       attn[:, u % 2, c * P:(c + 1) * P], ident[:, :])
                        last.then_inc(attnT_psum.sem, 1)
                    if 0 <= s - 3:
                        u = s - 3
                        hd, i = steps[u]
                        j = hd // HG
                        ready = (attnT_act, attnT_dve)[u % 2]
                        pe.wait_ge(ready.sem, ready.at(b, u // 2 + 1))
                        if u % GS == 0 and j >= 2:
                            pe.wait_ge(o_ready.sem, o_ready.at(b, j - 1))
                        for c in range(i + 1):
                            last = nc.tensor.matmul(ps_o[j % 2][:, i, 32 * (hd % HG):32 * (hd % HG) + 32],
                                                    attnT[:, u % 2, c * P:(c + 1) * P],
                                                    v[:, c, 32 * hd:32 * hd + 32], start=c == 0, stop=c == i)
                        last.then_inc(pv_done.sem, 1)
                pe.wait_ge(o_normed.sem, o_normed.at(b, 1))
                for j in range(G):
                    for t in range(NT):
                        last = nc.tensor.transpose(bank[j][:, t * P:(t + 1) * P], o[:, t, j * P:(j + 1) * P],
                                                   ident[:, :])
                    last.then_inc(oT_psum.sem, 1)
                pe.wait_ge(oT_ready.sem, oT_ready.at(b, G))
                for t in range(NT):
                    for j in range(G):
                        last = nc.tensor.matmul(ps_t[t // 2][:, (t % 2) * D:(t % 2 + 1) * D],
                                                oT[:, j, t * P:(t + 1) * P], wo_sb[:, j, :],
                                                start=j == 0, stop=j == G - 1)
                    if t % 2:
                        last.then_inc(y_psum.sem, 1)

        @block.scalar
        def _(act):
            act.wait_ge(setup_order.sem, 2)
            nc.scalar.activation(lam_s[:, :, :], lam_s[:, :, :], ACT.Exp).then_inc(setup_act.sem, 1)
            with act.Fori(0, B) as b:
                for k in range(KD):
                    act.wait_ge(hT_psum.sem, hT_psum.at(b, k + 1))
                    nc.scalar.copy(hT[:, k, :], ps_t[k][:, :]).then_inc(hT_ready.sem, 1)
                for j in range(G):
                    act.wait_ge(proj.sem, proj.at(b, 2 * j + 1))
                    nc.scalar.mul(qT[:, j, :], bank[2 * j % 4], DH ** -0.5).then_inc(q_ready.sem, 1)
                for t in range(NT):
                    act.wait_ge(proj.sem, proj.at(b, 2 * G + t + 1))
                    nc.scalar.copy(v[:, t, :], bank[t]).then_inc(v_ready.sem, 1)
                for s in range(STEPS + 5):
                    if s < STEPS:
                        hd, i = steps[s]
                        act.wait_ge(max_ready.sem, max_ready.at(b, s + 1))
                        if s >= 2:
                            act.wait_ge(attn_ready.sem, attn_ready.at(b, s - 1))
                        for m in range(2):
                            last = nc.scalar.activation(probs[:, s % 2, m, 0:(i + 1) * P],
                                                        ps_s[s % 2][:, m, 0:(i + 1) * P], ACT.Exp,
                                                        bias=neg_max[:, s % 2, m:m + 1],
                                                        accum_out=sums[:, s % 2, m:m + 1])
                        last.then_inc(probs_ready.sem, 1)
                    u = s - 2
                    if 0 <= u < STEPS and u % 2 == 0:
                        hd, i = steps[u]
                        act.wait_ge(attnT_psum.sem, attnT_psum.at(b, u + 1))
                        if u >= 2:
                            act.wait_ge(pv_done.sem, pv_done.at(b, u - 1))
                        nc.scalar.copy(attnT[:, 0, 0:(i + 1) * P], ps_t[0][:, 0:(i + 1) * P])\
                          .then_inc(attnT_act.sem, 1)
                    u = s - 4
                    if 0 <= u and u % GS == GS - 1:
                        j = u // GS
                        act.wait_ge(pv_done.sem, pv_done.at(b, u + 1))
                        nc.scalar.copy(o[:, :, j * P:(j + 1) * P], ps_o[j % 2][:, :, :]).then_inc(o_ready.sem, 1)
                act.wait_ge(o_ready.sem, o_ready.at(b, G))
                nc.scalar.activation(osq[:, :, :], o[:, :, :], ACT.Square).then_inc(osq_ready.sem, 1)
                for j in range(G):
                    act.wait_ge(oT_psum.sem, oT_psum.at(b, j + 1))
                    nc.scalar.mul(oT[:, j, :], bank[j], rms_col[:, :]).then_inc(oT_ready.sem, 1)

        @block.vector
        def _(dve):
            dve.wait_ge(weights_in.sem, 16 * len(loads))
            for n in range(2):
                last = nc.vector.tensor_tensor(lam_pr[:, n, :], lam_in[:, 2 * n, :], lam_in[:, 2 * n + 1, :], ALU.mult)
            last.then_inc(setup_order.sem, 1)
            dve.wait_ge(setup_order.sem, 1)
            nc.vector.tensor_reduce(lam_s[:, :, :], lam_pr[:, :, :].rearrange("p n (h d) -> p n h d", d=DH),
                                    AX.X, ALU.add).then_inc(setup_order.sem, 1)
            nc.vector.tensor_scalar(rms_col[:, :], rms_col[:, :], (1 - LAMBDA_INIT) * (2 * DH) ** 0.5, None,
                                    ALU.mult).then_inc(setup_order.sem, 1)
            dve.wait_ge(setup_act.sem, 1)
            nc.vector.tensor_tensor(neg_lam[:, :], lam_s[:, 1, :], lam_s[:, 0, :], ALU.subtract)\
              .then_inc(setup_order.sem, 1)
            dve.wait_ge(setup_order.sem, 4)
            nc.vector.tensor_scalar(neg_lam[:, :], neg_lam[:, :], LAMBDA_INIT, None, ALU.subtract)\
              .then_inc(setup_order.sem, 1)
            dve.wait_ge(setup_order.sem, 5)
            with dve.Fori(0, B) as b:
                link = Order(dve, dve_order, b)
                dve.wait_ge(x_loaded.sem, x_loaded.at(b, 16))
                row_stats(nc, link, [x_in[:, t, :] for t in range(NT)], stats, mv, roots.passed_dve.sem)\
                    .then_inc(roots.given.sem, 1)
                roots.wait(dve, b, 0)
                for t in range(NT):
                    last = normalise(nc, h[:, t, :], x_in[:, t, :], mv, rstd, t)
                last.then_inc(h_ready.sem, 1)
                for j in range(G):
                    dve.wait_ge(proj.sem, proj.at(b, 2 * j + 2))
                    for m in range(2):
                        last = nc.vector.tensor_scalar(kT[:, m, j, :], bank[(2 * j + 1) % 4], map_mask[:, m:m + 1],
                                                       None, ALU.mult)
                    last.then_inc(k_ready.sem, 1)
                for s in range(STEPS + 2):
                    if s < STEPS:
                        hd, i = steps[s]
                        dve.wait_ge(scores_ready.sem, scores_ready.at(b, s + 1))
                        if s >= 2:
                            dve.wait_ge(probs_ready.sem, probs_ready.at(b, s - 1))
                        nc.vector.tensor_reduce(neg_max[:, s % 2, :], ps_s[s % 2][:, :, 0:(i + 1) * P], AX.X,
                                                ALU.max, negate=True).then_inc(max_ready.sem, 1)
                    u = s - 1
                    if 0 <= u < STEPS:
                        hd, i = steps[u]
                        w, keys = u % 2, (i + 1) * P
                        dve.wait_ge(probs_ready.sem, probs_ready.at(b, u + 1))
                        link(nc.vector.reciprocal(inv[:, w, :], sums[:, w, :]))
                        link(nc.vector.tensor_tensor(inv[:, w, 1:2], inv[:, w, 1:2], neg_lam[:, hd:hd + 1], ALU.mult))
                        if u >= 2:
                            dve.wait_ge(attnT_psum.sem, attnT_psum.at(b, u - 1))
                        link(nc.vector.tensor_scalar(attn[:, w, 0:keys], probs[:, w, 0, 0:keys], inv[:, w, 0:1], None,
                                                     ALU.mult))
                        nc.vector.scalar_tensor_tensor(attn[:, w, 0:keys], probs[:, w, 1, 0:keys], inv[:, w, 1:2],
                                                       attn[:, w, 0:keys], ALU.mult, ALU.add)\
                          .then_inc(attn_ready.sem, 1)
                    u = s - 2
                    if 0 <= u and u % 2 == 1:
                        hd, i = steps[u]
                        dve.wait_ge(attnT_psum.sem, attnT_psum.at(b, u + 1))
                        if u >= 2:
                            dve.wait_ge(pv_done.sem, pv_done.at(b, u - 1))
                        nc.vector.tensor_copy(attnT[:, 1, 0:(i + 1) * P], ps_t[1][:, 0:(i + 1) * P])\
                          .then_inc(attnT_dve.sem, 1)
                dve.wait_ge(osq_ready.sem, osq_ready.at(b, 1))
                nc.vector.tensor_reduce(oss[:, :], osq[:, :, :].rearrange("p t (h d) -> p (t h) d", h=H), AX.X,
                                        ALU.add).then_inc(roots.given.sem, 1)
                roots.wait(dve, b, 1)
                o_heads = o[:, :, :].rearrange("p t (h d) -> p (t h) d", h=H)
                nc.vector.tensor_tensor(o_heads, o_heads, orstd[:, :].unsqueeze(2).to_broadcast([P, NT * H, 2 * DH]),
                                        ALU.mult).then_inc(o_normed.sem, 1)
                dve.wait_ge(y_psum.sem, y_psum.at(b, 2))
                dve.wait_ge(res_loaded.sem, res_loaded.at(b, 16))
                y_ps = [ps_t[t // 2][:, (t % 2) * D:(t % 2 + 1) * D] for t in range(NT)]
                row_stats(nc, link, y_ps, stats, mv, roots.passed_dve.sem).then_inc(roots.given.sem, 1)
                roots.wait(dve, b, 2)
                for t in range(NT):
                    last = normalise(nc, y[:, t, :], y_ps[t], mv, rstd, t)
                link(last)
                nc.vector.tensor_tensor(x_res[:, :, :], x_res[:, :, :], y[:, :, :], ALU.add).then_inc(y_ready.sem, 1)
                link.close()


def window_attention(nc, x_dram, out_dram, layer, w, con):
    H, DH = 8, 64
    INNER = H * DH
    J = INNER // P
    STEPS = H
    W = 2 * P
    FIRST = layer == 0
    QK = 2 * NT

    with stage(nc) as ctx:
        def sb(name, shape, dt=fp32):
            return ctx.enter_context(nc.sbuf_tensor(f"w{layer}_" + name, shape, dt))

        def signal(name, per_batch=1):
            return Signal(ctx, nc, f"w{layer}_" + name, per_batch)

        x_in, h = sb("x_in", [P, NT, D]), sb("h", [P, NT, D])
        out_sb = sb("out", [P, NT, D])
        hT = sb("hT", [P, KD, N + 1])
        sq = sb("sq", [P, 2, INNER])
        rope = sb("rope", [P, QK, INNER])
        crossed = sb("crossed", [P, 2, INNER])
        qkT = sb("qkT", [P, 2, J, N])
        v = sb("v", [P, NT, INNER])
        probs = sb("probs", [P, 2, NT, W])
        probsT = sb("probsT", [P, 2, NT, W])
        o, oT = sb("o", [P, NT, INNER]), sb("oT", [P, J, N])
        wqkv, wo = sb("wqkv", [P, KD, 3 * INNER]), sb("wo", [P, J, D])
        ident, ident_h = sb("ident", [P, P]), sb("ident_h", [P, P], bf16)
        mask = sb("mask", [P, 2, W], bf16)
        cos, sin = sb("cos", [P, 2, NT, DH]), sb("sin", [P, 2, NT, DH])
        scale, crossed_scale = sb("scale", [P, 2, DH]), sb("crossed_scale", [P, 2, DH])
        ss, inv_norm = sb("ss", [P, QK, H]), sb("inv_norm", [P, QK, H])
        stats, mv, rstd = sb("stats", [P, NT, 6]), sb("mv", [P, NT, 2]), sb("rstd", [P, NT])
        neg_half = sb("neg_half", [P, H])
        neg_max = sb("neg_max", [P, 2, NT])
        sums, inv = sb("sums", [P, 2, NT]), sb("inv", [P, 2, NT])

        ps_s = [ctx.enter_context(nc.psum_tensor(f"w{layer}_ps_s{i}", [P, NT, W], fp32)) for i in range(2)]
        ps_t = ctx.enter_context(nc.psum_tensor(f"w{layer}_ps_t", [P, NT, W], fp32))
        ps_o = [ctx.enter_context(nc.psum_tensor(f"w{layer}_ps_o{i}", [P, N], fp32)) for i in range(2)]
        halves = lambda ps: [ps[:, 2 * i:2 * i + 2, :].rearrange("p t n -> p (t n)") for i in range(2)]
        bank = halves(ps_s[0]) + halves(ps_s[1])
        bank2 = halves(ps_t) + [ps_o[0][:, :], ps_o[1][:, :]]

        weights_in, made, made_pool = signal("weights_in"), signal("made"), signal("made_pool")
        x_loaded, stored = signal("x_loaded", 16), signal("stored", 16)
        x_free, h_ready, y_ready = signal("x_free"), signal("h_ready"), signal("y_ready")
        hT_psum, hT_ready = signal("hT_psum", KD), signal("hT_ready", KD)
        qk_psum, v_psum, v_ready = signal("qk_psum", QK), signal("v_psum", NT), signal("v_ready", NT)
        sq_ready, qk_read, ss_ready = signal("sq_ready", QK), signal("qk_read", QK), signal("ss_ready", QK)
        pool_order, rope_ready = signal("pool_order", 3 * QK), signal("rope_ready", QK)
        qkT_psum, qkT_act, qkT_dve = signal("qkT_psum", 2 * J), signal("qkT_act", J), signal("qkT_dve", J)
        scores_ready, max_ready, probs_ready = (signal("scores_ready", STEPS), signal("max_ready", STEPS),
                                                signal("probs_ready", STEPS))
        probsT_psum, probsT_ready = signal("probsT_psum", STEPS), signal("probsT_ready", STEPS)
        pv_done, o_read = signal("pv_done", STEPS), signal("o_read", STEPS)
        oT_psum, oT_ready, y_psum = signal("oT_psum", J), signal("oT_ready", J), signal("y_psum")
        passed, out_free = signal("passed"), signal("out_free")
        if FIRST:
            roots = InverseRoots(ctx, nc, "w_roots", 1)
        dve_order = signal("dve_order", STEPS + FIRST)
        loads = []

        x_v = x_dram.rearrange("b (t p) d -> b p t d", p=P)
        out_v = out_dram.rearrange("b (t p) d -> b p t d", p=P)
        block = ctx.enter_context(nc.Block())

        @block.sync
        def _(sp):
            sp.dma_start(x_in[:, :, :], x_v[0]).then_inc(x_loaded.sem, 16)
            loads.append((wqkv[:, :, :], w["wqkv"][layer].rearrange("(k p) n -> p k n", p=P)))
            loads.append((wo[:, :, :], w["wo"][layer].rearrange("(k p) n -> p k n", p=P)))
            for n, name in enumerate(("q_scale", "k_scale")):
                vec = w[name][layer]
                loads.append((scale[:, n, :], vec.partition_broadcast(P)))
                for half in range(2):
                    other = 32 * (1 - half)
                    loads.append((crossed_scale[:, n, 32 * half:32 * half + 32],
                                  vec[other:other + 32].partition_broadcast(P)))
            for dst, name in ((ident, "ident"), (ident_h, "ident_h")):
                loads.append((dst[:, :], con[name]))
            loads.append((mask[:, :, :], con["window_mask"]))
            loads.append((cos[:, :, :, :], con["cos"].rearrange("c (t p) d -> p c t d", p=P)))
            loads.append((sin[:, :, :, :], con["sin"].rearrange("c (t p) d -> p c t d", p=P)))
            for dst, src in loads:
                sp.dma_start(dst, src).then_inc(weights_in.sem, 16)
            sp.sem_inc(out_free.sem, 1)
            with sp.Fori(0, B - 1) as b:
                sp.wait_ge(x_free.sem, x_free.at(b, 1))
                sp.dma_start(x_in[:, :, :], x_v[b + 1]).then_inc(x_loaded.sem, 16)
                sp.wait_ge(y_ready.sem, y_ready.at(b, 1))
                sp.dma_start(out_v[b], out_sb[:, :, :]).then_inc(stored.sem, 16)
                sp.wait_ge(stored.sem, stored.at(b, 16))
                sp.sem_inc(out_free.sem, 1)
            sp.wait_ge(y_ready.sem, B)
            sp.dma_start(out_v[B - 1], out_sb[:, :, :]).then_inc(stored.sem, 16)
            sp.wait_ge(stored.sem, 16 * B)

        @block.gpsimd
        def _(pool):
            nc.gpsimd.memset(hT[:, 1, 0:1], 0.0)
            nc.gpsimd.memset(neg_half[:, :], -0.5).then_inc(made_pool.sem, 1)
            pool.wait_ge(made_pool.sem, 1)
            with pool.Fori(0, B) as b:
                if FIRST:
                    roots.step(pool, b, 0, rstd[:, :], mv[:, :, 1], EPS, neg_half[:, 0:NT])
                link = Order(pool, pool_order, b)
                for n in range(QK):
                    pool.wait_ge(ss_ready.sem, ss_ready.at(b, n + 1))
                    pool.sem_inc(passed.sem, 1)
                    link(nc.gpsimd.tensor_scalar(inv_norm[:, n, :], ss[:, n, :], 1e-24, None, ALU.max))
                    link(nc.gpsimd.tensor_tensor(inv_norm[:, n, :], inv_norm[:, n, :], neg_half[:, :], ALU.pow))
                    link(nc.gpsimd.tensor_tensor(rope[:, n, :], rope[:, n, :], crossed[:, n % 2, :], ALU.add))
                    heads = rope[:, n, :].rearrange("p (h d) -> p h d", d=DH)
                    nc.gpsimd.tensor_tensor(heads, heads, inv_norm[:, n, :].unsqueeze(2).to_broadcast([P, H, DH]),
                                            ALU.mult).then_inc(rope_ready.sem, 1)

        @block.tensor
        def _(pe):
            pe.wait_ge(weights_in.sem, 16 * len(loads))
            with pe.Fori(0, B) as b:
                pe.wait_ge(h_ready.sem, h_ready.at(b, 1))
                for k in range(KD):
                    for t in range(NT):
                        last = nc.tensor.transpose(bank2[k][:, t * P:(t + 1) * P], h[:, t, k * P:(k + 1) * P],
                                                   ident[:, :])
                    last.then_inc(hT_psum.sem, 1)
                pe.wait_ge(hT_ready.sem, hT_ready.at(b, KD))
                for n in range(3 * NT):
                    t, c = n // 3, n % 3
                    if n >= 4:
                        tf, cf = (n - 4) // 3, (n - 4) % 3
                        free, k = (v_ready, tf + 1) if cf == 2 else (qk_read, 2 * tf + cf + 1)
                        pe.wait_ge(free.sem, free.at(b, k))
                    for k in range(KD):
                        last = nc.tensor.matmul(bank[n % 4], hT[:, k, t * P:(t + 1) * P],
                                                wqkv[:, k, c * INNER:(c + 1) * INNER], start=k == 0, stop=k == KD - 1)
                    last.then_inc((v_psum if c == 2 else qk_psum).sem, 1)
                pe.wait_ge(rope_ready.sem, rope_ready.at(b, QK))
                for n in range(2 * J):
                    c, j = n // J, n % J
                    if n >= 4:
                        free = (qkT_act, qkT_dve)[n % 2]
                        pe.wait_ge(free.sem, free.at(b, (n - 4) // 2 + 1))
                    for t in range(NT):
                        last = nc.tensor.transpose(bank2[n % 4][:, t * P:(t + 1) * P],
                                                   rope[:, 2 * t + c, j * P:(j + 1) * P], ident[:, :])
                    last.then_inc(qkT_psum.sem, 1)
                pe.wait_ge(qkT_act.sem, qkT_act.at(b, J))
                pe.wait_ge(qkT_dve.sem, qkT_dve.at(b, J))
                pe.wait_ge(v_ready.sem, v_ready.at(b, NT))
                for s in range(STEPS + 2):
                    if s < STEPS:
                        j, r = s // 2, DH * (s % 2)
                        if s >= 2:
                            pe.wait_ge(probs_ready.sem, probs_ready.at(b, s - 1))
                        for t in range(NT):
                            out = ps_s[s % 2][:, t, :]
                            nc.tensor.matmul(out, ident_h[:, :], mask[:, min(t, 1), :], start=True, stop=False)
                            keys = slice(max(t - 1, 0) * P, (t + 1) * P)
                            last = nc.tensor.matmul(out if t else out[:, P:W], qkT[r:r + DH, 0, j, t * P:(t + 1) * P],
                                                    qkT[r:r + DH, 1, j, keys], start=False, stop=True)
                        last.then_inc(scores_ready.sem, 1)
                    u = s - 1
                    if 0 <= u < STEPS:
                        pe.wait_ge(probs_ready.sem, probs_ready.at(b, u + 1))
                        if u >= 1:
                            pe.wait_ge(probsT_ready.sem, probsT_ready.at(b, u))
                        for t in range(NT):
                            for c in range(2):
                                last = nc.tensor.transpose(ps_t[:, t, c * P:(c + 1) * P],
                                                           probs[:, u % 2, t, c * P:(c + 1) * P], ident[:, :])
                        last.then_inc(probsT_psum.sem, 1)
                    u = s - 2
                    if 0 <= u:
                        pe.wait_ge(probsT_ready.sem, probsT_ready.at(b, u + 1))
                        if u >= 2:
                            pe.wait_ge(o_read.sem, o_read.at(b, u - 1))
                        for t in range(NT):
                            for c in range(0 if t else 1, 2):
                                last = nc.tensor.matmul(ps_o[u % 2][:, t * DH:(t + 1) * DH],
                                                        probsT[:, u % 2, t, c * P:(c + 1) * P],
                                                        v[:, t - 1 + c, u * DH:(u + 1) * DH],
                                                        start=c == (0 if t else 1), stop=c == 1)
                        last.then_inc(pv_done.sem, 1)
                pe.wait_ge(o_read.sem, o_read.at(b, STEPS))
                for j in range(J):
                    for t in range(NT):
                        last = nc.tensor.transpose(bank[j][:, t * P:(t + 1) * P], o[:, t, j * P:(j + 1) * P],
                                                   ident[:, :])
                    last.then_inc(oT_psum.sem, 1)
                pe.wait_ge(oT_ready.sem, oT_ready.at(b, J))
                for t in range(NT):
                    for j in range(J):
                        last = nc.tensor.matmul(ps_t[:, t, :], oT[:, j, t * P:(t + 1) * P], wo[:, j, :],
                                                start=j == 0, stop=j == J - 1)
                last.then_inc(y_psum.sem, 1)

        @block.scalar
        def _(act):
            act.wait_ge(made_pool.sem, 1)
            with act.Fori(0, B) as b:
                for k in range(KD):
                    act.wait_ge(hT_psum.sem, hT_psum.at(b, k + 1))
                    nc.scalar.copy(hT[:, k, k:k + N], bank2[k]).then_inc(hT_ready.sem, 1)
                for t in range(NT):
                    for c in range(2):
                        n = 2 * t + c
                        act.wait_ge(qk_psum.sem, qk_psum.at(b, n + 1))
                        if n >= 2:
                            act.wait_ge(ss_ready.sem, ss_ready.at(b, n - 1))
                        nc.scalar.activation(sq[:, n % 2, :], bank[(3 * t + c) % 4], ACT.Square)\
                          .then_inc(sq_ready.sem, 1)
                    act.wait_ge(v_psum.sem, v_psum.at(b, t + 1))
                    nc.scalar.copy(v[:, t, :], bank[(3 * t + 2) % 4]).then_inc(v_ready.sem, 1)
                for n in range(0, 2 * J, 2):
                    act.wait_ge(qkT_psum.sem, qkT_psum.at(b, n + 1))
                    nc.scalar.copy(qkT[:, n // J, n % J, :], bank2[n % 4]).then_inc(qkT_act.sem, 1)
                for s in range(STEPS):
                    act.wait_ge(max_ready.sem, max_ready.at(b, s + 1))
                    if s >= 2:
                        act.wait_ge(probsT_psum.sem, probsT_psum.at(b, s - 1))
                        act.wait_ge(o_read.sem, o_read.at(b, s - 1))
                    for t in range(NT):
                        last = nc.scalar.activation(probs[:, s % 2, t, :], ps_s[s % 2][:, t, :], ACT.Exp,
                                                    bias=neg_max[:, s % 2, t:t + 1],
                                                    accum_out=sums[:, s % 2, t:t + 1])
                    last.then_inc(probs_ready.sem, 1)
                for j in range(J):
                    act.wait_ge(oT_psum.sem, oT_psum.at(b, j + 1))
                    nc.scalar.copy(oT[:, j, :], bank[j]).then_inc(oT_ready.sem, 1)

        @block.vector
        def _(dve):
            dve.wait_ge(weights_in.sem, 16 * len(loads))
            for c in range(2):
                for table, factor in ((cos, scale), (sin, crossed_scale)):
                    last = nc.vector.tensor_tensor(table[:, c, :, :], table[:, c, :, :],
                                                   factor[:, c, :].unsqueeze(1).to_broadcast([P, NT, DH]), ALU.mult)
            last.then_inc(made.sem, 1)
            dve.wait_ge(made.sem, 1)
            with dve.Fori(0, B) as b:
                link = Order(dve, dve_order, b)
                dve.wait_ge(x_loaded.sem, x_loaded.at(b, 16))
                if FIRST:
                    row_stats(nc, link, [x_in[:, t, :] for t in range(NT)], stats, mv, roots.passed_dve.sem)\
                        .then_inc(roots.given.sem, 1)
                    roots.wait(dve, b, 0)
                    for t in range(NT):
                        last = normalise(nc, h[:, t, :], x_in[:, t, :], mv, rstd, t)
                else:
                    last = nc.vector.tensor_copy(h[:, :, :], x_in[:, :, :])
                last.then_inc(h_ready.sem, 1)
                dve.wait_ge(h_ready.sem, h_ready.at(b, 1))
                nc.vector.sem_inc(x_free.sem, 1)
                for t in range(NT):
                    for c in range(2):
                        n = 2 * t + c
                        src = bank[(3 * t + c) % 4].rearrange("p (h s d) -> p h s d", s=2, d=DH // 2)
                        straight = rope[:, n, :].rearrange("p (h d) -> p h d", d=DH)
                        across = crossed[:, n % 2, :].rearrange("p (h s d) -> p h s d", s=2, d=DH // 2)
                        dve.wait_ge(sq_ready.sem, sq_ready.at(b, n + 1))
                        nc.vector.tensor_tensor(straight, bank[(3 * t + c) % 4].rearrange("p (h d) -> p h d", d=DH),
                                                cos[:, c, t, :].unsqueeze(1).to_broadcast([P, H, DH]), ALU.mult)
                        if n >= 2:
                            dve.wait_ge(pool_order.sem, pool_order.at(b, 3 * (n - 1)))
                        for half in range(2):
                            last = nc.vector.tensor_tensor(
                                across[:, :, half, :], src[:, :, 1 - half, :],
                                sin[:, c, t, 32 * half:32 * half + 32].unsqueeze(1).to_broadcast([P, H, DH // 2]),
                                ALU.mult)
                        last.then_inc(qk_read.sem, 1)
                        nc.vector.tensor_reduce(ss[:, n, :], sq[:, n % 2, :].rearrange("p (h d) -> p h d", d=DH), AX.X,
                                                ALU.add).then_inc(ss_ready.sem, 1)
                for n in range(1, 2 * J, 2):
                    dve.wait_ge(qkT_psum.sem, qkT_psum.at(b, n + 1))
                    nc.vector.tensor_copy(qkT[:, n // J, n % J, :], bank2[n % 4]).then_inc(qkT_dve.sem, 1)
                for s in range(STEPS + 2):
                    if s < STEPS:
                        dve.wait_ge(scores_ready.sem, scores_ready.at(b, s + 1))
                        if s >= 2:
                            dve.wait_ge(probs_ready.sem, probs_ready.at(b, s - 1))
                        nc.vector.tensor_reduce(neg_max[:, s % 2, :], ps_s[s % 2][:, :, :], AX.X, ALU.max,
                                                negate=True).then_inc(max_ready.sem, 1)
                    u = s - 1
                    if 0 <= u < STEPS:
                        dve.wait_ge(probsT_psum.sem, probsT_psum.at(b, u + 1))
                        if u >= 2:
                            dve.wait_ge(pv_done.sem, pv_done.at(b, u - 1))
                        nc.vector.tensor_copy(probsT[:, u % 2, :, :], ps_t[:, :, :]).then_inc(probsT_ready.sem, 1)
                    u = s - 2
                    if 0 <= u:
                        link(nc.vector.reciprocal(inv[:, u % 2, :], sums[:, u % 2, :]))
                        dve.wait_ge(pv_done.sem, pv_done.at(b, u + 1))
                        nc.vector.tensor_tensor(o[:, :, u * DH:(u + 1) * DH],
                                                ps_o[u % 2][:, 0:NT * DH].rearrange("p (t d) -> p t d", d=DH),
                                                inv[:, u % 2, :].unsqueeze(2).to_broadcast([P, NT, DH]), ALU.mult)\
                          .then_inc(o_read.sem, 1)
                dve.wait_ge(y_psum.sem, y_psum.at(b, 1))
                dve.wait_ge(out_free.sem, out_free.at(b, 1))
                nc.vector.tensor_tensor(out_sb[:, :, :], h[:, :, :], ps_t[:, :, :], ALU.add).then_inc(y_ready.sem, 1)
                dve.wait_ge(y_ready.sem, y_ready.at(b, 1))
                link.close()


def gated_ffn(nc, y_dram, x_dram, out_dram, layer, w, con):
    HID = 682
    CK = -(-HID // P)
    LAST = layer == 1

    with stage(nc) as ctx:
        def sb(name, shape, dt=fp32):
            return ctx.enter_context(nc.sbuf_tensor(f"f{layer}_" + name, shape, dt))

        def signal(name, per_batch=1):
            return Signal(ctx, nc, f"f{layer}_" + name, per_batch)

        shifted = sb("shifted", [P, NT, D])
        y_res = sb("y_res", [P, NT, D])
        x_res = sb("x_res", [P, NT, D])
        out_sb, yn = sb("out", [P, NT, D]), sb("yn", [P, NT, D])
        hn, hT = sb("hn", [P, NT, D]), sb("hT", [P, KD, N])
        gated = sb("gated", [P, CK, N])
        gelu = sb("gelu", [P, 2, N])
        w1, w2 = sb("w1", [P, KD, 2 * HID]), sb("w2", [P, CK, D])
        b1, b2 = sb("b1", [P, 2, CK]), sb("b2", [P, D])
        ln = sb("ln", [P, 2, KD])
        ident = sb("ident", [P, P])
        stats, mv, rstd = sb("stats", [P, NT, 6]), sb("mv", [P, NT, 2]), sb("rstd", [P, NT])
        neg_half = sb("neg_half", [P, NT])

        ps_a = [ctx.enter_context(nc.psum_tensor(f"f{layer}_ps_a{i}", [P, N], fp32)) for i in range(2)]
        ps_g = [ctx.enter_context(nc.psum_tensor(f"f{layer}_ps_g{i}", [P, N], fp32)) for i in range(2)]
        ps_t = [ctx.enter_context(nc.psum_tensor(f"f{layer}_ps_t{i}", [P, N], fp32)) for i in range(2)]
        ps_y = ctx.enter_context(nc.psum_tensor(f"f{layer}_ps_y", [P, NT, D], fp32))

        weights_in, made_pool = signal("weights_in"), signal("made_pool")
        loaded, res_loaded, stored = signal("loaded", 3 * 16), signal("res_loaded", (1 + LAST) * 16), signal("stored", 16)
        hn_ready, y_ready = signal("hn_ready"), signal("y_ready")
        hT_psum, hT_ready = signal("hT_psum", KD), signal("hT_ready", KD)
        a_psum, g_psum = signal("a_psum", CK), signal("g_psum", CK)
        gelu_ready, gated_ready = signal("gelu_ready", CK), signal("gated_ready", CK)
        y_psum = signal("y_psum")
        roots = InverseRoots(ctx, nc, f"f{layer}_roots", 1 + LAST)
        dve_order = signal("dve_order", 2 + 3 * LAST)
        loads = []

        y_v = y_dram.rearrange("b (t p) d -> b p t d", p=P)
        x_v = x_dram.rearrange("b (t p) d -> b p t d", p=P)
        out_v = out_dram.rearrange("b (t p) d -> b p t d", p=P)
        part = lambda c: min(P, HID - c * P)
        block = ctx.enter_context(nc.Block())

        @block.sync
        def _(sp):
            def load(b):
                half = D // 2
                sp.dma_start(shifted[:, :, 0:half], y_v[b][:, :, 0:half]).then_inc(loaded.sem, 16)
                sp.dma_start(shifted[:, 1:NT, half:D],
                             y_dram[b][P - 1:N - 1, half:D].rearrange("(t p) d -> p t d", p=P)).then_inc(loaded.sem, 16)
                sp.dma_start(shifted[1:P, 0, half:D], y_dram[b][0:P - 1, half:D]).then_inc(loaded.sem, 16)

            def load_residuals(b):
                sp.dma_start(y_res[:, :, :], y_v[b]).then_inc(res_loaded.sem, 16)
                if LAST:
                    sp.dma_start(x_res[:, :, :], x_v[b]).then_inc(res_loaded.sem, 16)

            full = (CK - 1) * P
            for lo, n in ((0, 0), (HID, 1)):
                vec = w["b1"][layer]
                loads.append((b1[:, n, 0:CK - 1], column(vec[lo:lo + full])))
                loads.append((b1[0:HID - full, n, CK - 1:CK], vec[lo + full:lo + HID].rearrange("(p a) -> p a", a=1)))
            loads.append((w1[:, :, :], w["w1"][layer].rearrange("(k p) n -> p k n", p=P)))
            loads.append((w2[:, 0:CK - 1, :], w["w2"][layer][0:full, :].rearrange("(k p) n -> p k n", p=P)))
            loads.append((w2[0:HID - full, CK - 1, :], w["w2"][layer][full:HID, :]))
            loads.append((b2[:, :], w["b2"][layer].partition_broadcast(P)))
            for n, name in enumerate(("ln_g", "ln_b")):
                loads.append((ln[:, n, :], column(w[name][layer])))
            loads.append((ident[:, :], con["ident"]))
            load(0)
            with nc.allow_non_contiguous_dma(reason="a few small vectors, once"):
                for dst, src in loads:
                    sp.dma_start(dst, src).then_inc(weights_in.sem, 16)
            load_residuals(0)
            with sp.Fori(0, B - 1) as b:
                sp.wait_ge(hn_ready.sem, hn_ready.at(b, 1))
                load(b + 1)
                sp.wait_ge(y_ready.sem, y_ready.at(b, 1))
                sp.dma_start(out_v[b], out_sb[:, :, :]).then_inc(stored.sem, 16)
                sp.wait_ge(stored.sem, stored.at(b, 16))
                load_residuals(b + 1)
            sp.wait_ge(y_ready.sem, B)
            sp.dma_start(out_v[B - 1], out_sb[:, :, :]).then_inc(stored.sem, 16)
            sp.wait_ge(stored.sem, 16 * B)

        @block.gpsimd
        def _(pool):
            nc.gpsimd.memset(shifted[0:1, 0, D // 2:D], 0.0)
            nc.gpsimd.memset(neg_half[:, :], -0.5).then_inc(made_pool.sem, 1)
            pool.wait_ge(made_pool.sem, 1)
            with pool.Fori(0, B) as b:
                for k in range(1 + LAST):
                    roots.step(pool, b, k, rstd[:, :], mv[:, :, 1], EPS, neg_half[:, :])

        @block.tensor
        def _(pe):
            pe.wait_ge(weights_in.sem, 16 * len(loads))
            with pe.Fori(0, B) as b:
                pe.wait_ge(hn_ready.sem, hn_ready.at(b, 1))
                for k in range(KD):
                    for t in range(NT):
                        last = nc.tensor.transpose(ps_t[k][:, t * P:(t + 1) * P], hn[:, t, k * P:(k + 1) * P],
                                                   ident[:, :])
                    last.then_inc(hT_psum.sem, 1)
                pe.wait_ge(hT_ready.sem, hT_ready.at(b, KD))
                for c in range(CK):
                    m = part(c)
                    if c >= 2:
                        pe.wait_ge(gated_ready.sem, gated_ready.at(b, c - 1))
                    for ps, lo, done in ((ps_g, HID, g_psum), (ps_a, 0, a_psum)):
                        for k in range(KD):
                            last = nc.tensor.matmul(ps[c % 2][0:m, :], w1[:, k, lo + c * P:lo + c * P + m], hT[:, k, :],
                                                    start=k == 0, stop=k == KD - 1)
                        last.then_inc(done.sem, 1)
                pe.wait_ge(gated_ready.sem, gated_ready.at(b, CK))
                for t in range(NT):
                    for c in range(CK):
                        m = part(c)
                        last = nc.tensor.matmul(ps_y[:, t, :], gated[0:m, c, t * P:(t + 1) * P], w2[0:m, c, :],
                                                start=c == 0, stop=c == CK - 1)
                last.then_inc(y_psum.sem, 1)

        @block.scalar
        def _(act):
            act.wait_ge(weights_in.sem, 16 * len(loads))
            with act.Fori(0, B) as b:
                for k in range(KD):
                    act.wait_ge(hT_psum.sem, hT_psum.at(b, k + 1))
                    nc.scalar.activation(hT[:, k, :], ps_t[k][:, :], ACT.Identity, bias=ln[:, 1, k:k + 1],
                                         scale=ln[:, 0, k:k + 1]).then_inc(hT_ready.sem, 1)
                for c in range(CK):
                    m = part(c)
                    act.wait_ge(g_psum.sem, g_psum.at(b, c + 1))
                    if c >= 2:
                        act.wait_ge(gated_ready.sem, gated_ready.at(b, c - 1))
                    nc.scalar.activation(gelu[0:m, c % 2, :], ps_g[c % 2][0:m, :], ACT.Gelu, bias=b1[0:m, 1, c:c + 1])\
                      .then_inc(gelu_ready.sem, 1)

        @block.vector
        def _(dve):
            dve.wait_ge(weights_in.sem, 16 * len(loads))
            dve.wait_ge(made_pool.sem, 1)

            def norm(b, link, n, src, dst):
                row_stats(nc, link, [src[:, t, :] for t in range(NT)], stats, mv, roots.passed_dve.sem)\
                    .then_inc(roots.given.sem, 1)
                roots.wait(dve, b, n)
                for t in range(NT):
                    last = normalise(nc, dst[:, t, :], src[:, t, :], mv, rstd, t)
                return last

            with dve.Fori(0, B) as b:
                link = Order(dve, dve_order, b)
                dve.wait_ge(loaded.sem, loaded.at(b, 3 * 16))
                norm(b, link, 0, shifted, hn).then_inc(hn_ready.sem, 1)
                for c in range(CK):
                    m = part(c)
                    dve.wait_ge(gelu_ready.sem, gelu_ready.at(b, c + 1))
                    dve.wait_ge(a_psum.sem, a_psum.at(b, c + 1))
                    nc.vector.scalar_tensor_tensor(gated[0:m, c, :], ps_a[c % 2][0:m, :], b1[0:m, 0, c:c + 1],
                                                   gelu[0:m, c % 2, :], ALU.add, ALU.mult).then_inc(gated_ready.sem, 1)
                dve.wait_ge(res_loaded.sem, res_loaded.at(b, (1 + LAST) * 16))
                link(nc.vector.tensor_tensor(y_res[:, :, :], y_res[:, :, :],
                                             b2[:, :].unsqueeze(1).to_broadcast([P, NT, D]), ALU.add))
                dve.wait_ge(y_psum.sem, y_psum.at(b, 1))
                y_new = yn if LAST else out_sb
                add = nc.vector.tensor_tensor(y_new[:, :, :], y_res[:, :, :], ps_y[:, :, :], ALU.add)
                if LAST:
                    link(add)
                    link(norm(b, link, 1, yn, out_sb))
                    add = nc.vector.tensor_tensor(out_sb[:, :, :], out_sb[:, :, :], x_res[:, :, :], ALU.add)
                add.then_inc(y_ready.sem, 1)
                link.close()


def diffusion_attention(nc, x_dram, out_dram, w, con):
    H, DH = 16, 16
    CH, CDH = 8, 32
    ROWS = 32
    G = H * ROWS // P
    HG = H // G
    STEPS = H * NT
    C = float(DH) ** -0.5
    CC = float(N) ** -0.5

    with stage(nc) as ctx:
        def sb(name, shape, dt=fp32):
            return ctx.enter_context(nc.sbuf_tensor("c_" + name, shape, dt))

        def signal(name, per_batch=1):
            return Signal(ctx, nc, "c_" + name, per_batch)

        x_in = sb("x_in", [P, NT, D])
        x_res = sb("x_res", [P, NT, D])
        h = sb("h", [P, NT, D])
        hn = sb("hn", [P, NT, D])
        hT = sb("hT", [P, KD, N])
        qsq = sb("qsq", [P, 2, N])
        qT = sb("qT", [P, G, N])
        kT = sb("kT", [P, G, N])
        v = sb("v", [P, NT, D])
        probs = sb("probs", [P, 4, N])
        probsT = sb("probsT", [P, 2, N])
        o = sb("o", [P, NT, D])
        oT = sb("oT", [P, KD, N])
        y = sb("y", [P, NT, D])
        qc = sb("qc", [P, NT, D])
        vcT = sb("vcT", [P, KD, N])
        wqk = sb("wqk", [P, KD, H, ROWS])
        wv, wo = sb("wv", [P, KD, D]), sb("wo", [P, KD, D])
        wqc, wvc, woc = sb("wqc", [P, KD, D]), sb("wvc", [P, KD, D]), sb("woc", [P, KD, D])
        ln = sb("ln", [P, 4, KD])
        gamma = sb("gamma", [P, 2, D])
        tau = sb("tau", [P, G])
        tau_c = sb("tau_c", [P, KD])
        q_scale, q_bias = sb("q_scale", [P, G]), sb("q_bias", [P, G])
        rows = sb("rows", [P, 4])
        ident, ones = sb("ident", [P, P]), sb("ones", [P, P])
        neg_sum = sb("neg_sum", [P, P])
        block_mask = sb("block_mask", [P, P])
        stats, mv, rstd = sb("stats", [P, NT, 6]), sb("mv", [P, NT, 2]), sb("rstd", [P, NT])
        neg_max = sb("neg_max", [P, 4])
        sums, inv = sb("sums", [P, NT, H]), sb("inv", [P, NT, H])
        gdiag, gsum = sb("gdiag", [P, KD, P]), sb("gsum", [P, KD])
        logits, cattn = sb("logits", [P, KD, P]), sb("cattn", [P, KD, P])
        cmax, csum, cinv = sb("cmax", [P, KD]), sb("csum", [P, KD]), sb("cinv", [P, KD])
        mix = sb("mix", [P, KD, D])
        neg_half = sb("neg_half", [P, NT])

        bank = [ctx.enter_context(nc.psum_tensor(f"c_bank{i}", [P, N], fp32)) for i in range(4)]
        ps_t = [ctx.enter_context(nc.psum_tensor(f"c_ps_t{i}", [P, N], fp32)) for i in range(2)]
        ps_o = [ctx.enter_context(nc.psum_tensor(f"c_ps_o{i}", [P, 2, D], fp32)) for i in range(2)]

        weights_in, made, made_pool = signal("weights_in"), signal("made"), signal("made_pool")
        zeroed = signal("zeroed")
        x_loaded, res_loaded, stored = signal("x_loaded", 16), signal("res_loaded", 16), signal("stored", 16)
        x_free, y_ready = signal("x_free"), signal("y_ready")
        hn_ready = signal("hn_ready", 2)
        hT_psum, hT_ready = signal("hT_psum", 2 * KD), signal("hT_ready", 2 * KD)
        q_psum, qsq_ready, norms_psum = signal("q_psum", G), signal("qsq_ready", G), signal("norms_psum", G)
        q_ready, k_ready = signal("q_ready", G), signal("k_ready", G)
        v_psum, v_ready = signal("v_psum", NT), signal("v_ready", NT)
        scores_ready, max_ready = signal("scores_ready", STEPS), signal("max_ready", STEPS)
        probs_ready = signal("probs_ready", STEPS)
        probsT_psum, probsT_ready = signal("probsT_psum", STEPS), signal("probsT_ready", STEPS)
        pv_done = signal("pv_done", STEPS)
        o_ready, oT_psum, oT_ready = signal("o_ready"), signal("oT_psum", KD), signal("oT_ready", KD)
        yt_psum = signal("yt_psum", 2)
        qc_psum, qc_ready = signal("qc_psum", NT), signal("qc_ready", NT)
        vc_psum, vc_ready = signal("vc_psum", KD), signal("vc_ready", KD)
        gram_psum, gdiag_ready, gnorm_psum = signal("gram_psum"), signal("gdiag_ready"), signal("gnorm_psum")
        cmax_ready, cexp_ready, cattn_ready = signal("cmax_ready"), signal("cexp_ready"), signal("cattn_ready")
        mix_psum, mix_ready, yc_psum = signal("mix_psum"), signal("mix_ready"), signal("yc_psum", 2)
        roots = InverseRoots(ctx, nc, "c_roots", 4)
        dve_order = signal("dve_order", 15)
        loads = []

        x_v = x_dram.rearrange("b (t p) d -> b p t d", p=P)
        out_v = out_dram.rearrange("b (t p) d -> b p t d", p=P)
        steps = [(hd, i) for hd in range(H) for i in range(NT)]

        block = ctx.enter_context(nc.Block())

        @block.sync
        def _(sp):
            sp.dma_start(x_in[:, :, :], x_v[0]).then_inc(x_loaded.sem, 16)
            for dst, src in ((wv, w["Wv_t"]), (wo, w["Wo_t"]), (wqc, w["Wqk_c"]), (wvc, w["Wv_c"]), (woc, w["Wo_c"])):
                loads.append((dst[:, :, :], src.rearrange("(k p) n -> p k n", p=P)))
            for n, name in enumerate(("ln1_w", "ln1_b", "ln2_w", "ln2_b")):
                loads.append((ln[:, n, :], column(w[name])))
            for n in (1, 2):
                loads.append((gamma[:, n - 1, :], w[f"gamma{n}"].partition_broadcast(P)))
            for dst, src in ((tau, w["tau_t"]), (tau_c, w["tau_c"])):
                per_group = src.rearrange("(j r) a c -> r (j a c)", r=HG)
                for r in range(HG):
                    loads.append((dst[32 * r:32 * r + 32, :], per_group[r].partition_broadcast(32)))
            for dst, name in ((ident, "ident"), (neg_sum, "neg_sum"), (block_mask, "block_mask"), (rows, "rows")):
                loads.append((dst[:, :], con[name]))
            with nc.allow_non_contiguous_dma(reason="a few small vectors, once"):
                for dst, src in loads:
                    sp.dma_start(dst, src).then_inc(weights_in.sem, 16)
            sp.wait_ge(zeroed.sem, 1)
            for k in range(KD):
                sp.dma_start(wqk[:, k, :, 0:DH], w["Wqk_t"].rearrange("(k p) (h d) -> k p h d", p=P, d=DH)[k])\
                  .then_inc(weights_in.sem, 16)
            sp.dma_start(x_res[:, :, :], x_v[0]).then_inc(res_loaded.sem, 16)
            with sp.Fori(0, B - 1) as b:
                sp.wait_ge(x_free.sem, x_free.at(b, 1))
                sp.dma_start(x_in[:, :, :], x_v[b + 1]).then_inc(x_loaded.sem, 16)
                sp.wait_ge(y_ready.sem, y_ready.at(b, 1))
                sp.dma_start(out_v[b], x_res[:, :, :]).then_inc(stored.sem, 16)
                sp.wait_ge(stored.sem, stored.at(b, 16))
                sp.dma_start(x_res[:, :, :], x_v[b + 1]).then_inc(res_loaded.sem, 16)
            sp.wait_ge(y_ready.sem, B)
            sp.dma_start(out_v[B - 1], x_res[:, :, :]).then_inc(stored.sem, 16)
            sp.wait_ge(stored.sem, 16 * B)

        N_LOADED = 5 + 4 + 2 + 2 * HG + 4 + KD

        @block.gpsimd
        def _(pool):
            nc.gpsimd.memset(wqk[:, :, :, :], 0.0).then_inc(zeroed.sem, 1)
            nc.gpsimd.memset(ones[:, :], 1.0)
            nc.gpsimd.memset(neg_half[:, :], -0.5).then_inc(made_pool.sem, 1)
            pool.wait_ge(made_pool.sem, 1)
            with pool.Fori(0, B) as b:
                for k in range(4):
                    roots.step(pool, b, k, rstd[:, :], mv[:, :, 1], EPS, neg_half[:, :])

        @block.tensor
        def _(pe):
            pe.wait_ge(weights_in.sem, 16 * N_LOADED)
            pe.wait_ge(made_pool.sem, 1)

            def transpose_hn(b, n):
                pe.wait_ge(hn_ready.sem, hn_ready.at(b, n + 1))
                for k in range(KD):
                    for t in range(NT):
                        last = nc.tensor.transpose(ps_t[k][:, t * P:(t + 1) * P], hn[:, t, k * P:(k + 1) * P],
                                                   ident[:, :])
                    last.then_inc(hT_psum.sem, 1)
                pe.wait_ge(hT_ready.sem, hT_ready.at(b, KD * (n + 1)))

            with pe.Fori(0, B) as b:
                transpose_hn(b, 0)
                for j in range(G):
                    for k in range(KD):
                        last = nc.tensor.matmul(bank[j][:, :], wqk[:, k, HG * j:HG * (j + 1), :], hT[:, k, :],
                                                start=k == 0, stop=k == KD - 1)
                    last.then_inc(q_psum.sem, 1)
                for j in range(G):
                    pe.wait_ge(qsq_ready.sem, qsq_ready.at(b, j + 1))
                    if j >= 2:
                        pe.wait_ge(k_ready.sem, k_ready.at(b, j - 1))
                    for k in range(KD):
                        nc.tensor.matmul(ps_t[j % 2][:, :], wqk[:, k, HG * j:HG * (j + 1), :], hT[:, k, :],
                                         start=k == 0, stop=False)
                    nc.tensor.matmul(ps_t[j % 2][:, :], neg_sum[:, :], qsq[:, j % 2, :], start=False, stop=True)\
                      .then_inc(norms_psum.sem, 1)
                for t in range(NT):
                    for k in range(KD):
                        last = nc.tensor.matmul(bank[t][:, 0:D], hT[:, k, t * P:(t + 1) * P], wv[:, k, :],
                                                start=k == 0, stop=k == KD - 1)
                    last.then_inc(v_psum.sem, 1)
                pe.wait_ge(v_ready.sem, v_ready.at(b, NT))
                pe.wait_ge(k_ready.sem, k_ready.at(b, G))
                pe.wait_ge(q_ready.sem, q_ready.at(b, G))
                for s in range(STEPS + 3):
                    if s < STEPS:
                        hd, i = steps[s]
                        j, r = hd // HG, ROWS * (hd % HG)
                        if s >= 4:
                            pe.wait_ge(probs_ready.sem, probs_ready.at(b, s - 3))
                        nc.tensor.matmul(bank[s % 4][:, :], qT[r:r + ROWS, j, i * P:(i + 1) * P], kT[r:r + ROWS, j, :],
                                         start=True, stop=True).then_inc(scores_ready.sem, 1)
                    u = s - 2
                    if 0 <= u < STEPS:
                        pe.wait_ge(probs_ready.sem, probs_ready.at(b, u + 1))
                        if u >= 2:
                            pe.wait_ge(probsT_ready.sem, probsT_ready.at(b, u - 1))
                        for c in range(NT):
                            last = nc.tensor.transpose(ps_t[u % 2][:, c * P:(c + 1) * P],
                                                       probs[:, u % 4, c * P:(c + 1) * P], ident[:, :])
                        last.then_inc(probsT_psum.sem, 1)
                    u = s - 3
                    if 0 <= u:
                        hd, i = steps[u]
                        pe.wait_ge(probsT_ready.sem, probsT_ready.at(b, u + 1))
                        for c in range(NT):
                            last = nc.tensor.matmul(ps_o[i // 2][:, i % 2, hd * DH:(hd + 1) * DH],
                                                    probsT[:, u % 2, c * P:(c + 1) * P],
                                                    v[:, c, hd * DH:(hd + 1) * DH], start=c == 0, stop=c == NT - 1)
                        last.then_inc(pv_done.sem, 1)
                pe.wait_ge(o_ready.sem, o_ready.at(b, 1))
                for k in range(KD):
                    for t in range(NT):
                        last = nc.tensor.transpose(ps_t[k][:, t * P:(t + 1) * P], o[:, t, k * P:(k + 1) * P],
                                                   ident[:, :])
                    last.then_inc(oT_psum.sem, 1)
                pe.wait_ge(oT_ready.sem, oT_ready.at(b, KD))
                for t in range(NT):
                    for k in range(KD):
                        last = nc.tensor.matmul(ps_o[t // 2][:, t % 2, :], oT[:, k, t * P:(t + 1) * P], wo[:, k, :],
                                                start=k == 0, stop=k == KD - 1)
                    if t % 2:
                        last.then_inc(yt_psum.sem, 1)
                transpose_hn(b, 1)
                for t in range(NT):
                    for k in range(KD):
                        last = nc.tensor.matmul(bank[t][:, 0:D], hT[:, k, t * P:(t + 1) * P], wqc[:, k, :],
                                                start=k == 0, stop=k == KD - 1)
                    last.then_inc(qc_psum.sem, 1)
                for c in range(KD):
                    for k in range(KD):
                        last = nc.tensor.matmul(ps_t[c][:, :], wvc[:, k, c * P:(c + 1) * P], hT[:, k, :],
                                                start=k == 0, stop=k == KD - 1)
                    last.then_inc(vc_psum.sem, 1)
                pe.wait_ge(qc_ready.sem, qc_ready.at(b, NT))
                for c in range(KD):
                    for t in range(NT):
                        last = nc.tensor.matmul(bank[0][:, c * P:(c + 1) * P], qc[:, t, c * P:(c + 1) * P],
                                                qc[:, t, c * P:(c + 1) * P], start=t == 0, stop=t == NT - 1)
                last.then_inc(gram_psum.sem, 1)
                pe.wait_ge(gdiag_ready.sem, gdiag_ready.at(b, 1))
                nc.tensor.matmul(bank[1][:, 0:KD * P], ones[:, :], gdiag[:, :, :], start=True, stop=True)\
                  .then_inc(gnorm_psum.sem, 1)
                pe.wait_ge(cattn_ready.sem, cattn_ready.at(b, 1))
                for c in range(KD):
                    last = nc.tensor.matmul(bank[2][:, c * D:(c + 1) * D], cattn[:, c, :], woc[:, c, :],
                                            start=True, stop=True)
                last.then_inc(mix_psum.sem, 1)
                pe.wait_ge(mix_ready.sem, mix_ready.at(b, 1))
                pe.wait_ge(vc_ready.sem, vc_ready.at(b, KD))
                for t in range(NT):
                    for k in range(KD):
                        last = nc.tensor.matmul(ps_o[t // 2][:, t % 2, :], vcT[:, k, t * P:(t + 1) * P], mix[:, k, :],
                                                start=k == 0, stop=k == KD - 1)
                    if t % 2:
                        last.then_inc(yc_psum.sem, 1)

        @block.scalar
        def _(act):
            act.wait_ge(weights_in.sem, 16 * N_LOADED)
            act.wait_ge(made.sem, 3)

            def evacuate_hT(b, n):
                for k in range(KD):
                    act.wait_ge(hT_psum.sem, hT_psum.at(b, KD * n + k + 1))
                    nc.scalar.activation(hT[:, k, :], ps_t[k][:, :], ACT.Identity, bias=ln[:, 2 * n + 1, k:k + 1],
                                         scale=ln[:, 2 * n, k:k + 1]).then_inc(hT_ready.sem, 1)

            with act.Fori(0, B) as b:
                evacuate_hT(b, 0)
                for j in range(G):
                    act.wait_ge(q_psum.sem, q_psum.at(b, j + 1))
                    if j >= 2:
                        act.wait_ge(norms_psum.sem, norms_psum.at(b, j - 1))
                    nc.scalar.activation(qsq[:, j % 2, :], bank[j][:, :], ACT.Square).then_inc(qsq_ready.sem, 1)
                    if j >= 1:
                        u = j - 1
                        act.wait_ge(norms_psum.sem, norms_psum.at(b, u + 1))
                        nc.scalar.activation(qT[:, u, :], ps_t[u % 2][:, :], ACT.Identity, bias=q_bias[:, u:u + 1],
                                             scale=q_scale[:, u:u + 1]).then_inc(q_ready.sem, 1)
                act.wait_ge(norms_psum.sem, norms_psum.at(b, G))
                nc.scalar.activation(qT[:, G - 1, :], ps_t[(G - 1) % 2][:, :], ACT.Identity, bias=q_bias[:, G - 1:G],
                                     scale=q_scale[:, G - 1:G]).then_inc(q_ready.sem, 1)
                for t in range(NT):
                    act.wait_ge(v_psum.sem, v_psum.at(b, t + 1))
                    nc.scalar.copy(v[:, t, :], bank[t][:, 0:D]).then_inc(v_ready.sem, 1)
                for s in range(STEPS):
                    hd, i = steps[s]
                    act.wait_ge(max_ready.sem, max_ready.at(b, s + 1))
                    if s >= 4:
                        act.wait_ge(probsT_psum.sem, probsT_psum.at(b, s - 3))
                    nc.scalar.activation(probs[:, s % 4, :], bank[s % 4][:, :], ACT.Exp, bias=neg_max[:, s % 4:s % 4 + 1],
                                         accum_out=sums[:, i, hd:hd + 1]).then_inc(probs_ready.sem, 1)
                for k in range(KD):
                    act.wait_ge(oT_psum.sem, oT_psum.at(b, k + 1))
                    nc.scalar.copy(oT[:, k, :], ps_t[k][:, :]).then_inc(oT_ready.sem, 1)
                evacuate_hT(b, 1)
                for t in range(NT):
                    act.wait_ge(qc_psum.sem, qc_psum.at(b, t + 1))
                    nc.scalar.copy(qc[:, t, :], bank[t][:, 0:D]).then_inc(qc_ready.sem, 1)
                for c in range(KD):
                    act.wait_ge(vc_psum.sem, vc_psum.at(b, c + 1))
                    nc.scalar.copy(vcT[:, c, :], ps_t[c][:, :]).then_inc(vc_ready.sem, 1)
                act.wait_ge(cmax_ready.sem, cmax_ready.at(b, 1))
                for c in range(KD):
                    last = nc.scalar.activation(cattn[:, c, :], logits[:, c, :], ACT.Exp, bias=cmax[:, c:c + 1],
                                                accum_out=csum[:, c:c + 1])
                last.then_inc(cexp_ready.sem, 1)

        @block.vector
        def _(dve):
            dve.wait_ge(weights_in.sem, 16 * N_LOADED)
            nc.vector.tensor_scalar(q_scale[:, :], tau[:, :], rows[:, 0:1], C, ALU.mult, ALU.mult)
            nc.vector.tensor_scalar(q_bias[:, :], tau[:, :], rows[:, 1:2], C, ALU.mult, ALU.mult)
            nc.vector.tensor_scalar(tau_c[:, :], tau_c[:, :], CC, None, ALU.mult).then_inc(made.sem, 3)
            dve.wait_ge(made.sem, 3)

            def norm(b, link, n, srcs, dst):
                row_stats(nc, link, srcs, stats, mv, roots.passed_dve.sem).then_inc(roots.given.sem, 1)
                roots.wait(dve, b, n)
                for t in range(NT):
                    last = normalise(nc, dst[:, t, :], srcs[t], mv, rstd, t)
                return last

            tiles = lambda buf: [buf[:, t, :] for t in range(NT)]
            with dve.Fori(0, B) as b:
                link = Order(dve, dve_order, b)
                dve.wait_ge(x_loaded.sem, x_loaded.at(b, 16))
                norm(b, link, 0, tiles(x_in), h).then_inc(x_free.sem, 1)
                dve.wait_ge(x_free.sem, x_free.at(b, 1))
                norm(b, link, 1, tiles(h), hn).then_inc(hn_ready.sem, 1)
                for j in range(G):
                    dve.wait_ge(q_ready.sem, q_ready.at(b, j + 1))
                    nc.vector.tensor_scalar(kT[:, j, :], ps_t[j % 2][:, :], rows[:, 2:3], rows[:, 3:4], ALU.mult,
                                            ALU.add).then_inc(k_ready.sem, 1)
                for s in range(STEPS + 2):
                    if s < STEPS:
                        dve.wait_ge(scores_ready.sem, scores_ready.at(b, s + 1))
                        if s >= 4:
                            dve.wait_ge(probs_ready.sem, probs_ready.at(b, s - 3))
                        nc.vector.tensor_reduce(neg_max[:, s % 4:s % 4 + 1], bank[s % 4][:, :], AX.X, ALU.max,
                                                negate=True).then_inc(max_ready.sem, 1)
                    u = s - 2
                    if 0 <= u:
                        dve.wait_ge(probsT_psum.sem, probsT_psum.at(b, u + 1))
                        if u >= 2:
                            dve.wait_ge(pv_done.sem, pv_done.at(b, u - 1))
                        nc.vector.tensor_copy(probsT[:, u % 2, :], ps_t[u % 2][:, :]).then_inc(probsT_ready.sem, 1)
                dve.wait_ge(probs_ready.sem, probs_ready.at(b, STEPS))
                link(nc.vector.reciprocal(inv[:, :, :], sums[:, :, :]))
                dve.wait_ge(pv_done.sem, pv_done.at(b, STEPS))
                for n in range(2):
                    last = nc.vector.tensor_tensor(
                        o[:, 2 * n:2 * n + 2, :].rearrange("p t (h d) -> p (t h) d", d=DH),
                        ps_o[n][:, :, :].rearrange("p t (h d) -> p (t h) d", d=DH),
                        inv[:, 2 * n:2 * n + 2, :].rearrange("p t h -> p (t h)").unsqueeze(2)
                        .to_broadcast([P, 2 * H, DH]), ALU.mult)
                last.then_inc(o_ready.sem, 1)

                def residual(psum, n):
                    for t in range(NT):
                        if t % 2 == 0:
                            dve.wait_ge(psum.sem, psum.at(b, t // 2 + 1))
                        last = nc.vector.tensor_tensor(y[:, t, :], ps_o[t // 2][:, t % 2, :], gamma[:, n, :], ALU.mult)
                    link(last)
                    link(nc.vector.tensor_tensor(h[:, :, :], h[:, :, :], y[:, :, :], ALU.add))

                residual(yt_psum, 0)
                norm(b, link, 2, tiles(h), hn).then_inc(hn_ready.sem, 1)
                dve.wait_ge(gram_psum.sem, gram_psum.at(b, 1))
                gram = bank[0][:, 0:KD * P].rearrange("p (k d) -> p k d", k=KD)
                gnorm = bank[1][:, 0:KD * P].rearrange("p (k d) -> p k d", k=KD)
                for c in range(KD):
                    last = nc.vector.scalar_tensor_tensor(gdiag[:, c, :], gram[:, c, :], -1.0, ident[:, :], ALU.mult,
                                                          ALU.mult)
                last.then_inc(gdiag_ready.sem, 1)
                dve.wait_ge(gdiag_ready.sem, gdiag_ready.at(b, 1))
                link(nc.vector.tensor_reduce(gsum[:, :], gdiag[:, :, :], AX.X, ALU.add))
                for c in range(KD):
                    last = nc.vector.tensor_scalar(logits[:, c, :], gram[:, c, :], 2.0, gsum[:, c:c + 1], ALU.mult,
                                                   ALU.add)
                link(last)
                dve.wait_ge(gnorm_psum.sem, gnorm_psum.at(b, 1))
                link(nc.vector.tensor_tensor(logits[:, :, :], logits[:, :, :], gnorm, ALU.add))
                for c in range(KD):
                    last = nc.vector.scalar_tensor_tensor(logits[:, c, :], logits[:, c, :], tau_c[:, c:c + 1],
                                                          block_mask[:, :], ALU.mult, ALU.add)
                link(last)
                nc.vector.tensor_reduce(cmax[:, :], logits[:, :, :], AX.X, ALU.max, negate=True)\
                  .then_inc(cmax_ready.sem, 1)
                dve.wait_ge(cexp_ready.sem, cexp_ready.at(b, 1))
                link(nc.vector.reciprocal(cinv[:, :], csum[:, :]))
                for c in range(KD):
                    last = nc.vector.tensor_scalar(cattn[:, c, :], cattn[:, c, :], cinv[:, c:c + 1], None, ALU.mult)
                last.then_inc(cattn_ready.sem, 1)
                dve.wait_ge(mix_psum.sem, mix_psum.at(b, 1))
                nc.vector.tensor_copy(mix[:, :, :].rearrange("p k d -> p (k d)"), bank[2][:, :])\
                  .then_inc(mix_ready.sem, 1)
                residual(yc_psum, 1)
                link(norm(b, link, 3, tiles(h), y))
                dve.wait_ge(res_loaded.sem, res_loaded.at(b, 16))
                nc.vector.tensor_tensor(x_res[:, :, :], x_res[:, :, :], y[:, :, :], ALU.add).then_inc(y_ready.sem, 1)
                link.close()


def expert_mixture(nc, x_dram, out_dram, w, con):
    E, H = 8, 512
    KH = H // P

    with stage(nc) as ctx:
        def sb(name, shape, dt=fp32):
            return ctx.enter_context(nc.sbuf_tensor("d_" + name, shape, dt))

        def signal(name, per_batch=1):
            return Signal(ctx, nc, "d_" + name, per_batch)

        x_in, x_res = sb("x_in", [P, NT, D]), sb("x_res", [P, NT, D])
        h = sb("h", [P, NT, D])
        acc = sb("acc", [P, NT, D])
        y = sb("y", [P, NT, D])
        hT = sb("hT", [P, KD, N])
        z = sb("z", [P, NT, H])
        zn = sb("zn", [P, NT, H])
        gT = sb("gT", [P, 2, KH, N])
        w1, w2 = sb("w1", [P, E, KD, H]), sb("w2", [P, E, KH, D])
        b1 = sb("b1", [P, E, H])
        b2 = sb("b2", [E, D])
        gate_w = sb("gate_w", [P, KD, E])
        gain, bias = sb("gain", [P, E, KH]), sb("bias", [P, E, KH])
        ln_g, ln_b = sb("ln_g", [P, D]), sb("ln_b", [P, D])
        ident, iota = sb("ident", [P, P]), sb("iota", [P, E])
        logits, best = sb("logits", [P, NT, E]), sb("best", [P, NT, 8])
        index = sb("index", [P, NT, 8], mybir.dt.uint32)
        index_f = sb("index_f", [P, NT, 2])
        pair = sb("pair", [P, NT, 2])
        second = sb("second", [P, NT, E])
        combine = sb("combine", [P, NT, P])
        combineT = sb("combineT", [P, N])
        stats, mv, rstd = sb("stats", [P, NT, 6]), sb("mv", [P, NT, 2]), sb("rstd", [P, NT])
        neg_half = sb("neg_half", [P, NT])

        ps_z = [ctx.enter_context(nc.psum_tensor(f"d_ps_z{i}", [P, H], fp32)) for i in range(2)]
        ps_t = [ctx.enter_context(nc.psum_tensor(f"d_ps_t{i}", [P, N], fp32)) for i in range(2)]
        ps_y = [[ctx.enter_context(nc.psum_tensor(f"d_ps_y{i}{j}", [P, 2, D], fp32)) for j in range(2)]
                for i in range(2)]

        weights_in, made_pool = signal("weights_in"), signal("made_pool")
        x_loaded, res_loaded, stored = signal("x_loaded", 16), signal("res_loaded", 16), signal("stored", 16)
        h_ready, y_ready = signal("h_ready"), signal("y_ready")
        hT_psum, hT_ready = signal("hT_psum", KD), signal("hT_ready", KD)
        gates_psum, pair_ready, exp_ready = signal("gates_psum"), signal("pair_ready"), signal("exp_ready")
        combine_ready, combineT_psum, combineT_ready = (signal("combine_ready"), signal("combineT_psum"),
                                                        signal("combineT_ready"))
        b2_psum = signal("b2_psum")
        z_psum, z_read = signal("z_psum", E * NT), signal("z_read", E * NT)
        zn_ready, znT_psum, g_ready = signal("zn_ready", E), signal("znT_psum", E * KH), signal("g_ready", E * KH)
        y_psum, y_read = signal("y_psum", E), signal("y_read", E + 1)
        roots = InverseRoots(ctx, nc, "d_roots", 3 + E)
        dve_order = signal("dve_order", 22)
        loads = []

        x_v = x_dram.rearrange("b (t p) d -> b p t d", p=P)
        out_v = out_dram.rearrange("b (t p) d -> b p t d", p=P)

        block = ctx.enter_context(nc.Block())

        @block.sync
        def _(sp):
            sp.dma_start(x_in[:, :, :], x_v[0]).then_inc(x_loaded.sem, 16)
            loads.append((gate_w[:, :, :], w["gate_w"].rearrange("(k p) e -> p k e", p=P)))
            loads.append((ident[:, :], con["ident"]))
            loads.append((iota[:, :], con["iota"]))
            loads.append((b2[:, :], w["b2"]))
            for dst, name in ((ln_g, "ln_g"), (ln_b, "ln_b")):
                loads.append((dst[:, :], w[name].partition_broadcast(P)))
            loads.append((b1[:, :, :].rearrange("p e h -> p (e h)"),
                          w["b1"].rearrange("e h -> (e h)").partition_broadcast(P)))
            for e in range(E):
                for dst, name in ((gain, "ln1_g"), (bias, "ln1_b")):
                    loads.append((dst[:, e, :], column(w[name][e])))
                loads.append((w1[:, e, :, :], w["w1"][e].rearrange("(k p) h -> p k h", p=P)))
                loads.append((w2[:, e, :, :], w["w2"][e].rearrange("(k p) h -> p k h", p=P)))
            with nc.allow_non_contiguous_dma(reason="a few small vectors, once"):
                for dst, src in loads:
                    sp.dma_start(dst, src).then_inc(weights_in.sem, 16)
            sp.dma_start(x_res[:, :, :], x_v[0]).then_inc(res_loaded.sem, 16)
            with sp.Fori(0, B - 1) as b:
                sp.wait_ge(h_ready.sem, h_ready.at(b, 1))
                sp.dma_start(x_in[:, :, :], x_v[b + 1]).then_inc(x_loaded.sem, 16)
                sp.wait_ge(y_ready.sem, y_ready.at(b, 1))
                sp.dma_start(out_v[b], x_res[:, :, :]).then_inc(stored.sem, 16)
                sp.wait_ge(stored.sem, stored.at(b, 16))
                sp.dma_start(x_res[:, :, :], x_v[b + 1]).then_inc(res_loaded.sem, 16)
            sp.wait_ge(y_ready.sem, B)
            sp.dma_start(out_v[B - 1], x_res[:, :, :]).then_inc(stored.sem, 16)
            sp.wait_ge(stored.sem, 16 * B)

        @block.gpsimd
        def _(pool):
            nc.gpsimd.memset(combine[:, :, :], 0.0)
            nc.gpsimd.memset(neg_half[:, :], -0.5).then_inc(made_pool.sem, 1)
            pool.wait_ge(made_pool.sem, 1)
            with pool.Fori(0, B) as b:
                for k in range(3 + E):
                    roots.step(pool, b, k, rstd[:, :], mv[:, :, 1], EPS, neg_half[:, :])

        @block.tensor
        def _(pe):
            pe.wait_ge(weights_in.sem, 16 * len(loads))
            with pe.Fori(0, B) as b:
                pe.wait_ge(h_ready.sem, h_ready.at(b, 1))
                for k in range(KD):
                    for t in range(NT):
                        last = nc.tensor.transpose(ps_t[k][:, t * P:(t + 1) * P], h[:, t, k * P:(k + 1) * P],
                                                   ident[:, :])
                    last.then_inc(hT_psum.sem, 1)
                pe.wait_ge(hT_ready.sem, hT_ready.at(b, KD))
                for t in range(NT):
                    for k in range(KD):
                        last = nc.tensor.matmul(ps_t[0][:, t * E:(t + 1) * E], hT[:, k, t * P:(t + 1) * P],
                                                gate_w[:, k, :], start=k == 0, stop=k == KD - 1)
                last.then_inc(gates_psum.sem, 1)

                def hidden(e):
                    for t in range(NT):
                        n = e * NT + t
                        if n >= 2:
                            pe.wait_ge(z_read.sem, z_read.at(b, n - 1))
                        for k in range(KD):
                            last = nc.tensor.matmul(ps_z[n % 2][:, :], hT[:, k, t * P:(t + 1) * P], w1[:, e, k, :],
                                                    start=k == 0, stop=k == KD - 1)
                        last.then_inc(z_psum.sem, 1)

                def output(e):
                    pe.wait_ge(zn_ready.sem, zn_ready.at(b, e + 1))
                    for c in range(KH):
                        n = e * KH + c
                        if n >= 2:
                            pe.wait_ge(g_ready.sem, g_ready.at(b, n - 1))
                        for t in range(NT):
                            last = nc.tensor.transpose(ps_t[n % 2][:, t * P:(t + 1) * P], zn[:, t, c * P:(c + 1) * P],
                                                       ident[:, :])
                        last.then_inc(znT_psum.sem, 1)
                    pe.wait_ge(g_ready.sem, g_ready.at(b, (e + 1) * KH))
                    pe.wait_ge(y_read.sem, y_read.at(b, max(e, 1)))
                    for t in range(NT):
                        for c in range(KH):
                            last = nc.tensor.matmul(ps_y[e % 2][t // 2][:, t % 2, :], gT[:, e % 2, c, t * P:(t + 1) * P],
                                                    w2[:, e, c, :], start=c == 0, stop=c == KH - 1)
                    last.then_inc(y_psum.sem, 1)

                hidden(0)
                pe.wait_ge(combine_ready.sem, combine_ready.at(b, 1))
                for t in range(NT):
                    last = nc.tensor.transpose(ps_t[1][:, t * P:(t + 1) * P], combine[:, t, :], ident[:, :])
                last.then_inc(combineT_psum.sem, 1)
                pe.wait_ge(combineT_ready.sem, combineT_ready.at(b, 1))
                for t in range(NT):
                    last = nc.tensor.matmul(ps_y[0][t // 2][:, t % 2, :], combineT[0:E, t * P:(t + 1) * P], b2[:, :],
                                            start=True, stop=True)
                last.then_inc(b2_psum.sem, 1)
                for e in range(1, E + 1):
                    if e < E:
                        hidden(e)
                    output(e - 1)

        @block.scalar
        def _(act):
            act.wait_ge(weights_in.sem, 16 * len(loads))
            with act.Fori(0, B) as b:
                for k in range(KD):
                    act.wait_ge(hT_psum.sem, hT_psum.at(b, k + 1))
                    nc.scalar.copy(hT[:, k, :], ps_t[k][:, :]).then_inc(hT_ready.sem, 1)
                act.wait_ge(pair_ready.sem, pair_ready.at(b, 1))
                nc.scalar.activation(pair[:, :, 1:2], pair[:, :, 1:2], ACT.Exp).then_inc(exp_ready.sem, 1)
                act.wait_ge(combineT_psum.sem, combineT_psum.at(b, 1))
                nc.scalar.copy(combineT[:, :], ps_t[1][:, :]).then_inc(combineT_ready.sem, 1)
                for e in range(E):
                    for c in range(KH):
                        n = e * KH + c
                        act.wait_ge(znT_psum.sem, znT_psum.at(b, n + 1))
                        if e >= 2 and c == 0:
                            act.wait_ge(y_psum.sem, y_psum.at(b, e - 1))
                        nc.scalar.activation(gT[:, e % 2, c, :], ps_t[n % 2][:, :], ACT.Gelu,
                                             bias=bias[:, e, c:c + 1], scale=gain[:, e, c:c + 1])\
                          .then_inc(g_ready.sem, 1)

        @block.vector
        def _(dve):
            dve.wait_ge(weights_in.sem, 16 * len(loads))
            dve.wait_ge(made_pool.sem, 1)

            def norm(b, link, n, srcs, dst):
                row_stats(nc, link, srcs, stats, mv, roots.passed_dve.sem).then_inc(roots.given.sem, 1)
                roots.wait(dve, b, n)
                for t in range(NT):
                    last = normalise(nc, dst[:, t, :], srcs[t], mv, rstd, t)
                return last

            tiles = lambda buf: [buf[:, t, :] for t in range(NT)]
            with dve.Fori(0, B) as b:
                link = Order(dve, dve_order, b)
                dve.wait_ge(x_loaded.sem, x_loaded.at(b, 16))
                norm(b, link, 0, tiles(x_in), h).then_inc(h_ready.sem, 1)
                dve.wait_ge(gates_psum.sem, gates_psum.at(b, 1))
                link(nc.vector.tensor_copy(logits[:, :, :].rearrange("p t e -> p (t e)"), ps_t[0][:, 0:NT * E]),
                     standing=roots.passed_dve.sem)
                for t in range(NT):
                    last = nc.vector.max(best[:, t, :], logits[:, t, :])
                link(last, standing=roots.passed_dve.sem)
                for t in range(NT):
                    last = nc.vector.max_index(index[:, t, :], best[:, t, :], logits[:, t, :])
                link(last)
                nc.vector.tensor_copy(index_f[:, :, :], index[:, :, 0:2])
                nc.vector.tensor_tensor(pair[:, :, 1:2], best[:, :, 1:2], best[:, :, 0:1], ALU.subtract)\
                  .then_inc(pair_ready.sem, 1)
                dve.wait_ge(exp_ready.sem, exp_ready.at(b, 1))
                link(nc.vector.tensor_scalar(pair[:, :, 0:1], pair[:, :, 1:2], 1.0, None, ALU.add))
                link(nc.vector.reciprocal(pair[:, :, 0:1], pair[:, :, 0:1]))
                link(nc.vector.tensor_tensor(pair[:, :, 1:2], pair[:, :, 1:2], pair[:, :, 0:1], ALU.mult))
                for n, dst in ((0, combine), (1, second)):
                    for t in range(NT):
                        last = nc.vector.tensor_scalar(dst[:, t, 0:E], iota[:, :], index_f[:, t, n:n + 1],
                                                       pair[:, t, n:n + 1], ALU.is_equal, ALU.mult)
                link(last)
                nc.vector.tensor_tensor(combine[:, :, 0:E], combine[:, :, 0:E], second[:, :, :], ALU.add)\
                  .then_inc(combine_ready.sem, 1)

                def accumulate(e):
                    dve.wait_ge(y_psum.sem, y_psum.at(b, e + 1))
                    dve.wait_ge(y_read.sem, y_read.at(b, e + 1))
                    for t in range(NT):
                        last = nc.vector.scalar_tensor_tensor(acc[:, t, :], ps_y[e % 2][t // 2][:, t % 2, :],
                                                              combine[:, t, e:e + 1], acc[:, t, :], ALU.mult, ALU.add)
                    last.then_inc(y_read.sem, 1)

                for e in range(E):
                    for t in range(NT):
                        n = e * NT + t
                        dve.wait_ge(z_psum.sem, z_psum.at(b, n + 1))
                        nc.vector.tensor_tensor(z[:, t, :], ps_z[n % 2][:, :], b1[:, e, :], ALU.add)\
                          .then_inc(z_read.sem, 1)
                    dve.wait_ge(z_read.sem, z_read.at(b, (e + 1) * NT))
                    row_stats(nc, link, tiles(z), stats, mv, roots.passed_dve.sem).then_inc(roots.given.sem, 1)
                    if e == 0:
                        dve.wait_ge(b2_psum.sem, b2_psum.at(b, 1))
                        for n in range(2):
                            last = nc.vector.tensor_tensor(acc[:, 2 * n:2 * n + 2, :], h[:, 2 * n:2 * n + 2, :],
                                                           ps_y[0][n][:, :, :], ALU.add)
                        last.then_inc(y_read.sem, 1)
                    if e >= 2:
                        accumulate(e - 2)
                    roots.wait(dve, b, 1 + e)
                    if e >= 1:
                        dve.wait_ge(znT_psum.sem, znT_psum.at(b, e * KH))
                    for t in range(NT):
                        last = normalise(nc, zn[:, t, :], z[:, t, :], mv, rstd, t)
                    last.then_inc(zn_ready.sem, 1)
                    dve.wait_ge(zn_ready.sem, zn_ready.at(b, e + 1))
                accumulate(E - 2)
                accumulate(E - 1)
                dve.wait_ge(y_read.sem, y_read.at(b, E + 1))
                link(norm(b, link, 1 + E, tiles(acc), y))
                link(nc.vector.tensor_tensor(y[:, :, :], y[:, :, :],
                                             ln_g[:, :].unsqueeze(1).to_broadcast([P, NT, D]), ALU.mult))
                link(nc.vector.tensor_tensor(acc[:, :, :], y[:, :, :],
                                             ln_b[:, :].unsqueeze(1).to_broadcast([P, NT, D]), ALU.add))
                link(norm(b, link, 2 + E, tiles(acc), y))
                dve.wait_ge(res_loaded.sem, res_loaded.at(b, 16))
                nc.vector.tensor_tensor(x_res[:, :, :], x_res[:, :, :], y[:, :, :], ALU.add).then_inc(y_ready.sem, 1)
                link.close()


def build(nc, a, con, out):
    under = lambda prefix: {n[len(prefix):]: x for n, x in a.items() if n.startswith(prefix)}
    first, ffn, second, experts = under("L0_attn_"), under("L0_ffn_"), under("L1_attn_"), under("L1_ffn_")
    x1, x2, x3 = (nc.dram_tensor(f"x{n}_dram", (B, N, D), fp32).ap() for n in (1, 2, 3))
    y = [nc.dram_tensor(f"y{n}_dram", (B, N, D), fp32).ap() for n in range(3)]
    differential_attention(nc, first["X"], x1, first["Wq"], first["Wk"], first["Wv"], first["Wo"],
                           [first[n] for n in ("lq1", "lk1", "lq2", "lk2")], first["rms_scale"], con)
    window_attention(nc, x1, y[0], 0, ffn, con)
    gated_ffn(nc, y[0], x1, y[1], 0, ffn, con)
    window_attention(nc, y[1], y[2], 1, ffn, con)
    gated_ffn(nc, y[2], x1, x2, 1, ffn, con)
    diffusion_attention(nc, x2, x3, second, con)
    expert_mixture(nc, x3, out, experts, con)


def mask_constants(np, bf):
    low = -1e30
    q, k = np.arange(128)[:, None], np.arange(128)[None, :]
    con = {"ident": np.eye(128, dtype=np.float32), "ident_h": np.eye(128, dtype=bf)}
    con["causal"] = np.where(k > q, low, 0.0).astype(bf)
    con["map_mask"] = (np.arange(128)[:, None] % 32 // 16 == np.arange(2)[None, :]).astype(np.float32)
    row, head = np.arange(128) % 32, np.arange(128) // 32
    con["rows"] = np.stack([2.0 * (row < 16) + (row == 17), row == 16, row <= 16, row == 17], 1).astype(np.float32)
    same = head[:, None] == head[None, :]
    con["neg_sum"] = (same & (row[:, None] < 16) & ((row == 16) | (row == 17))[None, :]) * np.float32(-1)
    con["block_mask"] = np.where(same, 0.0, low).astype(np.float32)
    before, own = np.where(k < q, low, 0.0), np.where(k > q, low, 0.0)
    first = np.concatenate([np.full_like(before, low), own], 1)
    con["window_mask"] = np.stack([first, np.concatenate([before, own], 1)], 1).astype(bf)
    half = np.arange(0, 64, 2, dtype=np.float32)
    inv_freq = np.float32(1.0) / np.float32(10000.0) ** (half / np.float32(64))
    t = np.arange(512, dtype=np.float32)
    freqs = (t[:, None] * inv_freq[None, :]).astype(np.float64)
    base = (half + np.float32(0.4 * 64)) / np.float32(1.4 * 64)
    scale = base.astype(np.float64)[None, :] ** ((t - 256) / 64.0)[:, None]
    cos, sin = np.cos(freqs), np.sin(freqs)
    both = lambda x: np.concatenate([x, x], 1)
    signed = lambda x: np.concatenate([-x, x], 1)
    con["cos"] = np.stack([both(8 * cos * scale), both(cos / scale)]).astype(np.float32)
    con["sin"] = np.stack([signed(8 * sin * scale), signed(sin / scale)]).astype(np.float32)
    con["iota"] = np.tile(np.arange(8, dtype=np.float32), (128, 1))
    return con


def kernel(**inputs):
    import numpy as _np
    import ml_dtypes as _ml
    import concourse.bacc as _bacc
    from concourse import mybir as _mybir
    from concourse.bass_utils import run_bass_kernel_spmd as _run

    nc = _bacc.Bacc("TRN2", target_bir_lowering=False, num_devices=1)
    arrays, a = {}, {}

    def give(name, x):
        x = _np.ascontiguousarray(x)
        arrays["in_" + name] = x
        return nc.dram_tensor("in_" + name, x.shape, _mybir.dt.from_np(x.dtype), kind="ExternalInput").ap()

    for name, x in inputs.items():
        if name in ("L0_attn_Wq", "L0_attn_Wk", "L0_attn_Wv", "L0_attn_Wo"):
            x = _np.asarray(x).T
        a[name] = give(name, x)
    con = {name: give("con_" + name, x) for name, x in mask_constants(_np, _ml.bfloat16).items()}
    out = nc.dram_tensor("out_0_dram", (8, 512, 256), _mybir.dt.float32, kind="ExternalOutput").ap()
    build(nc, a, con, out)
    r = _run(nc, [arrays], core_ids=[0])
    return r.results[0]["out_0_dram"]
```

```python
import concourse.bass as bass
from concourse import mybir
from contextlib import ExitStack, contextmanager

fp32 = mybir.dt.float32
fp32r = mybir.dt.float32r
bf16 = mybir.dt.bfloat16
ALU = mybir.AluOpType
ACT = mybir.ActivationFunctionType
AX = mybir.AxisListType

B, N, D = 8, 512, 256
P = 128
NT = N // P
KD = D // P
EPS = 1e-5


@contextmanager
def stage(nc):
    with ExitStack() as ctx:
        ctx.semaphores = []
        yield ctx
    nc.clear_and_free_semaphores(ctx.semaphores)
    nc.all_engine_barrier()


class Signal:

    def __init__(self, ctx, nc, name, per_batch):
        self.sem = nc.alloc_semaphore(name=name)
        ctx.semaphores.append(self.sem)
        self.per_batch = per_batch

    def at(self, b, k):
        b, ahead = b if isinstance(b, tuple) else (b, 0)
        return b * self.per_batch + (ahead * self.per_batch + k)


def standing_wait(eng, sem, value, passed):
    eng.wait_ge(sem, value)
    eng.sem_inc(passed, 1)


class Order:

    def __init__(self, eng, steps, b):
        self.eng, self.steps, self.b, self.n = eng, steps, b, 0

    def __call__(self, ins, standing=None):
        self.n += 1
        ins.then_inc(self.steps.sem, 1)
        self.eng.wait_ge(self.steps.sem, self.steps.at(self.b, self.n))
        if standing is not None:
            self.eng.sem_inc(standing, 1)

    def close(self):
        assert self.n == self.steps.per_batch, f"{self.n} links in a batch"


def row_stats(nc, link, srcs, stats, mv, passed):
    for t, src in enumerate(srcs):
        last = nc.vector.bn_stats(stats[:, t, :], src)
    link(last, standing=passed)
    for t in range(len(srcs)):
        last = nc.vector.bn_aggr(mv[:, t, :], stats[:, t, :])
    return last


class InverseRoots:

    def __init__(self, ctx, nc, name, per_batch):
        self.nc = nc
        self.given = Signal(ctx, nc, name + "_given", per_batch)
        self.added = Signal(ctx, nc, name + "_added", per_batch)
        self.passed = Signal(ctx, nc, name + "_passed", 0)
        self.passed_dve = Signal(ctx, nc, name + "_passed_dve", 0)
        self.ready = Signal(ctx, nc, name + "_ready", per_batch)

    def step(self, pool, b, k, out, src, eps, neg_half):
        standing_wait(pool, self.given.sem, self.given.at(b, k + 1), self.passed.sem)
        self.nc.gpsimd.tensor_scalar(out, src, eps, None, ALU.add).then_inc(self.added.sem, 1)
        pool.wait_ge(self.added.sem, self.added.at(b, k + 1))
        self.nc.gpsimd.tensor_tensor(out, out, neg_half, ALU.pow).then_inc(self.ready.sem, 1)

    def wait(self, eng, b, k):
        eng.wait_ge(self.ready.sem, self.ready.at(b, k + 1))


def normalise(nc, dst, src, mv, rstd, t):
    return nc.vector.tensor_scalar(dst, src, mv[:, t, 0:1], rstd[:, t:t + 1], ALU.subtract, ALU.mult)


def column(vec, p=P):
    return vec.rearrange("(n p) -> p n", p=p)


def differential_attention(nc, x_dram, out_dram, wq, wk, wv, wo, lam_vecs, rms_scale, con):
    H, DH, M = 16, 16, 2
    D2 = M * DH * H
    HV = M * DH
    G = D2 // P
    J = 2
    HJ = H // J
    TILES = J * 2 * M
    K_ALL = 4 * DH
    SLOTS = 8
    PAIRS = H // 2
    LAG = 3
    ITERS = H + LAG + 2
    LAMBDA_INIT = 0.8

    UNITS_S = [(0, (0, 1)), (1, (0, 1)), (2, (0,)), (2, (1,)), (3, (0,)), (3, (1,))]
    UNITS_T = [[(0, 0, 0)], [(0, 1, 0)], [(1, 0, 0), (3, 0, 3 * P)], [(1, 1, 0), (3, 1, 3 * P)],
               [(2, 0, 0), (2, 1, 2 * P)]]
    US, UT = len(UNITS_S), len(UNITS_T)

    with stage(nc) as ctx:
        def sb(name, shape, dt=fp32):
            return ctx.enter_context(nc.sbuf_tensor("a_" + name, shape, dt))

        def signal(name, per_batch=1):
            return Signal(ctx, nc, "a_" + name, per_batch)

        x_in = sb("x_in", [P, NT, D])
        x_res = sb("x_res", [P, NT, D])
        h = sb("h", [P, NT, D])
        y = sb("y", [P, NT, D])
        hT = sb("hT", [P, KD, N])
        halves = sb("halves", [P, 4, J, M, N], fp32r)
        packed_qk = sb("packed_qk", [P, 2, SLOTS, M, N], fp32r)
        v = sb("v", [P, NT, H, 2 * HV])
        probsT = sb("probsT", [P, 3, N])
        sumsT = sb("sumsT", [P, 2, N])
        o = sb("o", [P, NT, D2])
        o_tmp = sb("o_tmp", [P, NT, HV])
        oT = sb("oT", [P, G, N])
        wq_sb, wk_sb = sb("wq", [P, KD, M, H, DH]), sb("wk", [P, KD, M, H, DH])
        wv_sb = sb("wv", [P, KD, D2])
        wo_sb = sb("wo", [P, G, D])
        lam_s = sb("lam_s", [P, 2, H])
        neg_lam = sb("neg_lam", [P, H])
        rms_col = sb("rms_col", [P, 1])
        ident = sb("ident", [P, P])
        ident_h = sb("ident_h", [P, P], bf16)
        causal = sb("causal", [P, P], bf16)
        stats, mv, rstd = sb("stats", [P, NT, 6]), sb("mv", [P, NT, 2]), sb("rstd", [P, NT])
        stats_y, mv_y, rstd_y = sb("stats_y", [P, NT, 6]), sb("mv_y", [P, NT, 2]), sb("rstd_y", [P, NT])
        neg_max = sb("neg_max", [P, 2, 2, M, NT])
        max_half = sb("max_half", [2 * M * NT, 2, 2, P], fp32r)
        inv = sb("inv", [P, NT, M])
        oss, orstd = sb("oss", [P, NT * H]), sb("orstd", [P, NT * H])
        neg_half = sb("neg_half", [P, NT * H])
        osq = oT[:, :, :]
        lam_in = y[:, :, :]
        lam_pr = oT[:, 0, :].rearrange("p (n d) -> p n d", n=2)

        ps = [ctx.enter_context(nc.psum_tensor(f"a_ps{i}", [P, N], fp32)) for i in range(8)]
        ps_first, ps_again, ps_o, ps_misc = ps[0:2], ps[2:5], ps[5:7], ps[7]
        bank = ps[0:4]
        ps_oT = ps[4:8]
        y_ps = [ps_o[t // 2][:, (t % 2) * D:(t % 2 + 1) * D] for t in range(NT)]

        weights_in = signal("weights_in")
        x_loaded, res_loaded = signal("x_loaded", 16), signal("res_loaded", 16)
        stored = signal("stored", 16)
        setup_act = signal("setup_act")
        h_ready = signal("h_ready")
        hT_psum, hT_ready = signal("hT_psum", KD), signal("hT_ready", KD)
        proj = signal("proj", TILES)
        highs, lows = signal("highs", TILES), signal("lows", TILES)
        v_psum, v_ready = signal("v_psum", NT), signal("v_ready", NT)
        packed = [signal(f"packed{n}", 16 * 4 * H // SLOTS) for n in range(SLOTS)]
        scores_ready, max_ready = signal("scores_ready", US * H), signal("max_ready", US * H)
        max_psum, max_high, max_low = signal("max_psum", PAIRS), signal("max_high", PAIRS), signal("max_low", PAIRS)
        max_packed = [signal(f"max_packed{n}", 2 * 16 * PAIRS // 2) for n in range(2)]
        scoresT_ready, probs_ready = signal("scoresT_ready", UT * H), signal("probs_ready", UT * H)
        pv_done = signal("pv_done", UT * H)
        sumsT_ready, sums_psum, o_ready = signal("sumsT_ready", H), signal("sums_psum", H), signal("o_ready", H)
        osq_ready, o_normed = signal("osq_ready"), signal("o_normed")
        oT_psum, oT_ready = signal("oT_psum", G), signal("oT_ready", G)
        y_psum, y_free, y_ready = signal("y_psum", 2), signal("y_free"), signal("y_ready")
        half_made, filled = signal("half_made"), signal("filled")
        setup_order = signal("setup_order")
        passed = signal("passed", 0)
        in_order, dve_order = signal("in_order"), signal("dve_order", 3 * H + 1)
        roots_in = InverseRoots(ctx, nc, "a_roots_in", 1)
        roots_o = InverseRoots(ctx, nc, "a_roots_o", 1)
        roots_y = InverseRoots(ctx, nc, "a_roots_y", 1)

        x_v = x_dram.rearrange("b (t p) d -> b p t d", p=P)
        out_v = out_dram.rearrange("b (t p) d -> b p t d", p=P)
        loads = []

        def batches(eng, before, body):
            before(0)
            with eng.Fori(0, B - 1) as b:
                body(b, False)
            body(B - 1, True)

        block = ctx.enter_context(nc.Block())

        @block.sync
        def _(sp):
            sp.dma_start(x_in[:, :, :], x_v[0]).then_inc(x_loaded.sem, 16)
            for dst, src in ((wq_sb, wq), (wk_sb, wk)):
                for m in range(M):
                    for k in range(KD):
                        loads.append((dst[:, k, m, :, :],
                                      src.rearrange("(k p) (h m d) -> k m p h d", p=P, m=M, d=DH)[k, m]))
            for dst, src in ((wv_sb, wv), (wo_sb, wo)):
                loads.append((dst[:, :, :], src.rearrange("(k p) n -> p k n", p=P)))
            for n, vec in enumerate(lam_vecs):
                loads.append((lam_in[:, n, :], vec.rearrange("h d -> (h d)").partition_broadcast(P)))
            for r in range(P // HV):
                loads.append((rms_col[HV * r:HV * r + HV, :], rms_scale.rearrange("(p a) -> p a", a=1)))
            loads.extend([(ident[:, :], con["ident"]), (ident_h[:, :], con["ident_h"]), (causal[:, :], con["causal"])])
            with nc.allow_non_contiguous_dma(reason="weights by map, once"):
                for dst, src in loads:
                    sp.dma_start(dst, src).then_inc(weights_in.sem, 16)
            sp.dma_start(x_res[:, :, :], x_v[0]).then_inc(res_loaded.sem, 16)

            def pack(b, hd):
                slot, j, r = hd % SLOTS, hd // HJ, DH * (hd % HJ)
                for n, pair in enumerate((slice(0, 3, 2), slice(0, 4, 3), slice(1, 3, 1), slice(1, 4, 2))):
                    sp.dma_start(packed_qk[DH * n:DH * (n + 1), :, slot, :, :].bitcast(fp32),
                                 halves[r:r + DH, pair, j, :, :].bitcast(fp32)).then_inc(packed[slot].sem, 16)

            def pack_first(b, after=None):
                standing_wait(sp, lows.sem, lows.at(b, TILES // J), passed.sem)
                for hd in range(SLOTS):
                    if after is not None:
                        sp.wait_ge(scoresT_ready.sem, scoresT_ready.at(after, UT * (hd + SLOTS + 1)))
                    pack(b, hd)

            def body(b, last):
                if not last:
                    sp.wait_ge(h_ready.sem, h_ready.at(b, 1))
                    sp.dma_start(x_in[:, :, :], x_v[b + 1]).then_inc(x_loaded.sem, 16)
                for s in range(2, H + 1):
                    if s % 2 == 0:
                        p = s // 2 - 1
                        sp.wait_ge(max_low.sem, max_low.at(b, p + 1))
                        slot = 2 * p % SLOTS
                        for half in range(2):
                            sp.dma_start(packed_qk[K_ALL + half:K_ALL + half + 1, 0, slot:slot + 2, :, :].bitcast(fp32),
                                         max_half[:, p % 2, half, :].bitcast(fp32)).then_inc(max_packed[p % 2].sem, 16)
                    hd = s + SLOTS - LAG
                    if SLOTS <= hd < H:
                        if hd == SLOTS:
                            standing_wait(sp, lows.sem, lows.at(b, TILES), passed.sem)
                        sp.wait_ge(scoresT_ready.sem, scoresT_ready.at(b, UT * (hd - SLOTS + 1)))
                        pack(b, hd)
                if not last:
                    pack_first((b, 1), b)
                sp.wait_ge(y_ready.sem, y_ready.at(b, 1))
                sp.dma_start(out_v[b], x_res[:, :, :]).then_inc(stored.sem, 16)
                sp.wait_ge(stored.sem, stored.at(b, 16))
                if not last:
                    sp.dma_start(x_res[:, :, :], x_v[b + 1]).then_inc(res_loaded.sem, 16)

            batches(sp, pack_first, body)

        @block.gpsimd
        def _(pool):
            nc.gpsimd.memset(packed_qk[K_ALL:K_ALL + 32, 1, :, :, :].bitcast(fp32), 1.0).then_inc(filled.sem, 1)
            pool.wait_ge(filled.sem, 1)
            nc.gpsimd.memset(v[:, :, :, :], 0.0).then_inc(filled.sem, 1)
            pool.wait_ge(filled.sem, 2)
            nc.gpsimd.memset(v[:, :, :, HV:HV + 1], 1.0)
            nc.gpsimd.memset(neg_half[:, :], -0.5).then_inc(half_made.sem, 1)
            pool.wait_ge(half_made.sem, 1)

            def before(b):
                roots_in.step(pool, b, 0, rstd[:, :], mv[:, :, 1], EPS, neg_half[:, 0:NT])

            def body(b, last):
                if not last:
                    before((b, 1))
                roots_o.step(pool, b, 0, orstd[:, :], oss[:, :], HV * EPS, neg_half[:, :])
                roots_y.step(pool, b, 0, rstd_y[:, :], mv_y[:, :, 1], EPS, neg_half[:, 0:NT])

            batches(pool, before, body)

        @block.tensor
        def _(pe):
            pe.wait_ge(weights_in.sem, 16 * len(loads))
            pe.wait_ge(half_made.sem, 1)

            def project_qk(b):
                pe.wait_ge(h_ready.sem, h_ready.at(b, 1))
                for k in range(KD):
                    for t in range(NT):
                        last = nc.tensor.transpose(bank[k][:, t * P:(t + 1) * P], h[:, t, k * P:(k + 1) * P],
                                                   ident[:, :])
                    last.then_inc(hT_psum.sem, 1)
                pe.wait_ge(hT_ready.sem, hT_ready.at(b, KD))
                for n in range(TILES):
                    j, w, m = n // 4, (wq_sb, wk_sb)[n // 2 % 2], n % 2
                    if n >= 4:
                        pe.wait_ge(lows.sem, lows.at(b, n - 3))
                    for k in range(KD):
                        last = nc.tensor.matmul(bank[n % 4][:, :], w[:, k, m, HJ * j:HJ * (j + 1), :], hT[:, k, :],
                                                start=k == 0, stop=k == KD - 1)
                    last.then_inc(proj.sem, 1)

            def project_v(b):
                for t in range(NT):
                    pe.wait_ge(lows.sem, lows.at(b, 5 + t))
                    for k in range(KD):
                        last = nc.tensor.matmul(bank[t][:, :], hT[:, k, t * P:(t + 1) * P], wv_sb[:, k, :],
                                                start=k == 0, stop=k == KD - 1)
                    last.then_inc(v_psum.sem, 1)

            def scores(b, hd, k):
                if k == 0:
                    pe.wait_ge(packed[hd % SLOTS].sem, packed[hd % SLOTS].at(b, 64 * (hd // SLOTS + 1)))
                i, maps = UNITS_S[k]
                u, keys, slot = US * hd + k, (i + 1) * P, hd % SLOTS
                if u >= 2:
                    pe.wait_ge(max_ready.sem, max_ready.at(b, u - 1))
                for n, m in enumerate(maps):
                    out = ps_first[u % 2][:, n * keys:(n + 1) * keys]
                    nc.tensor.matmul(out, packed_qk[0:K_ALL, 0, slot, m, i * P:(i + 1) * P],
                                     packed_qk[0:K_ALL, 1, slot, m, 0:keys], start=True, stop=False)
                    last = nc.tensor.matmul(out[:, i * P:keys], ident_h[:, :], causal[:, :], start=False, stop=True)
                last.then_inc(scores_ready.sem, 1)

            def scores_again(b, hd, k):
                u, slot = UT * hd + k, hd % SLOTS
                if k == 0 and hd % 2 == 0:
                    group = max_packed[hd // 2 % 2]
                    pe.wait_ge(group.sem, group.at(b, 32 * (hd // 4 + 1)))
                if u >= 3:
                    pe.wait_ge(probs_ready.sem, probs_ready.at(b, u - 2))
                for c, m, at in UNITS_T[k]:
                    cols = N - c * P
                    nc.tensor.matmul(ps_again[u % 3][:, at:at + cols], packed_qk[0:K_ALL + 2, 1, slot, m, c * P:(c + 1) * P],
                                     packed_qk[0:K_ALL + 2, 0, slot, m, c * P:N], start=True, stop=False)
                    last = nc.tensor.matmul(ps_again[u % 3][:, at:at + P], causal[:, :], ident_h[:, :],
                                            start=False, stop=True)
                last.then_inc(scoresT_ready.sem, 1)

            def weigh(b, u):
                hd, k = u // UT, u % UT
                pe.wait_ge(probs_ready.sem, probs_ready.at(b, u + 1))
                if k == 0 and hd >= 2:
                    pe.wait_ge(sumsT_ready.sem, sumsT_ready.at(b, hd - 1))
                for c, m, at in UNITS_T[k]:
                    last = nc.tensor.matmul(ps_o[hd % 2][64 * m:64 * (m + 1), c * P:N], v[:, c, hd, :],
                                            probsT[:, u % 3, at:at + N - c * P], start=c == 0, stop=c == 2)
                last.then_inc(pv_done.sem, 1)

            def transpose_maxima(b, p):
                pe.wait_ge(max_ready.sem, max_ready.at(b, US * 2 * (p + 1)))
                if 2 * p + 1 - LAG > 0:
                    pe.wait_ge(o_ready.sem, o_ready.at(b, 2 * p + 1 - LAG))
                nc.tensor.matmul(ps_misc[0:2 * M * NT, 0:P], neg_max[:, p % 2, :, :, :], ident[:, :],
                                 start=True, stop=True).then_inc(max_psum.sem, 1)

            def transpose_sums(b, hd):
                pe.wait_ge(sumsT_ready.sem, sumsT_ready.at(b, hd + 1))
                if hd >= 1:
                    pe.wait_ge(o_ready.sem, o_ready.at(b, hd))
                pe.wait_ge(max_low.sem, max_low.at(b, min((hd + LAG + 1) // 2, PAIRS)))
                for t in range(NT):
                    last = nc.tensor.transpose(ps_misc[:, t * P:(t + 1) * P], sumsT[:, hd % 2, t * P:(t + 1) * P],
                                               ident[:, :])
                last.then_inc(sums_psum.sem, 1)

            def before(b):
                project_qk(b)
                project_v(b)

            def body(b, last):
                pe.wait_ge(v_ready.sem, v_ready.at(b, NT))
                for s in range(ITERS - 1):
                    for k in range(US):
                        if s < H:
                            scores(b, s, k)
                        if k == 2 and s % 2 == 0 and 2 <= s <= H:
                            transpose_maxima(b, s // 2 - 1)
                        u = UT * (s - LAG) + k
                        if k < UT and 0 <= s - LAG < H:
                            scores_again(b, s - LAG, k)
                        if k < UT and 0 <= u - 2 < UT * H:
                            if u == 2:
                                pe.wait_ge(y_free.sem, y_free.at(b, 1))
                            weigh(b, u - 2)
                        if k == US - 1 and 0 <= s - LAG - 1 < H:
                            transpose_sums(b, s - LAG - 1)
                if not last:
                    project_qk((b, 1))
                pe.wait_ge(o_normed.sem, o_normed.at(b, 1))
                for j in range(G):
                    for t in range(NT):
                        last_t = nc.tensor.transpose(ps_oT[j][:, t * P:(t + 1) * P], o[:, t, j * P:(j + 1) * P],
                                                     ident[:, :])
                    last_t.then_inc(oT_psum.sem, 1)
                if not last:
                    project_v((b, 1))
                pe.wait_ge(oT_ready.sem, oT_ready.at(b, G))
                for t in range(NT):
                    for j in range(G):
                        last_t = nc.tensor.matmul(y_ps[t], oT[:, j, t * P:(t + 1) * P], wo_sb[:, j, :],
                                                  start=j == 0, stop=j == G - 1)
                    if t % 2:
                        last_t.then_inc(y_psum.sem, 1)

            batches(pe, before, body)

        @block.scalar
        def _(act):
            act.wait_ge(setup_order.sem, 2)
            nc.scalar.activation(lam_s[:, :, :], lam_s[:, :, :], ACT.Exp).then_inc(setup_act.sem, 1)
            act.wait_ge(half_made.sem, 1)

            def evacuate_hT(b):
                for k in range(KD):
                    act.wait_ge(hT_psum.sem, hT_psum.at(b, k + 1))
                    nc.scalar.copy(hT[:, k, :], bank[k][:, :]).then_inc(hT_ready.sem, 1)

            def split_high(b, after=None):
                if after is not None:
                    for group in packed:
                        act.wait_ge(group.sem, group.at(after, group.per_batch))
                for n in range(TILES):
                    act.wait_ge(proj.sem, proj.at(b, n + 1))
                    nc.scalar.copy(halves[:, 2 * (n // 2 % 2), n // 4, n % 2, :], bank[n % 4][:, :]).then_inc(highs.sem, 1)

            def evacuate_v(b):
                for t in range(NT):
                    act.wait_ge(v_psum.sem, v_psum.at(b, t + 1))
                    nc.scalar.copy(v[:, t, :, 0:HV], bank[t][:, :].rearrange("p (h d) -> p h d", d=HV))\
                      .then_inc(v_ready.sem, 1)

            def before(b):
                evacuate_hT(b)
                split_high(b)
                evacuate_v(b)

            def body(b, last):
                for s in range(ITERS - 1):
                    for k in range(UT):
                        if 0 <= s - LAG < H:
                            u = UT * (s - LAG) + k
                            act.wait_ge(scoresT_ready.sem, scoresT_ready.at(b, u + 1))
                            if u >= 3:
                                act.wait_ge(pv_done.sem, pv_done.at(b, u - 2))
                            nc.scalar.activation(probsT[:, u % 3, :], ps_again[u % 3][:, :], ACT.Exp, scale=DH ** -0.5)\
                              .then_inc(probs_ready.sem, 1)
                        hd = s - LAG - 1
                        if k == 2 and 0 <= hd < H:
                            act.wait_ge(pv_done.sem, pv_done.at(b, UT * (hd + 1)))
                            if hd >= 2:
                                act.wait_ge(sums_psum.sem, sums_psum.at(b, hd - 1))
                            nc.scalar.copy(sumsT[:, hd % 2, :], ps_o[hd % 2][:, :]).then_inc(sumsT_ready.sem, 1)
                        if k == 3 and s % 2 == 0 and 2 <= s <= H:
                            p = s // 2 - 1
                            act.wait_ge(max_psum.sem, max_psum.at(b, p + 1))
                            if p >= 2:
                                group = max_packed[p % 2]
                                act.wait_ge(group.sem, group.at(b, 32 * (p // 2)))
                            nc.scalar.copy(max_half[:, p % 2, 0, :], ps_misc[0:2 * M * NT, 0:P]).then_inc(max_high.sem, 1)
                if not last:
                    evacuate_hT((b, 1))
                act.wait_ge(o_ready.sem, o_ready.at(b, H))
                nc.scalar.activation(osq, o[:, :, :], ACT.Square).then_inc(osq_ready.sem, 1)
                if not last:
                    split_high((b, 1), b)
                for j in range(G):
                    act.wait_ge(oT_psum.sem, oT_psum.at(b, j + 1))
                    nc.scalar.mul(oT[:, j, :], ps_oT[j][:, :], rms_col[:, :]).then_inc(oT_ready.sem, 1)
                if not last:
                    evacuate_v((b, 1))

            batches(act, before, body)

        @block.vector
        def _(dve):
            dve.wait_ge(weights_in.sem, 16 * len(loads))
            for n in range(2):
                last_n = nc.vector.tensor_tensor(lam_pr[:, n, :], lam_in[:, 2 * n, :], lam_in[:, 2 * n + 1, :], ALU.mult)
            last_n.then_inc(setup_order.sem, 1)
            dve.wait_ge(setup_order.sem, 1)
            nc.vector.tensor_reduce(lam_s[:, :, :], lam_pr.rearrange("p n (h d) -> p n h d", d=DH),
                                    AX.X, ALU.add).then_inc(setup_order.sem, 1)
            nc.vector.tensor_scalar(rms_col[:, :], rms_col[:, :], (1 - LAMBDA_INIT) * (2 * DH) ** 0.5, None,
                                    ALU.mult).then_inc(setup_order.sem, 1)
            dve.wait_ge(setup_act.sem, 1)
            nc.vector.tensor_tensor(neg_lam[:, :], lam_s[:, 1, :], lam_s[:, 0, :], ALU.subtract)\
              .then_inc(setup_order.sem, 1)
            dve.wait_ge(setup_order.sem, 4)
            nc.vector.tensor_scalar(neg_lam[:, :], neg_lam[:, :], LAMBDA_INIT, None, ALU.subtract)\
              .then_inc(setup_order.sem, 1)
            dve.wait_ge(setup_order.sem, 5)
            dve.sem_inc(y_free.sem, 1)

            def norm_stats(b):
                dve.wait_ge(x_loaded.sem, x_loaded.at(b, 16))
                link = Order(dve, in_order, b)
                row_stats(nc, link, [x_in[:, t, :] for t in range(NT)], stats, mv, roots_in.passed_dve.sem)\
                    .then_inc(roots_in.given.sem, 1)
                link.close()

            def norm_input(b):
                roots_in.wait(dve, b, 0)
                for t in range(NT):
                    last_t = normalise(nc, h[:, t, :], x_in[:, t, :], mv, rstd, t)
                last_t.then_inc(h_ready.sem, 1)

            def split_low(b, j):
                for n in range(4 * j, 4 * j + 4):
                    dve.wait_ge(highs.sem, highs.at(b, n + 1))
                    w = 2 * (n // 2 % 2)
                    nc.vector.tensor_tensor(halves[:, w + 1, j, n % 2, :], bank[n % 4][:, :],
                                            halves[:, w, j, n % 2, :].bitcast(fp32), ALU.subtract).then_inc(lows.sem, 1)

            def maxima(b, hd, k):
                i, maps = UNITS_S[k]
                u, keys = US * hd + k, (i + 1) * P
                dve.wait_ge(scores_ready.sem, scores_ready.at(b, u + 1))
                if hd % 2 == 0 and k == 0 and hd >= 4:
                    dve.wait_ge(max_psum.sem, max_psum.at(b, hd // 2 - 1))
                nc.vector.tensor_reduce(neg_max[:, hd // 2 % 2, hd % 2, maps[0]:maps[-1] + 1, i],
                                        ps_first[u % 2][:, 0:len(maps) * keys].rearrange("p (m n) -> p m n", n=keys),
                                        AX.X, ALU.max, negate=True).then_inc(max_ready.sem, 1)

            def combine(b, link, hd):
                dve.wait_ge(sums_psum.sem, sums_psum.at(b, hd + 1))
                sums = ps_misc[:, :].rearrange("p (t m d) -> p t m d", t=NT, m=M)
                link(nc.vector.reciprocal(inv[:, :, :], sums[:, :, :, HV]))
                link(nc.vector.tensor_scalar(inv[:, :, 1], inv[:, :, 1], neg_lam[:, hd:hd + 1], None, ALU.mult))
                o_head = o[:, :, HV * hd:HV * (hd + 1)]
                for dst, m in ((o_head, 0), (o_tmp[:, :, :], 1)):
                    last_m = nc.vector.tensor_tensor(dst, sums[:, :, m, 0:HV],
                                                     inv[:, :, m].unsqueeze(2).to_broadcast([P, NT, HV]), ALU.mult)
                link(last_m)
                nc.vector.tensor_tensor(o_head, o_head, o_tmp[:, :, :], ALU.add).then_inc(o_ready.sem, 1)

            def before(b):
                norm_stats(b)
                norm_input(b)
                split_low(b, 0)
                split_low(b, 1)

            def body(b, last):
                link = Order(dve, dve_order, b)
                for s in range(ITERS):
                    for k in range(US):
                        if s < H:
                            maxima(b, s, k)
                        if k == 1 and 0 <= s - LAG - 2 < H:
                            combine(b, link, s - LAG - 2)
                        if k == 4 and s % 2 == 0 and 2 <= s <= H:
                            p = s // 2 - 1
                            dve.wait_ge(max_high.sem, max_high.at(b, p + 1))
                            nc.vector.tensor_tensor(max_half[:, p % 2, 1, :], ps_misc[0:2 * M * NT, 0:P],
                                                    max_half[:, p % 2, 0, :].bitcast(fp32), ALU.subtract)\
                              .then_inc(max_low.sem, 1)
                        if not last and k == 3 and s == H // 2:
                            norm_stats((b, 1))
                        if not last and k == 3 and s == H // 2 + 1:
                            norm_input((b, 1))
                dve.wait_ge(osq_ready.sem, osq_ready.at(b, 1))
                nc.vector.tensor_reduce(oss[:, :], osq.rearrange("p t (h d) -> p (t h) d", h=H), AX.X,
                                        ALU.add).then_inc(roots_o.given.sem, 1)
                if not last:
                    split_low((b, 1), 0)
                roots_o.wait(dve, b, 0)
                o_heads = o[:, :, :].rearrange("p t (h d) -> p (t h) d", h=H)
                nc.vector.tensor_tensor(o_heads, o_heads, orstd[:, :].unsqueeze(2).to_broadcast([P, NT * H, HV]),
                                        ALU.mult).then_inc(o_normed.sem, 1)
                if not last:
                    split_low((b, 1), 1)
                dve.wait_ge(y_psum.sem, y_psum.at(b, 2))
                dve.wait_ge(res_loaded.sem, res_loaded.at(b, 16))
                row_stats(nc, link, y_ps, stats_y, mv_y, roots_y.passed_dve.sem).then_inc(roots_y.given.sem, 1)
                roots_y.wait(dve, b, 0)
                for t in range(NT):
                    last_t = normalise(nc, y[:, t, :], y_ps[t], mv_y, rstd_y, t)
                last_t.then_inc(y_free.sem, 1)
                dve.wait_ge(y_free.sem, y_free.at(b, 2))
                nc.vector.tensor_tensor(x_res[:, :, :], x_res[:, :, :], y[:, :, :], ALU.add).then_inc(y_ready.sem, 1)
                link.close()

            batches(dve, before, body)


def window_attention(nc, x_dram, out_dram, layer, w, con):
    H, DH = 8, 64
    INNER = H * DH
    J = INNER // P
    STEPS = H
    W = 2 * P
    FIRST = layer == 0
    QK = 2 * NT

    with stage(nc) as ctx:
        def sb(name, shape, dt=fp32):
            return ctx.enter_context(nc.sbuf_tensor(f"w{layer}_" + name, shape, dt))

        def signal(name, per_batch=1):
            return Signal(ctx, nc, f"w{layer}_" + name, per_batch)

        x_in, h = sb("x_in", [P, NT, D]), sb("h", [P, NT, D])
        out_sb = sb("out", [P, NT, D])
        hT = sb("hT", [P, KD, N + 1])
        sq = sb("sq", [P, 2, INNER])
        rope = sb("rope", [P, QK, INNER])
        crossed = sb("crossed", [P, 2, INNER])
        qkT = sb("qkT", [P, 2, J, N])
        v = sb("v", [P, NT, INNER])
        probs = sb("probs", [P, 2, NT, W])
        probsT = sb("probsT", [P, 2, NT, W])
        o, oT = sb("o", [P, NT, INNER]), sb("oT", [P, J, N])
        wqkv, wo = sb("wqkv", [P, KD, 3 * INNER]), sb("wo", [P, J, D])
        ident, ident_h = sb("ident", [P, P]), sb("ident_h", [P, P], bf16)
        mask = sb("mask", [P, 2, W], bf16)
        cos, sin = sb("cos", [P, 2, NT, DH]), sb("sin", [P, 2, NT, DH])
        scale, crossed_scale = sb("scale", [P, 2, DH]), sb("crossed_scale", [P, 2, DH])
        ss, inv_norm = sb("ss", [P, QK, H]), sb("inv_norm", [P, QK, H])
        stats, mv, rstd = sb("stats", [P, NT, 6]), sb("mv", [P, NT, 2]), sb("rstd", [P, NT])
        neg_half = sb("neg_half", [P, H])
        neg_max = sb("neg_max", [P, 2, NT])
        sums, inv = sb("sums", [P, 2, NT]), sb("inv", [P, 2, NT])

        ps_s = [ctx.enter_context(nc.psum_tensor(f"w{layer}_ps_s{i}", [P, NT, W], fp32)) for i in range(2)]
        ps_t = ctx.enter_context(nc.psum_tensor(f"w{layer}_ps_t", [P, NT, W], fp32))
        ps_o = [ctx.enter_context(nc.psum_tensor(f"w{layer}_ps_o{i}", [P, N], fp32)) for i in range(2)]
        halves = lambda ps: [ps[:, 2 * i:2 * i + 2, :].rearrange("p t n -> p (t n)") for i in range(2)]
        bank = halves(ps_s[0]) + halves(ps_s[1])
        bank2 = halves(ps_t) + [ps_o[0][:, :], ps_o[1][:, :]]

        weights_in, made, made_pool = signal("weights_in"), signal("made"), signal("made_pool")
        x_loaded, stored = signal("x_loaded", 16), signal("stored", 16)
        x_free, h_ready, y_ready = signal("x_free"), signal("h_ready"), signal("y_ready")
        hT_psum, hT_ready = signal("hT_psum", KD), signal("hT_ready", KD)
        qk_psum, v_psum, v_ready = signal("qk_psum", QK), signal("v_psum", NT), signal("v_ready", NT)
        sq_ready, qk_read, ss_ready = signal("sq_ready", QK), signal("qk_read", QK), signal("ss_ready", QK)
        pool_order, rope_ready = signal("pool_order", 3 * QK), signal("rope_ready", QK)
        qkT_psum, qkT_act, qkT_dve = signal("qkT_psum", 2 * J), signal("qkT_act", J), signal("qkT_dve", J)
        scores_ready, max_ready, probs_ready = (signal("scores_ready", STEPS), signal("max_ready", STEPS),
                                                signal("probs_ready", STEPS))
        probsT_psum, probsT_ready = signal("probsT_psum", STEPS), signal("probsT_ready", STEPS)
        pv_done, o_read = signal("pv_done", STEPS), signal("o_read", STEPS)
        oT_psum, oT_ready, y_psum = signal("oT_psum", J), signal("oT_ready", J), signal("y_psum")
        passed, out_free = signal("passed"), signal("out_free")
        if FIRST:
            roots = InverseRoots(ctx, nc, "w_roots", 1)
        dve_order = signal("dve_order", STEPS + FIRST)
        loads = []

        x_v = x_dram.rearrange("b (t p) d -> b p t d", p=P)
        out_v = out_dram.rearrange("b (t p) d -> b p t d", p=P)
        block = ctx.enter_context(nc.Block())

        @block.sync
        def _(sp):
            sp.dma_start(x_in[:, :, :], x_v[0]).then_inc(x_loaded.sem, 16)
            loads.append((wqkv[:, :, :], w["wqkv"][layer].rearrange("(k p) n -> p k n", p=P)))
            loads.append((wo[:, :, :], w["wo"][layer].rearrange("(k p) n -> p k n", p=P)))
            for n, name in enumerate(("q_scale", "k_scale")):
                vec = w[name][layer]
                loads.append((scale[:, n, :], vec.partition_broadcast(P)))
                for half in range(2):
                    other = 32 * (1 - half)
                    loads.append((crossed_scale[:, n, 32 * half:32 * half + 32],
                                  vec[other:other + 32].partition_broadcast(P)))
            for dst, name in ((ident, "ident"), (ident_h, "ident_h")):
                loads.append((dst[:, :], con[name]))
            loads.append((mask[:, :, :], con["window_mask"]))
            loads.append((cos[:, :, :, :], con["cos"].rearrange("c (t p) d -> p c t d", p=P)))
            loads.append((sin[:, :, :, :], con["sin"].rearrange("c (t p) d -> p c t d", p=P)))
            for dst, src in loads:
                sp.dma_start(dst, src).then_inc(weights_in.sem, 16)
            sp.sem_inc(out_free.sem, 1)
            with sp.Fori(0, B - 1) as b:
                sp.wait_ge(x_free.sem, x_free.at(b, 1))
                sp.dma_start(x_in[:, :, :], x_v[b + 1]).then_inc(x_loaded.sem, 16)
                sp.wait_ge(y_ready.sem, y_ready.at(b, 1))
                sp.dma_start(out_v[b], out_sb[:, :, :]).then_inc(stored.sem, 16)
                sp.wait_ge(stored.sem, stored.at(b, 16))
                sp.sem_inc(out_free.sem, 1)
            sp.wait_ge(y_ready.sem, B)
            sp.dma_start(out_v[B - 1], out_sb[:, :, :]).then_inc(stored.sem, 16)
            sp.wait_ge(stored.sem, 16 * B)

        @block.gpsimd
        def _(pool):
            nc.gpsimd.memset(hT[:, 1, 0:1], 0.0)
            nc.gpsimd.memset(neg_half[:, :], -0.5).then_inc(made_pool.sem, 1)
            pool.wait_ge(made_pool.sem, 1)
            with pool.Fori(0, B) as b:
                if FIRST:
                    roots.step(pool, b, 0, rstd[:, :], mv[:, :, 1], EPS, neg_half[:, 0:NT])
                link = Order(pool, pool_order, b)
                for n in range(QK):
                    pool.wait_ge(ss_ready.sem, ss_ready.at(b, n + 1))
                    pool.sem_inc(passed.sem, 1)
                    link(nc.gpsimd.tensor_scalar(inv_norm[:, n, :], ss[:, n, :], 1e-24, None, ALU.max))
                    link(nc.gpsimd.tensor_tensor(inv_norm[:, n, :], inv_norm[:, n, :], neg_half[:, :], ALU.pow))
                    link(nc.gpsimd.tensor_tensor(rope[:, n, :], rope[:, n, :], crossed[:, n % 2, :], ALU.add))
                    heads = rope[:, n, :].rearrange("p (h d) -> p h d", d=DH)
                    nc.gpsimd.tensor_tensor(heads, heads, inv_norm[:, n, :].unsqueeze(2).to_broadcast([P, H, DH]),
                                            ALU.mult).then_inc(rope_ready.sem, 1)

        @block.tensor
        def _(pe):
            pe.wait_ge(weights_in.sem, 16 * len(loads))
            with pe.Fori(0, B) as b:
                pe.wait_ge(h_ready.sem, h_ready.at(b, 1))
                for k in range(KD):
                    for t in range(NT):
                        last = nc.tensor.transpose(bank2[k][:, t * P:(t + 1) * P], h[:, t, k * P:(k + 1) * P],
                                                   ident[:, :])
                    last.then_inc(hT_psum.sem, 1)
                pe.wait_ge(hT_ready.sem, hT_ready.at(b, KD))
                for n in range(3 * NT):
                    t, c = n // 3, n % 3
                    if n >= 4:
                        tf, cf = (n - 4) // 3, (n - 4) % 3
                        free, k = (v_ready, tf + 1) if cf == 2 else (qk_read, 2 * tf + cf + 1)
                        pe.wait_ge(free.sem, free.at(b, k))
                    for k in range(KD):
                        last = nc.tensor.matmul(bank[n % 4], hT[:, k, t * P:(t + 1) * P],
                                                wqkv[:, k, c * INNER:(c + 1) * INNER], start=k == 0, stop=k == KD - 1)
                    last.then_inc((v_psum if c == 2 else qk_psum).sem, 1)
                pe.wait_ge(rope_ready.sem, rope_ready.at(b, QK))
                for n in range(2 * J):
                    c, j = n // J, n % J
                    if n >= 4:
                        free = (qkT_act, qkT_dve)[n % 2]
                        pe.wait_ge(free.sem, free.at(b, (n - 4) // 2 + 1))
                    for t in range(NT):
                        last = nc.tensor.transpose(bank2[n % 4][:, t * P:(t + 1) * P],
                                                   rope[:, 2 * t + c, j * P:(j + 1) * P], ident[:, :])
                    last.then_inc(qkT_psum.sem, 1)
                pe.wait_ge(qkT_act.sem, qkT_act.at(b, J))
                pe.wait_ge(qkT_dve.sem, qkT_dve.at(b, J))
                pe.wait_ge(v_ready.sem, v_ready.at(b, NT))
                for s in range(STEPS + 2):
                    if s < STEPS:
                        j, r = s // 2, DH * (s % 2)
                        if s >= 2:
                            pe.wait_ge(probs_ready.sem, probs_ready.at(b, s - 1))
                        for t in range(NT):
                            out = ps_s[s % 2][:, t, :]
                            nc.tensor.matmul(out, ident_h[:, :], mask[:, min(t, 1), :], start=True, stop=False)
                            keys = slice(max(t - 1, 0) * P, (t + 1) * P)
                            last = nc.tensor.matmul(out if t else out[:, P:W], qkT[r:r + DH, 0, j, t * P:(t + 1) * P],
                                                    qkT[r:r + DH, 1, j, keys], start=False, stop=True)
                        last.then_inc(scores_ready.sem, 1)
                    u = s - 1
                    if 0 <= u < STEPS:
                        pe.wait_ge(probs_ready.sem, probs_ready.at(b, u + 1))
                        if u >= 1:
                            pe.wait_ge(probsT_ready.sem, probsT_ready.at(b, u))
                        for t in range(NT):
                            for c in range(2):
                                last = nc.tensor.transpose(ps_t[:, t, c * P:(c + 1) * P],
                                                           probs[:, u % 2, t, c * P:(c + 1) * P], ident[:, :])
                        last.then_inc(probsT_psum.sem, 1)
                    u = s - 2
                    if 0 <= u:
                        pe.wait_ge(probsT_ready.sem, probsT_ready.at(b, u + 1))
                        if u >= 2:
                            pe.wait_ge(o_read.sem, o_read.at(b, u - 1))
                        for t in range(NT):
                            for c in range(0 if t else 1, 2):
                                last = nc.tensor.matmul(ps_o[u % 2][:, t * DH:(t + 1) * DH],
                                                        probsT[:, u % 2, t, c * P:(c + 1) * P],
                                                        v[:, t - 1 + c, u * DH:(u + 1) * DH],
                                                        start=c == (0 if t else 1), stop=c == 1)
                        last.then_inc(pv_done.sem, 1)
                pe.wait_ge(o_read.sem, o_read.at(b, STEPS))
                for j in range(J):
                    for t in range(NT):
                        last = nc.tensor.transpose(bank[j][:, t * P:(t + 1) * P], o[:, t, j * P:(j + 1) * P],
                                                   ident[:, :])
                    last.then_inc(oT_psum.sem, 1)
                pe.wait_ge(oT_ready.sem, oT_ready.at(b, J))
                for t in range(NT):
                    for j in range(J):
                        last = nc.tensor.matmul(ps_t[:, t, :], oT[:, j, t * P:(t + 1) * P], wo[:, j, :],
                                                start=j == 0, stop=j == J - 1)
                last.then_inc(y_psum.sem, 1)

        @block.scalar
        def _(act):
            act.wait_ge(made_pool.sem, 1)
            with act.Fori(0, B) as b:
                for k in range(KD):
                    act.wait_ge(hT_psum.sem, hT_psum.at(b, k + 1))
                    nc.scalar.copy(hT[:, k, k:k + N], bank2[k]).then_inc(hT_ready.sem, 1)
                for t in range(NT):
                    for c in range(2):
                        n = 2 * t + c
                        act.wait_ge(qk_psum.sem, qk_psum.at(b, n + 1))
                        if n >= 2:
                            act.wait_ge(ss_ready.sem, ss_ready.at(b, n - 1))
                        nc.scalar.activation(sq[:, n % 2, :], bank[(3 * t + c) % 4], ACT.Square)\
                          .then_inc(sq_ready.sem, 1)
                    act.wait_ge(v_psum.sem, v_psum.at(b, t + 1))
                    nc.scalar.copy(v[:, t, :], bank[(3 * t + 2) % 4]).then_inc(v_ready.sem, 1)
                for n in range(0, 2 * J, 2):
                    act.wait_ge(qkT_psum.sem, qkT_psum.at(b, n + 1))
                    nc.scalar.copy(qkT[:, n // J, n % J, :], bank2[n % 4]).then_inc(qkT_act.sem, 1)
                for s in range(STEPS):
                    act.wait_ge(max_ready.sem, max_ready.at(b, s + 1))
                    if s >= 2:
                        act.wait_ge(probsT_psum.sem, probsT_psum.at(b, s - 1))
                        act.wait_ge(o_read.sem, o_read.at(b, s - 1))
                    for t in range(NT):
                        last = nc.scalar.activation(probs[:, s % 2, t, :], ps_s[s % 2][:, t, :], ACT.Exp,
                                                    bias=neg_max[:, s % 2, t:t + 1],
                                                    accum_out=sums[:, s % 2, t:t + 1])
                    last.then_inc(probs_ready.sem, 1)
                for j in range(J):
                    act.wait_ge(oT_psum.sem, oT_psum.at(b, j + 1))
                    nc.scalar.copy(oT[:, j, :], bank[j]).then_inc(oT_ready.sem, 1)

        @block.vector
        def _(dve):
            dve.wait_ge(weights_in.sem, 16 * len(loads))
            for c in range(2):
                for table, factor in ((cos, scale), (sin, crossed_scale)):
                    last = nc.vector.tensor_tensor(table[:, c, :, :], table[:, c, :, :],
                                                   factor[:, c, :].unsqueeze(1).to_broadcast([P, NT, DH]), ALU.mult)
            last.then_inc(made.sem, 1)
            dve.wait_ge(made.sem, 1)
            with dve.Fori(0, B) as b:
                link = Order(dve, dve_order, b)
                dve.wait_ge(x_loaded.sem, x_loaded.at(b, 16))
                if FIRST:
                    row_stats(nc, link, [x_in[:, t, :] for t in range(NT)], stats, mv, roots.passed_dve.sem)\
                        .then_inc(roots.given.sem, 1)
                    roots.wait(dve, b, 0)
                    for t in range(NT):
                        last = normalise(nc, h[:, t, :], x_in[:, t, :], mv, rstd, t)
                else:
                    last = nc.vector.tensor_copy(h[:, :, :], x_in[:, :, :])
                last.then_inc(h_ready.sem, 1)
                dve.wait_ge(h_ready.sem, h_ready.at(b, 1))
                nc.vector.sem_inc(x_free.sem, 1)
                for t in range(NT):
                    for c in range(2):
                        n = 2 * t + c
                        src = bank[(3 * t + c) % 4].rearrange("p (h s d) -> p h s d", s=2, d=DH // 2)
                        straight = rope[:, n, :].rearrange("p (h d) -> p h d", d=DH)
                        across = crossed[:, n % 2, :].rearrange("p (h s d) -> p h s d", s=2, d=DH // 2)
                        dve.wait_ge(sq_ready.sem, sq_ready.at(b, n + 1))
                        nc.vector.tensor_tensor(straight, bank[(3 * t + c) % 4].rearrange("p (h d) -> p h d", d=DH),
                                                cos[:, c, t, :].unsqueeze(1).to_broadcast([P, H, DH]), ALU.mult)
                        if n >= 2:
                            dve.wait_ge(pool_order.sem, pool_order.at(b, 3 * (n - 1)))
                        for half in range(2):
                            last = nc.vector.tensor_tensor(
                                across[:, :, half, :], src[:, :, 1 - half, :],
                                sin[:, c, t, 32 * half:32 * half + 32].unsqueeze(1).to_broadcast([P, H, DH // 2]),
                                ALU.mult)
                        last.then_inc(qk_read.sem, 1)
                        nc.vector.tensor_reduce(ss[:, n, :], sq[:, n % 2, :].rearrange("p (h d) -> p h d", d=DH), AX.X,
                                                ALU.add).then_inc(ss_ready.sem, 1)
                for n in range(1, 2 * J, 2):
                    dve.wait_ge(qkT_psum.sem, qkT_psum.at(b, n + 1))
                    nc.vector.tensor_copy(qkT[:, n // J, n % J, :], bank2[n % 4]).then_inc(qkT_dve.sem, 1)
                for s in range(STEPS + 2):
                    if s < STEPS:
                        dve.wait_ge(scores_ready.sem, scores_ready.at(b, s + 1))
                        if s >= 2:
                            dve.wait_ge(probs_ready.sem, probs_ready.at(b, s - 1))
                        nc.vector.tensor_reduce(neg_max[:, s % 2, :], ps_s[s % 2][:, :, :], AX.X, ALU.max,
                                                negate=True).then_inc(max_ready.sem, 1)
                    u = s - 1
                    if 0 <= u < STEPS:
                        dve.wait_ge(probsT_psum.sem, probsT_psum.at(b, u + 1))
                        if u >= 2:
                            dve.wait_ge(pv_done.sem, pv_done.at(b, u - 1))
                        nc.vector.tensor_copy(probsT[:, u % 2, :, :], ps_t[:, :, :]).then_inc(probsT_ready.sem, 1)
                    u = s - 2
                    if 0 <= u:
                        link(nc.vector.reciprocal(inv[:, u % 2, :], sums[:, u % 2, :]))
                        dve.wait_ge(pv_done.sem, pv_done.at(b, u + 1))
                        nc.vector.tensor_tensor(o[:, :, u * DH:(u + 1) * DH],
                                                ps_o[u % 2][:, 0:NT * DH].rearrange("p (t d) -> p t d", d=DH),
                                                inv[:, u % 2, :].unsqueeze(2).to_broadcast([P, NT, DH]), ALU.mult)\
                          .then_inc(o_read.sem, 1)
                dve.wait_ge(y_psum.sem, y_psum.at(b, 1))
                dve.wait_ge(out_free.sem, out_free.at(b, 1))
                nc.vector.tensor_tensor(out_sb[:, :, :], h[:, :, :], ps_t[:, :, :], ALU.add).then_inc(y_ready.sem, 1)
                dve.wait_ge(y_ready.sem, y_ready.at(b, 1))
                link.close()


def gated_ffn(nc, y_dram, x_dram, out_dram, layer, w, con):
    HID = 682
    CK = -(-HID // P)
    LAST = layer == 1

    with stage(nc) as ctx:
        def sb(name, shape, dt=fp32):
            return ctx.enter_context(nc.sbuf_tensor(f"f{layer}_" + name, shape, dt))

        def signal(name, per_batch=1):
            return Signal(ctx, nc, f"f{layer}_" + name, per_batch)

        shifted = sb("shifted", [P, NT, D])
        y_res = sb("y_res", [P, NT, D])
        x_res = sb("x_res", [P, NT, D])
        out_sb, yn = sb("out", [P, NT, D]), sb("yn", [P, NT, D])
        hn, hT = sb("hn", [P, NT, D]), sb("hT", [P, KD, N])
        gated = sb("gated", [P, CK, N])
        gelu = sb("gelu", [P, 2, N])
        w1, w2 = sb("w1", [P, KD, 2 * HID]), sb("w2", [P, CK, D])
        b1, b2 = sb("b1", [P, 2, CK]), sb("b2", [P, D])
        ln = sb("ln", [P, 2, KD])
        ident = sb("ident", [P, P])
        stats, mv, rstd = sb("stats", [P, NT, 6]), sb("mv", [P, NT, 2]), sb("rstd", [P, NT])
        neg_half = sb("neg_half", [P, NT])

        ps_a = [ctx.enter_context(nc.psum_tensor(f"f{layer}_ps_a{i}", [P, N], fp32)) for i in range(2)]
        ps_g = [ctx.enter_context(nc.psum_tensor(f"f{layer}_ps_g{i}", [P, N], fp32)) for i in range(2)]
        ps_t = [ctx.enter_context(nc.psum_tensor(f"f{layer}_ps_t{i}", [P, N], fp32)) for i in range(2)]
        ps_y = ctx.enter_context(nc.psum_tensor(f"f{layer}_ps_y", [P, NT, D], fp32))

        weights_in, made_pool = signal("weights_in"), signal("made_pool")
        loaded, res_loaded, stored = signal("loaded", 3 * 16), signal("res_loaded", (1 + LAST) * 16), signal("stored", 16)
        hn_ready, y_ready = signal("hn_ready"), signal("y_ready")
        hT_psum, hT_ready = signal("hT_psum", KD), signal("hT_ready", KD)
        a_psum, g_psum = signal("a_psum", CK), signal("g_psum", CK)
        gelu_ready, gated_ready = signal("gelu_ready", CK), signal("gated_ready", CK)
        y_psum = signal("y_psum")
        roots = InverseRoots(ctx, nc, f"f{layer}_roots", 1 + LAST)
        dve_order = signal("dve_order", 2 + 3 * LAST)
        loads = []

        y_v = y_dram.rearrange("b (t p) d -> b p t d", p=P)
        x_v = x_dram.rearrange("b (t p) d -> b p t d", p=P)
        out_v = out_dram.rearrange("b (t p) d -> b p t d", p=P)
        part = lambda c: min(P, HID - c * P)
        block = ctx.enter_context(nc.Block())

        @block.sync
        def _(sp):
            def load(b):
                half = D // 2
                sp.dma_start(shifted[:, :, 0:half], y_v[b][:, :, 0:half]).then_inc(loaded.sem, 16)
                sp.dma_start(shifted[:, 1:NT, half:D],
                             y_dram[b][P - 1:N - 1, half:D].rearrange("(t p) d -> p t d", p=P)).then_inc(loaded.sem, 16)
                sp.dma_start(shifted[1:P, 0, half:D], y_dram[b][0:P - 1, half:D]).then_inc(loaded.sem, 16)

            def load_residuals(b):
                sp.dma_start(y_res[:, :, :], y_v[b]).then_inc(res_loaded.sem, 16)
                if LAST:
                    sp.dma_start(x_res[:, :, :], x_v[b]).then_inc(res_loaded.sem, 16)

            full = (CK - 1) * P
            for lo, n in ((0, 0), (HID, 1)):
                vec = w["b1"][layer]
                loads.append((b1[:, n, 0:CK - 1], column(vec[lo:lo + full])))
                loads.append((b1[0:HID - full, n, CK - 1:CK], vec[lo + full:lo + HID].rearrange("(p a) -> p a", a=1)))
            loads.append((w1[:, :, :], w["w1"][layer].rearrange("(k p) n -> p k n", p=P)))
            loads.append((w2[:, 0:CK - 1, :], w["w2"][layer][0:full, :].rearrange("(k p) n -> p k n", p=P)))
            loads.append((w2[0:HID - full, CK - 1, :], w["w2"][layer][full:HID, :]))
            loads.append((b2[:, :], w["b2"][layer].partition_broadcast(P)))
            for n, name in enumerate(("ln_g", "ln_b")):
                loads.append((ln[:, n, :], column(w[name][layer])))
            loads.append((ident[:, :], con["ident"]))
            load(0)
            with nc.allow_non_contiguous_dma(reason="a few small vectors, once"):
                for dst, src in loads:
                    sp.dma_start(dst, src).then_inc(weights_in.sem, 16)
            load_residuals(0)
            with sp.Fori(0, B - 1) as b:
                sp.wait_ge(hn_ready.sem, hn_ready.at(b, 1))
                load(b + 1)
                sp.wait_ge(y_ready.sem, y_ready.at(b, 1))
                sp.dma_start(out_v[b], out_sb[:, :, :]).then_inc(stored.sem, 16)
                sp.wait_ge(stored.sem, stored.at(b, 16))
                load_residuals(b + 1)
            sp.wait_ge(y_ready.sem, B)
            sp.dma_start(out_v[B - 1], out_sb[:, :, :]).then_inc(stored.sem, 16)
            sp.wait_ge(stored.sem, 16 * B)

        @block.gpsimd
        def _(pool):
            nc.gpsimd.memset(shifted[0:1, 0, D // 2:D], 0.0)
            nc.gpsimd.memset(neg_half[:, :], -0.5).then_inc(made_pool.sem, 1)
            pool.wait_ge(made_pool.sem, 1)
            with pool.Fori(0, B) as b:
                for k in range(1 + LAST):
                    roots.step(pool, b, k, rstd[:, :], mv[:, :, 1], EPS, neg_half[:, :])

        @block.tensor
        def _(pe):
            pe.wait_ge(weights_in.sem, 16 * len(loads))
            with pe.Fori(0, B) as b:
                pe.wait_ge(hn_ready.sem, hn_ready.at(b, 1))
                for k in range(KD):
                    for t in range(NT):
                        last = nc.tensor.transpose(ps_t[k][:, t * P:(t + 1) * P], hn[:, t, k * P:(k + 1) * P],
                                                   ident[:, :])
                    last.then_inc(hT_psum.sem, 1)
                pe.wait_ge(hT_ready.sem, hT_ready.at(b, KD))
                for c in range(CK):
                    m = part(c)
                    if c >= 2:
                        pe.wait_ge(gated_ready.sem, gated_ready.at(b, c - 1))
                    for ps, lo, done in ((ps_g, HID, g_psum), (ps_a, 0, a_psum)):
                        for k in range(KD):
                            last = nc.tensor.matmul(ps[c % 2][0:m, :], w1[:, k, lo + c * P:lo + c * P + m], hT[:, k, :],
                                                    start=k == 0, stop=k == KD - 1)
                        last.then_inc(done.sem, 1)
                pe.wait_ge(gated_ready.sem, gated_ready.at(b, CK))
                for t in range(NT):
                    for c in range(CK):
                        m = part(c)
                        last = nc.tensor.matmul(ps_y[:, t, :], gated[0:m, c, t * P:(t + 1) * P], w2[0:m, c, :],
                                                start=c == 0, stop=c == CK - 1)
                last.then_inc(y_psum.sem, 1)

        @block.scalar
        def _(act):
            act.wait_ge(weights_in.sem, 16 * len(loads))
            with act.Fori(0, B) as b:
                for k in range(KD):
                    act.wait_ge(hT_psum.sem, hT_psum.at(b, k + 1))
                    nc.scalar.activation(hT[:, k, :], ps_t[k][:, :], ACT.Identity, bias=ln[:, 1, k:k + 1],
                                         scale=ln[:, 0, k:k + 1]).then_inc(hT_ready.sem, 1)
                for c in range(CK):
                    m = part(c)
                    act.wait_ge(g_psum.sem, g_psum.at(b, c + 1))
                    if c >= 2:
                        act.wait_ge(gated_ready.sem, gated_ready.at(b, c - 1))
                    nc.scalar.activation(gelu[0:m, c % 2, :], ps_g[c % 2][0:m, :], ACT.Gelu, bias=b1[0:m, 1, c:c + 1])\
                      .then_inc(gelu_ready.sem, 1)

        @block.vector
        def _(dve):
            dve.wait_ge(weights_in.sem, 16 * len(loads))
            dve.wait_ge(made_pool.sem, 1)

            def norm(b, link, n, src, dst):
                row_stats(nc, link, [src[:, t, :] for t in range(NT)], stats, mv, roots.passed_dve.sem)\
                    .then_inc(roots.given.sem, 1)
                roots.wait(dve, b, n)
                for t in range(NT):
                    last = normalise(nc, dst[:, t, :], src[:, t, :], mv, rstd, t)
                return last

            with dve.Fori(0, B) as b:
                link = Order(dve, dve_order, b)
                dve.wait_ge(loaded.sem, loaded.at(b, 3 * 16))
                norm(b, link, 0, shifted, hn).then_inc(hn_ready.sem, 1)
                for c in range(CK):
                    m = part(c)
                    dve.wait_ge(gelu_ready.sem, gelu_ready.at(b, c + 1))
                    dve.wait_ge(a_psum.sem, a_psum.at(b, c + 1))
                    nc.vector.scalar_tensor_tensor(gated[0:m, c, :], ps_a[c % 2][0:m, :], b1[0:m, 0, c:c + 1],
                                                   gelu[0:m, c % 2, :], ALU.add, ALU.mult).then_inc(gated_ready.sem, 1)
                dve.wait_ge(res_loaded.sem, res_loaded.at(b, (1 + LAST) * 16))
                link(nc.vector.tensor_tensor(y_res[:, :, :], y_res[:, :, :],
                                             b2[:, :].unsqueeze(1).to_broadcast([P, NT, D]), ALU.add))
                dve.wait_ge(y_psum.sem, y_psum.at(b, 1))
                y_new = yn if LAST else out_sb
                add = nc.vector.tensor_tensor(y_new[:, :, :], y_res[:, :, :], ps_y[:, :, :], ALU.add)
                if LAST:
                    link(add)
                    link(norm(b, link, 1, yn, out_sb))
                    add = nc.vector.tensor_tensor(out_sb[:, :, :], out_sb[:, :, :], x_res[:, :, :], ALU.add)
                add.then_inc(y_ready.sem, 1)
                link.close()


def diffusion_attention(nc, x_dram, out_dram, w, con):
    H, DH = 16, 16
    CH, CDH = 8, 32
    ROWS = 32
    USED = DH + 2
    K_ALL = 4 * USED
    LAG = 22
    G = H * ROWS // P
    HG = H // G
    GS = HG * NT
    STEPS = H * NT
    C = float(DH) ** -0.5
    CC = float(N) ** -0.5

    with stage(nc) as ctx:
        def sb(name, shape, dt=fp32):
            return ctx.enter_context(nc.sbuf_tensor("c_" + name, shape, dt))

        def signal(name, per_batch=1):
            return Signal(ctx, nc, "c_" + name, per_batch)

        x_in = sb("x_in", [P, NT, D])
        x_res = sb("x_res", [P, NT, D])
        h = sb("h", [P, NT, D])
        hn = sb("hn", [P, NT, D])
        hT = sb("hT", [P, KD, N])
        qsq = sb("qsq", [P, 2, N])
        qT, kT = sb("qT", [P, 2, N]), sb("kT", [P, 2, N])
        q_half, k_half = sb("q_half", [P, 2, G, N], fp32r), sb("k_half", [P, 2, G, N], fp32r)
        q_all, k_all = sb("q_all", [P, H, N], fp32r), sb("k_all", [P, H, N], fp32r)
        v = sb("v", [P, NT, H, ROWS])
        probsT = sb("probsT", [P, 3, N])
        sumsT = sb("sumsT", [P, 2, N])
        o = sb("o", [P, NT, D])
        oT = sb("oT", [P, KD, N])
        y = sb("y", [P, NT, D])
        qc = sb("qc", [P, NT, D])
        vcT = sb("vcT", [P, KD, N])
        wqk = sb("wqk", [P, KD, H, ROWS])
        wv, wo = sb("wv", [P, KD, D]), sb("wo", [P, KD, D])
        wqc, wvc, woc = sb("wqc", [P, KD, D]), sb("wvc", [P, KD, D]), sb("woc", [P, KD, D])
        ln = sb("ln", [P, 4, KD])
        gamma = sb("gamma", [P, 2, D])
        tau = sb("tau", [P, G])
        tau_c = sb("tau_c", [P, KD])
        q_scale, q_bias = sb("q_scale", [P, G]), sb("q_bias", [P, G])
        rows = sb("rows", [P, 4])
        ident, ones = sb("ident", [P, P]), sb("ones", [P, P])
        neg_sum = sb("neg_sum", [P, P])
        block_mask = sb("block_mask", [P, P])
        stats, mv, rstd = sb("stats", [P, NT, 6]), sb("mv", [P, NT, 2]), sb("rstd", [P, NT])
        neg_max = sb("neg_max", [P, 2, HG * NT])
        max_half = sb("max_half", [HG * NT, 2, 2, P], fp32r)
        inv = sb("inv", [P, 2, NT, HG])
        gdiag, gsum = sb("gdiag", [P, KD, P]), sb("gsum", [P, KD])
        logits, cattn = sb("logits", [P, KD, P]), sb("cattn", [P, KD, P])
        cmax, csum, cinv = sb("cmax", [P, KD]), sb("csum", [P, KD]), sb("cinv", [P, KD])
        mix = sb("mix", [P, KD, D])
        neg_half = sb("neg_half", [P, NT])

        bank = [ctx.enter_context(nc.psum_tensor(f"c_bank{i}", [P, N], fp32)) for i in range(4)]
        ps_t = [ctx.enter_context(nc.psum_tensor(f"c_ps_t{i}", [P, N], fp32)) for i in range(2)]
        ps_o = [ctx.enter_context(nc.psum_tensor(f"c_ps_o{i}", [P, N], fp32)) for i in range(2)]
        ps_y = [ps[:, :].rearrange("p (t d) -> p t d", t=2) for ps in ps_o]

        ps_first, ps_again, ps_misc = bank[0:2], [bank[2], bank[3], ps_t[0]], ps_t[1]

        weights_in, made, made_pool = signal("weights_in"), signal("made"), signal("made_pool")
        zeroed = signal("zeroed")
        x_loaded, res_loaded, stored = signal("x_loaded", 16), signal("res_loaded", 16), signal("stored", 16)
        x_free, y_ready = signal("x_free"), signal("y_ready")
        hn_ready = signal("hn_ready", 2)
        hT_psum, hT_ready = signal("hT_psum", 2 * KD), signal("hT_ready", 2 * KD)
        q_psum, qsq_ready, norms_psum = signal("q_psum", G), signal("qsq_ready", G), signal("norms_psum", G)
        q_ready, k_ready = signal("q_ready", G), signal("k_ready", G)
        q_halves, k_halves = signal("q_halves", G), signal("k_halves", G)
        q_order = signal("q_order", G)
        packed = [signal(f"packed{j}", 16 * 8 * HG) for j in range(G)]
        v_psum, v_ready = signal("v_psum", NT), signal("v_ready", NT)
        scores_ready, max_ready = signal("scores_ready", STEPS), signal("max_ready", STEPS)
        max_psum, max_high, max_halves = signal("max_psum", G), signal("max_high", G), signal("max_halves", G)
        max_packed = signal("max_packed", 2 * 16 * G)
        scoresT_ready, probs_ready, pv_done = (signal("scoresT_ready", STEPS), signal("probs_ready", STEPS),
                                               signal("pv_done", STEPS))
        sumsT_ready, sums_psum = signal("sumsT_ready", G), signal("sums_psum", G)
        o_ready, oT_psum, oT_ready = signal("o_ready", G), signal("oT_psum", KD), signal("oT_ready", KD)
        yt_psum = signal("yt_psum", 2)
        qc_psum, qc_ready = signal("qc_psum", NT), signal("qc_ready", NT)
        vc_psum, vc_ready = signal("vc_psum", KD), signal("vc_ready", KD)
        gram_psum, gdiag_ready, gnorm_psum = signal("gram_psum"), signal("gdiag_ready"), signal("gnorm_psum")
        cmax_ready, cexp_ready, cattn_ready = signal("cmax_ready"), signal("cexp_ready"), signal("cattn_ready")
        mix_psum, mix_ready, yc_psum = signal("mix_psum"), signal("mix_ready"), signal("yc_psum", 2)
        roots = InverseRoots(ctx, nc, "c_roots", 4)
        dve_order = signal("dve_order", 14 + 2 * G)
        loads = []

        x_v = x_dram.rearrange("b (t p) d -> b p t d", p=P)
        out_v = out_dram.rearrange("b (t p) d -> b p t d", p=P)
        steps = [(hd, i) for hd in range(H) for i in range(NT)]

        block = ctx.enter_context(nc.Block())

        @block.sync
        def _(sp):
            sp.dma_start(x_in[:, :, :], x_v[0]).then_inc(x_loaded.sem, 16)
            for dst, src in ((wv, w["Wv_t"]), (wo, w["Wo_t"]), (wqc, w["Wqk_c"]), (wvc, w["Wv_c"]), (woc, w["Wo_c"])):
                loads.append((dst[:, :, :], src.rearrange("(k p) n -> p k n", p=P)))
            for n, name in enumerate(("ln1_w", "ln1_b", "ln2_w", "ln2_b")):
                loads.append((ln[:, n, :], column(w[name])))
            for n in (1, 2):
                loads.append((gamma[:, n - 1, :], w[f"gamma{n}"].partition_broadcast(P)))
            for dst, src in ((tau, w["tau_t"]), (tau_c, w["tau_c"])):
                per_group = src.rearrange("(j r) a c -> r (j a c)", r=HG)
                for r in range(HG):
                    loads.append((dst[32 * r:32 * r + 32, :], per_group[r].partition_broadcast(32)))
            for dst, name in ((ident, "ident"), (neg_sum, "neg_sum"), (block_mask, "block_mask"), (rows, "rows")):
                loads.append((dst[:, :], con[name]))
            with nc.allow_non_contiguous_dma(reason="a few small vectors, once"):
                for dst, src in loads:
                    sp.dma_start(dst, src).then_inc(weights_in.sem, 16)
            sp.wait_ge(zeroed.sem, 1)
            for k in range(KD):
                sp.dma_start(wqk[:, k, :, 0:DH], w["Wqk_t"].rearrange("(k p) (h d) -> k p h d", p=P, d=DH)[k])\
                  .then_inc(weights_in.sem, 16)
            sp.dma_start(x_res[:, :, :], x_v[0]).then_inc(res_loaded.sem, 16)

            def pack(b):
                for j in range(G):
                    sp.wait_ge(q_halves.sem, q_halves.at(b, j + 1))
                    sp.wait_ge(k_halves.sem, k_halves.at(b, j + 1))
                    for r in range(HG):
                        for n in range(4):
                            for dst, src, half in ((q_all, q_half, n // 2), (k_all, k_half, n % 2)):
                                sp.dma_start(dst[n * USED:(n + 1) * USED, HG * j + r, :].bitcast(fp32),
                                             src[ROWS * r:ROWS * r + USED, half, j, :].bitcast(fp32)).then_inc(packed[j].sem, 16)

                for g in range(G):
                    sp.wait_ge(max_halves.sem, max_halves.at(b, g + 1))
                    for half in range(2):
                        sp.dma_start(q_all[K_ALL + half:K_ALL + half + 1, HG * g:HG * (g + 1), :].bitcast(fp32),
                                     max_half[:, g % 2, half, :].bitcast(fp32)).then_inc(max_packed.sem, 16)

            with sp.Fori(0, B - 1) as b:
                pack(b)
                sp.wait_ge(x_free.sem, x_free.at(b, 1))
                sp.dma_start(x_in[:, :, :], x_v[b + 1]).then_inc(x_loaded.sem, 16)
                sp.wait_ge(y_ready.sem, y_ready.at(b, 1))
                sp.dma_start(out_v[b], x_res[:, :, :]).then_inc(stored.sem, 16)
                sp.wait_ge(stored.sem, stored.at(b, 16))
                sp.dma_start(x_res[:, :, :], x_v[b + 1]).then_inc(res_loaded.sem, 16)
            pack(B - 1)
            sp.wait_ge(y_ready.sem, B)
            sp.dma_start(out_v[B - 1], x_res[:, :, :]).then_inc(stored.sem, 16)
            sp.wait_ge(stored.sem, 16 * B)

        N_LOADED = 5 + 4 + 2 + 2 * HG + 4 + KD

        @block.gpsimd
        def _(pool):
            nc.gpsimd.memset(wqk[:, :, :, :], 0.0).then_inc(zeroed.sem, 1)
            nc.gpsimd.memset(ones[:, :], 1.0)
            nc.gpsimd.memset(k_all[:, :, :].bitcast(fp32), 1.0)
            nc.gpsimd.memset(v[:, :, :, :], 0.0).then_inc(zeroed.sem, 1)
            pool.wait_ge(zeroed.sem, 2)
            nc.gpsimd.memset(v[:, :, :, DH:DH + 1], 1.0)
            nc.gpsimd.memset(neg_half[:, :], -0.5).then_inc(made_pool.sem, 1)
            pool.wait_ge(made_pool.sem, 1)
            with pool.Fori(0, B) as b:
                for k in range(4):
                    roots.step(pool, b, k, rstd[:, :], mv[:, :, 1], EPS, neg_half[:, :])
                    if k == 1:
                        for j in range(G):
                            pool.wait_ge(q_ready.sem, q_ready.at(b, j + 1))
                            pool.sem_inc(roots.passed.sem, 1)
                            nc.gpsimd.tensor_copy(q_half[:, 0, j, :], qT[:, j % 2, :]).then_inc(q_order.sem, 1)
                            pool.wait_ge(q_order.sem, q_order.at(b, j + 1))
                            nc.gpsimd.tensor_tensor(q_half[:, 1, j, :], qT[:, j % 2, :],
                                                    q_half[:, 0, j, :].bitcast(fp32), ALU.subtract)\
                                .then_inc(q_halves.sem, 1)

        @block.tensor
        def _(pe):
            pe.wait_ge(weights_in.sem, 16 * N_LOADED)
            pe.wait_ge(made_pool.sem, 1)

            def transpose_hn(b, n):
                pe.wait_ge(hn_ready.sem, hn_ready.at(b, n + 1))
                for k in range(KD):
                    for t in range(NT):
                        last = nc.tensor.transpose(ps_t[k][:, t * P:(t + 1) * P], hn[:, t, k * P:(k + 1) * P],
                                                   ident[:, :])
                    last.then_inc(hT_psum.sem, 1)
                pe.wait_ge(hT_ready.sem, hT_ready.at(b, KD * (n + 1)))

            with pe.Fori(0, B) as b:
                transpose_hn(b, 0)
                for j in range(G):
                    for k in range(KD):
                        last = nc.tensor.matmul(bank[j][:, :], wqk[:, k, HG * j:HG * (j + 1), :], hT[:, k, :],
                                                start=k == 0, stop=k == KD - 1)
                    last.then_inc(q_psum.sem, 1)
                for j in range(G):
                    pe.wait_ge(qsq_ready.sem, qsq_ready.at(b, j + 1))
                    if j >= 2:
                        pe.wait_ge(k_ready.sem, k_ready.at(b, j - 1))
                    for k in range(KD):
                        nc.tensor.matmul(ps_t[j % 2][:, :], wqk[:, k, HG * j:HG * (j + 1), :], hT[:, k, :],
                                         start=k == 0, stop=False)
                    nc.tensor.matmul(ps_t[j % 2][:, :], neg_sum[:, :], qsq[:, j % 2, :], start=False, stop=True)\
                      .then_inc(norms_psum.sem, 1)
                for t in range(NT):
                    for k in range(KD):
                        last = nc.tensor.matmul(bank[t][:, 0:D], hT[:, k, t * P:(t + 1) * P], wv[:, k, :],
                                                start=k == 0, stop=k == KD - 1)
                    last.then_inc(v_psum.sem, 1)
                pe.wait_ge(v_ready.sem, v_ready.at(b, NT))
                pe.wait_ge(k_ready.sem, k_ready.at(b, G))
                for s in range(STEPS + LAG + 5):
                    if s < STEPS:
                        hd, i = steps[s]
                        if hd % HG == 0 and i == 0:
                            group = packed[hd // HG]
                            pe.wait_ge(group.sem, group.at(b, group.per_batch))
                        if s >= 2:
                            pe.wait_ge(max_ready.sem, max_ready.at(b, s - 1))
                        nc.tensor.matmul(ps_first[s % 2][:, :], q_all[0:K_ALL, hd, i * P:(i + 1) * P],
                                         k_all[0:K_ALL, hd, :], start=True, stop=True).then_inc(scores_ready.sem, 1)
                    if s >= 1 and s <= STEPS and s % GS == 0:
                        g = s // GS - 1
                        pe.wait_ge(max_ready.sem, max_ready.at(b, s))
                        nc.tensor.matmul(ps_misc[0:HG * NT, 0:P], neg_max[:, g % 2, :], ident[:, :],
                                         start=True, stop=True).then_inc(max_psum.sem, 1)
                    u = s - LAG
                    if 0 <= u < STEPS:
                        hd, c = steps[u]
                        if u % GS == 0:
                            pe.wait_ge(max_packed.sem, max_packed.at(b, 32 * (u // GS + 1)))
                        if u >= 3:
                            pe.wait_ge(probs_ready.sem, probs_ready.at(b, u - 2))
                        nc.tensor.matmul(ps_again[u % 3][:, :], k_all[0:K_ALL + 2, hd, c * P:(c + 1) * P],
                                         q_all[0:K_ALL + 2, hd, :], start=True, stop=True)\
                            .then_inc(scoresT_ready.sem, 1)
                    u = s - LAG - 2
                    if 0 <= u < STEPS:
                        hd, c = steps[u]
                        g, r = hd // HG, ROWS * (hd % HG)
                        pe.wait_ge(probs_ready.sem, probs_ready.at(b, u + 1))
                        if u % GS == 0 and g >= 2:
                            pe.wait_ge(sumsT_ready.sem, sumsT_ready.at(b, g - 1))
                        nc.tensor.matmul(ps_o[g % 2][r:r + ROWS, :], v[:, c, hd, :], probsT[:, u % 3, :],
                                         start=c == 0, stop=c == NT - 1).then_inc(pv_done.sem, 1)
                    u = s - LAG - 5
                    if 0 <= u and u % GS == GS - 1:
                        g = u // GS
                        pe.wait_ge(sumsT_ready.sem, sumsT_ready.at(b, g + 1))
                        if g >= 1:
                            pe.wait_ge(o_ready.sem, o_ready.at(b, g))
                        pe.wait_ge(max_halves.sem, max_halves.at(b, min(g + 2, G)))
                        for t in range(NT):
                            last = nc.tensor.transpose(ps_misc[:, t * P:(t + 1) * P],
                                                       sumsT[:, g % 2, t * P:(t + 1) * P], ident[:, :])
                        last.then_inc(sums_psum.sem, 1)
                pe.wait_ge(o_ready.sem, o_ready.at(b, G))
                for k in range(KD):
                    for t in range(NT):
                        last = nc.tensor.transpose(ps_t[k][:, t * P:(t + 1) * P], o[:, t, k * P:(k + 1) * P],
                                                   ident[:, :])
                    last.then_inc(oT_psum.sem, 1)
                pe.wait_ge(oT_ready.sem, oT_ready.at(b, KD))
                for t in range(NT):
                    for k in range(KD):
                        last = nc.tensor.matmul(ps_y[t // 2][:, t % 2, :], oT[:, k, t * P:(t + 1) * P], wo[:, k, :],
                                                start=k == 0, stop=k == KD - 1)
                    if t % 2:
                        last.then_inc(yt_psum.sem, 1)
                transpose_hn(b, 1)
                for t in range(NT):
                    for k in range(KD):
                        last = nc.tensor.matmul(bank[t][:, 0:D], hT[:, k, t * P:(t + 1) * P], wqc[:, k, :],
                                                start=k == 0, stop=k == KD - 1)
                    last.then_inc(qc_psum.sem, 1)
                for c in range(KD):
                    for k in range(KD):
                        last = nc.tensor.matmul(ps_t[c][:, :], wvc[:, k, c * P:(c + 1) * P], hT[:, k, :],
                                                start=k == 0, stop=k == KD - 1)
                    last.then_inc(vc_psum.sem, 1)
                pe.wait_ge(qc_ready.sem, qc_ready.at(b, NT))
                for c in range(KD):
                    for t in range(NT):
                        last = nc.tensor.matmul(bank[0][:, c * P:(c + 1) * P], qc[:, t, c * P:(c + 1) * P],
                                                qc[:, t, c * P:(c + 1) * P], start=t == 0, stop=t == NT - 1)
                last.then_inc(gram_psum.sem, 1)
                pe.wait_ge(gdiag_ready.sem, gdiag_ready.at(b, 1))
                nc.tensor.matmul(bank[1][:, 0:KD * P], ones[:, :], gdiag[:, :, :], start=True, stop=True)\
                  .then_inc(gnorm_psum.sem, 1)
                pe.wait_ge(cattn_ready.sem, cattn_ready.at(b, 1))
                for c in range(KD):
                    last = nc.tensor.matmul(bank[2][:, c * D:(c + 1) * D], cattn[:, c, :], woc[:, c, :],
                                            start=True, stop=True)
                last.then_inc(mix_psum.sem, 1)
                pe.wait_ge(mix_ready.sem, mix_ready.at(b, 1))
                pe.wait_ge(vc_ready.sem, vc_ready.at(b, KD))
                for t in range(NT):
                    for k in range(KD):
                        last = nc.tensor.matmul(ps_y[t // 2][:, t % 2, :], vcT[:, k, t * P:(t + 1) * P], mix[:, k, :],
                                                start=k == 0, stop=k == KD - 1)
                    if t % 2:
                        last.then_inc(yc_psum.sem, 1)

        @block.scalar
        def _(act):
            act.wait_ge(weights_in.sem, 16 * N_LOADED)
            act.wait_ge(made.sem, 3)

            def evacuate_hT(b, n):
                for k in range(KD):
                    act.wait_ge(hT_psum.sem, hT_psum.at(b, KD * n + k + 1))
                    nc.scalar.activation(hT[:, k, :], ps_t[k][:, :], ACT.Identity, bias=ln[:, 2 * n + 1, k:k + 1],
                                         scale=ln[:, 2 * n, k:k + 1]).then_inc(hT_ready.sem, 1)

            with act.Fori(0, B) as b:
                evacuate_hT(b, 0)
                for j in range(G):
                    act.wait_ge(q_psum.sem, q_psum.at(b, j + 1))
                    if j >= 2:
                        act.wait_ge(norms_psum.sem, norms_psum.at(b, j - 1))
                    nc.scalar.activation(qsq[:, j % 2, :], bank[j][:, :], ACT.Square).then_inc(qsq_ready.sem, 1)
                    if j >= 1:
                        u = j - 1
                        act.wait_ge(norms_psum.sem, norms_psum.at(b, u + 1))
                        if u >= 2:
                            act.wait_ge(q_halves.sem, q_halves.at(b, u - 1))
                        nc.scalar.activation(qT[:, u % 2, :], ps_t[u % 2][:, :], ACT.Identity, bias=q_bias[:, u:u + 1],
                                             scale=q_scale[:, u:u + 1]).then_inc(q_ready.sem, 1)
                act.wait_ge(norms_psum.sem, norms_psum.at(b, G))
                act.wait_ge(q_halves.sem, q_halves.at(b, G - 2))
                nc.scalar.activation(qT[:, (G - 1) % 2, :], ps_t[(G - 1) % 2][:, :], ACT.Identity, bias=q_bias[:, G - 1:G],
                                     scale=q_scale[:, G - 1:G]).then_inc(q_ready.sem, 1)
                for t in range(NT):
                    act.wait_ge(v_psum.sem, v_psum.at(b, t + 1))
                    nc.scalar.copy(v[:, t, :, 0:DH], bank[t][:, 0:D].rearrange("p (h d) -> p h d", d=DH)).then_inc(v_ready.sem, 1)
                for s in range(STEPS + LAG + 5):
                    if s >= 1 and s <= STEPS and s % GS == 0:
                        g = s // GS - 1
                        act.wait_ge(max_psum.sem, max_psum.at(b, g + 1))
                        if g >= 2:
                            act.wait_ge(max_packed.sem, max_packed.at(b, 32 * (g - 1)))
                        nc.scalar.copy(max_half[:, g % 2, 0, :], ps_misc[0:HG * NT, 0:P]).then_inc(max_high.sem, 1)
                    u = s - LAG
                    if 0 <= u < STEPS:
                        act.wait_ge(scoresT_ready.sem, scoresT_ready.at(b, u + 1))
                        if u >= 3:
                            act.wait_ge(pv_done.sem, pv_done.at(b, u - 2))
                        nc.scalar.activation(probsT[:, u % 3, :], ps_again[u % 3][:, :], ACT.Exp)\
                            .then_inc(probs_ready.sem, 1)
                    u = s - LAG - 4
                    if 0 <= u and u % GS == GS - 1:
                        g = u // GS
                        act.wait_ge(pv_done.sem, pv_done.at(b, u + 1))
                        if g >= 2:
                            act.wait_ge(sums_psum.sem, sums_psum.at(b, g - 1))
                        nc.scalar.copy(sumsT[:, g % 2, :], ps_o[g % 2][:, :]).then_inc(sumsT_ready.sem, 1)
                for k in range(KD):
                    act.wait_ge(oT_psum.sem, oT_psum.at(b, k + 1))
                    nc.scalar.copy(oT[:, k, :], ps_t[k][:, :]).then_inc(oT_ready.sem, 1)
                evacuate_hT(b, 1)
                for t in range(NT):
                    act.wait_ge(qc_psum.sem, qc_psum.at(b, t + 1))
                    nc.scalar.copy(qc[:, t, :], bank[t][:, 0:D]).then_inc(qc_ready.sem, 1)
                for c in range(KD):
                    act.wait_ge(vc_psum.sem, vc_psum.at(b, c + 1))
                    nc.scalar.copy(vcT[:, c, :], ps_t[c][:, :]).then_inc(vc_ready.sem, 1)
                act.wait_ge(cmax_ready.sem, cmax_ready.at(b, 1))
                for c in range(KD):
                    last = nc.scalar.activation(cattn[:, c, :], logits[:, c, :], ACT.Exp, bias=cmax[:, c:c + 1],
                                                accum_out=csum[:, c:c + 1])
                last.then_inc(cexp_ready.sem, 1)

        @block.vector
        def _(dve):
            dve.wait_ge(weights_in.sem, 16 * N_LOADED)
            nc.vector.tensor_scalar(q_scale[:, :], tau[:, :], rows[:, 0:1], C, ALU.mult, ALU.mult)
            nc.vector.tensor_scalar(q_bias[:, :], tau[:, :], rows[:, 1:2], C, ALU.mult, ALU.mult)
            nc.vector.tensor_scalar(tau_c[:, :], tau_c[:, :], CC, None, ALU.mult).then_inc(made.sem, 3)
            dve.wait_ge(made.sem, 3)

            def norm(b, link, n, srcs, dst):
                row_stats(nc, link, srcs, stats, mv, roots.passed_dve.sem).then_inc(roots.given.sem, 1)
                roots.wait(dve, b, n)
                for t in range(NT):
                    last = normalise(nc, dst[:, t, :], srcs[t], mv, rstd, t)
                return last

            tiles = lambda buf: [buf[:, t, :] for t in range(NT)]
            with dve.Fori(0, B) as b:
                link = Order(dve, dve_order, b)
                dve.wait_ge(x_loaded.sem, x_loaded.at(b, 16))
                norm(b, link, 0, tiles(x_in), h).then_inc(x_free.sem, 1)
                dve.wait_ge(x_free.sem, x_free.at(b, 1))
                norm(b, link, 1, tiles(h), hn).then_inc(hn_ready.sem, 1)
                for j in range(G):
                    dve.wait_ge(q_ready.sem, q_ready.at(b, j + 1))
                    nc.vector.tensor_scalar(kT[:, j % 2, :], ps_t[j % 2][:, :], rows[:, 2:3], rows[:, 3:4], ALU.mult,
                                            ALU.add).then_inc(k_ready.sem, 1)
                    dve.wait_ge(k_ready.sem, k_ready.at(b, j + 1))
                    link(nc.vector.tensor_copy(k_half[:, 0, j, :], kT[:, j % 2, :]))
                    nc.vector.tensor_tensor(k_half[:, 1, j, :], kT[:, j % 2, :], k_half[:, 0, j, :].bitcast(fp32),
                                            ALU.subtract).then_inc(k_halves.sem, 1)
                for s in range(STEPS + LAG + 6):
                    if s < STEPS:
                        dve.wait_ge(scores_ready.sem, scores_ready.at(b, s + 1))
                        g = s // GS
                        if s % GS == 0 and g >= 2:
                            dve.wait_ge(max_psum.sem, max_psum.at(b, g - 1))
                        nc.vector.tensor_reduce(neg_max[:, g % 2, s % GS:s % GS + 1], ps_first[s % 2][:, :], AX.X,
                                                ALU.max, negate=True).then_inc(max_ready.sem, 1)
                    if s >= 2 and s - 2 <= STEPS and (s - 2) % GS == 0 and s > 2:
                        g = (s - 2) // GS - 1
                        dve.wait_ge(max_high.sem, max_high.at(b, g + 1))
                        nc.vector.tensor_tensor(max_half[:, g % 2, 1, :], ps_misc[0:HG * NT, 0:P],
                                                max_half[:, g % 2, 0, :].bitcast(fp32), ALU.subtract)\
                            .then_inc(max_halves.sem, 1)
                    u = s - LAG - 6
                    if 0 <= u and u % GS == GS - 1:
                        g = u // GS
                        dve.wait_ge(sums_psum.sem, sums_psum.at(b, g + 1))
                        heads = ps_misc[:, :].rearrange("p (t r d) -> p t r d", t=NT, d=ROWS)
                        link(nc.vector.reciprocal(inv[:, g % 2, :, :], heads[:, :, :, DH]))
                        o_group = o[:, :, g * HG * DH:(g + 1) * HG * DH].rearrange("p t (r d) -> p t r d", d=DH)
                        for t in range(NT):
                            last = nc.vector.tensor_tensor(o_group[:, t], heads[:, t, :, 0:DH],
                                                           inv[:, g % 2, t, :].unsqueeze(2).to_broadcast([P, HG, DH]),
                                                           ALU.mult)
                        last.then_inc(o_ready.sem, 1)

                def residual(psum, n):
                    for t in range(NT):
                        if t % 2 == 0:
                            dve.wait_ge(psum.sem, psum.at(b, t // 2 + 1))
                        last = nc.vector.tensor_tensor(y[:, t, :], ps_y[t // 2][:, t % 2, :], gamma[:, n, :], ALU.mult)
                    link(last)
                    link(nc.vector.tensor_tensor(h[:, :, :], h[:, :, :], y[:, :, :], ALU.add))

                residual(yt_psum, 0)
                norm(b, link, 2, tiles(h), hn).then_inc(hn_ready.sem, 1)
                dve.wait_ge(gram_psum.sem, gram_psum.at(b, 1))
                gram = bank[0][:, 0:KD * P].rearrange("p (k d) -> p k d", k=KD)
                gnorm = bank[1][:, 0:KD * P].rearrange("p (k d) -> p k d", k=KD)
                for c in range(KD):
                    last = nc.vector.scalar_tensor_tensor(gdiag[:, c, :], gram[:, c, :], -1.0, ident[:, :], ALU.mult,
                                                          ALU.mult)
                last.then_inc(gdiag_ready.sem, 1)
                dve.wait_ge(gdiag_ready.sem, gdiag_ready.at(b, 1))
                link(nc.vector.tensor_reduce(gsum[:, :], gdiag[:, :, :], AX.X, ALU.add))
                for c in range(KD):
                    last = nc.vector.tensor_scalar(logits[:, c, :], gram[:, c, :], 2.0, gsum[:, c:c + 1], ALU.mult,
                                                   ALU.add)
                link(last)
                dve.wait_ge(gnorm_psum.sem, gnorm_psum.at(b, 1))
                link(nc.vector.tensor_tensor(logits[:, :, :], logits[:, :, :], gnorm, ALU.add))
                for c in range(KD):
                    last = nc.vector.scalar_tensor_tensor(logits[:, c, :], logits[:, c, :], tau_c[:, c:c + 1],
                                                          block_mask[:, :], ALU.mult, ALU.add)
                link(last)
                nc.vector.tensor_reduce(cmax[:, :], logits[:, :, :], AX.X, ALU.max, negate=True)\
                  .then_inc(cmax_ready.sem, 1)
                dve.wait_ge(cexp_ready.sem, cexp_ready.at(b, 1))
                link(nc.vector.reciprocal(cinv[:, :], csum[:, :]))
                for c in range(KD):
                    last = nc.vector.tensor_scalar(cattn[:, c, :], cattn[:, c, :], cinv[:, c:c + 1], None, ALU.mult)
                last.then_inc(cattn_ready.sem, 1)
                dve.wait_ge(mix_psum.sem, mix_psum.at(b, 1))
                nc.vector.tensor_copy(mix[:, :, :].rearrange("p k d -> p (k d)"), bank[2][:, :])\
                  .then_inc(mix_ready.sem, 1)
                residual(yc_psum, 1)
                link(norm(b, link, 3, tiles(h), y))
                dve.wait_ge(res_loaded.sem, res_loaded.at(b, 16))
                nc.vector.tensor_tensor(x_res[:, :, :], x_res[:, :, :], y[:, :, :], ALU.add).then_inc(y_ready.sem, 1)
                link.close()


def expert_mixture(nc, x_dram, out_dram, w, con):
    E, H = 8, 512
    KH = H // P

    with stage(nc) as ctx:
        def sb(name, shape, dt=fp32):
            return ctx.enter_context(nc.sbuf_tensor("d_" + name, shape, dt))

        def signal(name, per_batch=1):
            return Signal(ctx, nc, "d_" + name, per_batch)

        x_in, x_res = sb("x_in", [P, NT, D]), sb("x_res", [P, NT, D])
        h = sb("h", [P, NT, D])
        acc = sb("acc", [P, NT, D])
        y = sb("y", [P, NT, D])
        hT = sb("hT", [P, KD, N])
        z = sb("z", [P, NT, H])
        zn = sb("zn", [P, NT, H])
        gT = sb("gT", [P, 2, KH, N])
        w1, w2 = sb("w1", [P, E, KD, H]), sb("w2", [P, E, KH, D])
        b1 = sb("b1", [P, E, H])
        b2 = sb("b2", [E, D])
        gate_w = sb("gate_w", [P, KD, E])
        gain, bias = sb("gain", [P, E, KH]), sb("bias", [P, E, KH])
        ln_g, ln_b = sb("ln_g", [P, D]), sb("ln_b", [P, D])
        ident, iota = sb("ident", [P, P]), sb("iota", [P, E])
        logits, best = sb("logits", [P, NT, E]), sb("best", [P, NT, 8])
        index = sb("index", [P, NT, 8], mybir.dt.uint32)
        index_f = sb("index_f", [P, NT, 2])
        pair = sb("pair", [P, NT, 2])
        second = sb("second", [P, NT, E])
        combine = sb("combine", [P, NT, P])
        combineT = sb("combineT", [P, N])
        stats, mv, rstd = sb("stats", [P, NT, 6]), sb("mv", [P, NT, 2]), sb("rstd", [P, NT])
        neg_half = sb("neg_half", [P, NT])

        ps_z = [ctx.enter_context(nc.psum_tensor(f"d_ps_z{i}", [P, H], fp32)) for i in range(2)]
        ps_t = [ctx.enter_context(nc.psum_tensor(f"d_ps_t{i}", [P, N], fp32)) for i in range(2)]
        ps_y = [[ctx.enter_context(nc.psum_tensor(f"d_ps_y{i}{j}", [P, 2, D], fp32)) for j in range(2)]
                for i in range(2)]

        weights_in, made_pool = signal("weights_in"), signal("made_pool")
        x_loaded, res_loaded, stored = signal("x_loaded", 16), signal("res_loaded", 16), signal("stored", 16)
        h_ready, y_ready = signal("h_ready"), signal("y_ready")
        hT_psum, hT_ready = signal("hT_psum", KD), signal("hT_ready", KD)
        gates_psum, pair_ready, exp_ready = signal("gates_psum"), signal("pair_ready"), signal("exp_ready")
        combine_ready, combineT_psum, combineT_ready = (signal("combine_ready"), signal("combineT_psum"),
                                                        signal("combineT_ready"))
        b2_psum = signal("b2_psum")
        z_psum, z_read = signal("z_psum", E * NT), signal("z_read", E * NT)
        zn_ready, znT_psum, g_ready = signal("zn_ready", E), signal("znT_psum", E * KH), signal("g_ready", E * KH)
        y_psum, y_read = signal("y_psum", E), signal("y_read", E + 1)
        roots = InverseRoots(ctx, nc, "d_roots", 3 + E)
        dve_order = signal("dve_order", 22)
        loads = []

        x_v = x_dram.rearrange("b (t p) d -> b p t d", p=P)
        out_v = out_dram.rearrange("b (t p) d -> b p t d", p=P)

        block = ctx.enter_context(nc.Block())

        @block.sync
        def _(sp):
            sp.dma_start(x_in[:, :, :], x_v[0]).then_inc(x_loaded.sem, 16)
            loads.append((gate_w[:, :, :], w["gate_w"].rearrange("(k p) e -> p k e", p=P)))
            loads.append((ident[:, :], con["ident"]))
            loads.append((iota[:, :], con["iota"]))
            loads.append((b2[:, :], w["b2"]))
            for dst, name in ((ln_g, "ln_g"), (ln_b, "ln_b")):
                loads.append((dst[:, :], w[name].partition_broadcast(P)))
            loads.append((b1[:, :, :].rearrange("p e h -> p (e h)"),
                          w["b1"].rearrange("e h -> (e h)").partition_broadcast(P)))
            for e in range(E):
                for dst, name in ((gain, "ln1_g"), (bias, "ln1_b")):
                    loads.append((dst[:, e, :], column(w[name][e])))
                loads.append((w1[:, e, :, :], w["w1"][e].rearrange("(k p) h -> p k h", p=P)))
                loads.append((w2[:, e, :, :], w["w2"][e].rearrange("(k p) h -> p k h", p=P)))
            with nc.allow_non_contiguous_dma(reason="a few small vectors, once"):
                for dst, src in loads:
                    sp.dma_start(dst, src).then_inc(weights_in.sem, 16)
            sp.dma_start(x_res[:, :, :], x_v[0]).then_inc(res_loaded.sem, 16)
            with sp.Fori(0, B - 1) as b:
                sp.wait_ge(h_ready.sem, h_ready.at(b, 1))
                sp.dma_start(x_in[:, :, :], x_v[b + 1]).then_inc(x_loaded.sem, 16)
                sp.wait_ge(y_ready.sem, y_ready.at(b, 1))
                sp.dma_start(out_v[b], x_res[:, :, :]).then_inc(stored.sem, 16)
                sp.wait_ge(stored.sem, stored.at(b, 16))
                sp.dma_start(x_res[:, :, :], x_v[b + 1]).then_inc(res_loaded.sem, 16)
            sp.wait_ge(y_ready.sem, B)
            sp.dma_start(out_v[B - 1], x_res[:, :, :]).then_inc(stored.sem, 16)
            sp.wait_ge(stored.sem, 16 * B)

        @block.gpsimd
        def _(pool):
            nc.gpsimd.memset(combine[:, :, :], 0.0)
            nc.gpsimd.memset(neg_half[:, :], -0.5).then_inc(made_pool.sem, 1)
            pool.wait_ge(made_pool.sem, 1)
            with pool.Fori(0, B) as b:
                for k in range(3 + E):
                    roots.step(pool, b, k, rstd[:, :], mv[:, :, 1], EPS, neg_half[:, :])

        @block.tensor
        def _(pe):
            pe.wait_ge(weights_in.sem, 16 * len(loads))
            with pe.Fori(0, B) as b:
                pe.wait_ge(h_ready.sem, h_ready.at(b, 1))
                for k in range(KD):
                    for t in range(NT):
                        last = nc.tensor.transpose(ps_t[k][:, t * P:(t + 1) * P], h[:, t, k * P:(k + 1) * P],
                                                   ident[:, :])
                    last.then_inc(hT_psum.sem, 1)
                pe.wait_ge(hT_ready.sem, hT_ready.at(b, KD))
                for t in range(NT):
                    for k in range(KD):
                        last = nc.tensor.matmul(ps_t[0][:, t * E:(t + 1) * E], hT[:, k, t * P:(t + 1) * P],
                                                gate_w[:, k, :], start=k == 0, stop=k == KD - 1)
                last.then_inc(gates_psum.sem, 1)

                def hidden(e):
                    for t in range(NT):
                        n = e * NT + t
                        if n >= 2:
                            pe.wait_ge(z_read.sem, z_read.at(b, n - 1))
                        for k in range(KD):
                            last = nc.tensor.matmul(ps_z[n % 2][:, :], hT[:, k, t * P:(t + 1) * P], w1[:, e, k, :],
                                                    start=k == 0, stop=k == KD - 1)
                        last.then_inc(z_psum.sem, 1)

                def output(e):
                    pe.wait_ge(zn_ready.sem, zn_ready.at(b, e + 1))
                    for c in range(KH):
                        n = e * KH + c
                        if n >= 2:
                            pe.wait_ge(g_ready.sem, g_ready.at(b, n - 1))
                        for t in range(NT):
                            last = nc.tensor.transpose(ps_t[n % 2][:, t * P:(t + 1) * P], zn[:, t, c * P:(c + 1) * P],
                                                       ident[:, :])
                        last.then_inc(znT_psum.sem, 1)
                    pe.wait_ge(g_ready.sem, g_ready.at(b, (e + 1) * KH))
                    pe.wait_ge(y_read.sem, y_read.at(b, max(e, 1)))
                    for t in range(NT):
                        for c in range(KH):
                            last = nc.tensor.matmul(ps_y[e % 2][t // 2][:, t % 2, :], gT[:, e % 2, c, t * P:(t + 1) * P],
                                                    w2[:, e, c, :], start=c == 0, stop=c == KH - 1)
                    last.then_inc(y_psum.sem, 1)

                hidden(0)
                pe.wait_ge(combine_ready.sem, combine_ready.at(b, 1))
                for t in range(NT):
                    last = nc.tensor.transpose(ps_t[1][:, t * P:(t + 1) * P], combine[:, t, :], ident[:, :])
                last.then_inc(combineT_psum.sem, 1)
                pe.wait_ge(combineT_ready.sem, combineT_ready.at(b, 1))
                for t in range(NT):
                    last = nc.tensor.matmul(ps_y[0][t // 2][:, t % 2, :], combineT[0:E, t * P:(t + 1) * P], b2[:, :],
                                            start=True, stop=True)
                last.then_inc(b2_psum.sem, 1)
                for e in range(1, E + 1):
                    if e < E:
                        hidden(e)
                    output(e - 1)

        @block.scalar
        def _(act):
            act.wait_ge(weights_in.sem, 16 * len(loads))
            with act.Fori(0, B) as b:
                for k in range(KD):
                    act.wait_ge(hT_psum.sem, hT_psum.at(b, k + 1))
                    nc.scalar.copy(hT[:, k, :], ps_t[k][:, :]).then_inc(hT_ready.sem, 1)
                act.wait_ge(pair_ready.sem, pair_ready.at(b, 1))
                nc.scalar.activation(pair[:, :, 1:2], pair[:, :, 1:2], ACT.Exp).then_inc(exp_ready.sem, 1)
                act.wait_ge(combineT_psum.sem, combineT_psum.at(b, 1))
                nc.scalar.copy(combineT[:, :], ps_t[1][:, :]).then_inc(combineT_ready.sem, 1)
                for e in range(E):
                    for c in range(KH):
                        n = e * KH + c
                        act.wait_ge(znT_psum.sem, znT_psum.at(b, n + 1))
                        if e >= 2 and c == 0:
                            act.wait_ge(y_psum.sem, y_psum.at(b, e - 1))
                        nc.scalar.activation(gT[:, e % 2, c, :], ps_t[n % 2][:, :], ACT.Gelu,
                                             bias=bias[:, e, c:c + 1], scale=gain[:, e, c:c + 1])\
                          .then_inc(g_ready.sem, 1)

        @block.vector
        def _(dve):
            dve.wait_ge(weights_in.sem, 16 * len(loads))
            dve.wait_ge(made_pool.sem, 1)

            def norm(b, link, n, srcs, dst):
                row_stats(nc, link, srcs, stats, mv, roots.passed_dve.sem).then_inc(roots.given.sem, 1)
                roots.wait(dve, b, n)
                for t in range(NT):
                    last = normalise(nc, dst[:, t, :], srcs[t], mv, rstd, t)
                return last

            tiles = lambda buf: [buf[:, t, :] for t in range(NT)]
            with dve.Fori(0, B) as b:
                link = Order(dve, dve_order, b)
                dve.wait_ge(x_loaded.sem, x_loaded.at(b, 16))
                norm(b, link, 0, tiles(x_in), h).then_inc(h_ready.sem, 1)
                dve.wait_ge(gates_psum.sem, gates_psum.at(b, 1))
                link(nc.vector.tensor_copy(logits[:, :, :].rearrange("p t e -> p (t e)"), ps_t[0][:, 0:NT * E]),
                     standing=roots.passed_dve.sem)
                for t in range(NT):
                    last = nc.vector.max(best[:, t, :], logits[:, t, :])
                link(last, standing=roots.passed_dve.sem)
                for t in range(NT):
                    last = nc.vector.max_index(index[:, t, :], best[:, t, :], logits[:, t, :])
                link(last)
                nc.vector.tensor_copy(index_f[:, :, :], index[:, :, 0:2])
                nc.vector.tensor_tensor(pair[:, :, 1:2], best[:, :, 1:2], best[:, :, 0:1], ALU.subtract)\
                  .then_inc(pair_ready.sem, 1)
                dve.wait_ge(exp_ready.sem, exp_ready.at(b, 1))
                link(nc.vector.tensor_scalar(pair[:, :, 0:1], pair[:, :, 1:2], 1.0, None, ALU.add))
                link(nc.vector.reciprocal(pair[:, :, 0:1], pair[:, :, 0:1]))
                link(nc.vector.tensor_tensor(pair[:, :, 1:2], pair[:, :, 1:2], pair[:, :, 0:1], ALU.mult))
                for n, dst in ((0, combine), (1, second)):
                    for t in range(NT):
                        last = nc.vector.tensor_scalar(dst[:, t, 0:E], iota[:, :], index_f[:, t, n:n + 1],
                                                       pair[:, t, n:n + 1], ALU.is_equal, ALU.mult)
                link(last)
                nc.vector.tensor_tensor(combine[:, :, 0:E], combine[:, :, 0:E], second[:, :, :], ALU.add)\
                  .then_inc(combine_ready.sem, 1)

                def accumulate(e):
                    dve.wait_ge(y_psum.sem, y_psum.at(b, e + 1))
                    dve.wait_ge(y_read.sem, y_read.at(b, e + 1))
                    for t in range(NT):
                        last = nc.vector.scalar_tensor_tensor(acc[:, t, :], ps_y[e % 2][t // 2][:, t % 2, :],
                                                              combine[:, t, e:e + 1], acc[:, t, :], ALU.mult, ALU.add)
                    last.then_inc(y_read.sem, 1)

                for e in range(E):
                    for t in range(NT):
                        n = e * NT + t
                        dve.wait_ge(z_psum.sem, z_psum.at(b, n + 1))
                        nc.vector.tensor_tensor(z[:, t, :], ps_z[n % 2][:, :], b1[:, e, :], ALU.add)\
                          .then_inc(z_read.sem, 1)
                    dve.wait_ge(z_read.sem, z_read.at(b, (e + 1) * NT))
                    row_stats(nc, link, tiles(z), stats, mv, roots.passed_dve.sem).then_inc(roots.given.sem, 1)
                    if e == 0:
                        dve.wait_ge(b2_psum.sem, b2_psum.at(b, 1))
                        for n in range(2):
                            last = nc.vector.tensor_tensor(acc[:, 2 * n:2 * n + 2, :], h[:, 2 * n:2 * n + 2, :],
                                                           ps_y[0][n][:, :, :], ALU.add)
                        last.then_inc(y_read.sem, 1)
                    if e >= 2:
                        accumulate(e - 2)
                    roots.wait(dve, b, 1 + e)
                    if e >= 1:
                        dve.wait_ge(znT_psum.sem, znT_psum.at(b, e * KH))
                    for t in range(NT):
                        last = normalise(nc, zn[:, t, :], z[:, t, :], mv, rstd, t)
                    last.then_inc(zn_ready.sem, 1)
                    dve.wait_ge(zn_ready.sem, zn_ready.at(b, e + 1))
                accumulate(E - 2)
                accumulate(E - 1)
                dve.wait_ge(y_read.sem, y_read.at(b, E + 1))
                link(norm(b, link, 1 + E, tiles(acc), y))
                link(nc.vector.tensor_tensor(y[:, :, :], y[:, :, :],
                                             ln_g[:, :].unsqueeze(1).to_broadcast([P, NT, D]), ALU.mult))
                link(nc.vector.tensor_tensor(acc[:, :, :], y[:, :, :],
                                             ln_b[:, :].unsqueeze(1).to_broadcast([P, NT, D]), ALU.add))
                link(norm(b, link, 2 + E, tiles(acc), y))
                dve.wait_ge(res_loaded.sem, res_loaded.at(b, 16))
                nc.vector.tensor_tensor(x_res[:, :, :], x_res[:, :, :], y[:, :, :], ALU.add).then_inc(y_ready.sem, 1)
                link.close()


def build(nc, a, con, out):
    under = lambda prefix: {n[len(prefix):]: x for n, x in a.items() if n.startswith(prefix)}
    first, ffn, second, experts = under("L0_attn_"), under("L0_ffn_"), under("L1_attn_"), under("L1_ffn_")
    x1, x2, x3 = (nc.dram_tensor(f"x{n}_dram", (B, N, D), fp32).ap() for n in (1, 2, 3))
    y = [nc.dram_tensor(f"y{n}_dram", (B, N, D), fp32).ap() for n in range(3)]
    differential_attention(nc, first["X"], x1, first["Wq"], first["Wk"], first["Wv"], first["Wo"],
                           [first[n] for n in ("lq1", "lk1", "lq2", "lk2")], first["rms_scale"], con)
    window_attention(nc, x1, y[0], 0, ffn, con)
    gated_ffn(nc, y[0], x1, y[1], 0, ffn, con)
    window_attention(nc, y[1], y[2], 1, ffn, con)
    gated_ffn(nc, y[2], x1, x2, 1, ffn, con)
    diffusion_attention(nc, x2, x3, second, con)
    expert_mixture(nc, x3, out, experts, con)


def mask_constants(np, bf):
    low = -1e30
    q, k = np.arange(128)[:, None], np.arange(128)[None, :]
    con = {"ident": np.eye(128, dtype=np.float32), "ident_h": np.eye(128, dtype=bf)}
    con["causal"] = np.where(k > q, low, 0.0).astype(bf)
    con["map_mask"] = (np.arange(128)[:, None] % 32 // 16 == np.arange(2)[None, :]).astype(np.float32)
    row, head = np.arange(128) % 32, np.arange(128) // 32
    con["rows"] = np.stack([2.0 * (row < 16) + (row == 17), row == 16, row <= 16, row == 17], 1).astype(np.float32)
    same = head[:, None] == head[None, :]
    con["neg_sum"] = (same & (row[:, None] < 16) & ((row == 16) | (row == 17))[None, :]) * np.float32(-1)
    con["block_mask"] = np.where(same, 0.0, low).astype(np.float32)
    before, own = np.where(k < q, low, 0.0), np.where(k > q, low, 0.0)
    first = np.concatenate([np.full_like(before, low), own], 1)
    con["window_mask"] = np.stack([first, np.concatenate([before, own], 1)], 1).astype(bf)
    half = np.arange(0, 64, 2, dtype=np.float32)
    inv_freq = np.float32(1.0) / np.float32(10000.0) ** (half / np.float32(64))
    t = np.arange(512, dtype=np.float32)
    freqs = (t[:, None] * inv_freq[None, :]).astype(np.float64)
    base = (half + np.float32(0.4 * 64)) / np.float32(1.4 * 64)
    scale = base.astype(np.float64)[None, :] ** ((t - 256) / 64.0)[:, None]
    cos, sin = np.cos(freqs), np.sin(freqs)
    both = lambda x: np.concatenate([x, x], 1)
    signed = lambda x: np.concatenate([-x, x], 1)
    con["cos"] = np.stack([both(8 * cos * scale), both(cos / scale)]).astype(np.float32)
    con["sin"] = np.stack([signed(8 * sin * scale), signed(sin / scale)]).astype(np.float32)
    con["iota"] = np.tile(np.arange(8, dtype=np.float32), (128, 1))
    return con


def kernel(**inputs):
    import numpy as _np
    import ml_dtypes as _ml
    import concourse.bacc as _bacc
    from concourse import mybir as _mybir
    from concourse.bass_utils import run_bass_kernel_spmd as _run

    nc = _bacc.Bacc("TRN2", target_bir_lowering=False, num_devices=1)
    arrays, a = {}, {}

    def give(name, x):
        x = _np.ascontiguousarray(x)
        arrays["in_" + name] = x
        return nc.dram_tensor("in_" + name, x.shape, _mybir.dt.from_np(x.dtype), kind="ExternalInput").ap()

    for name, x in inputs.items():
        if name in ("L0_attn_Wq", "L0_attn_Wk", "L0_attn_Wv", "L0_attn_Wo"):
            x = _np.asarray(x).T
        a[name] = give(name, x)
    con = {name: give("con_" + name, x) for name, x in mask_constants(_np, _ml.bfloat16).items()}
    out = nc.dram_tensor("out_0_dram", (8, 512, 256), _mybir.dt.float32, kind="ExternalOutput").ap()
    build(nc, a, con, out)
    r = _run(nc, [arrays], core_ids=[0])
    return r.results[0]["out_0_dram"]
```
